# Optimizing a Trainium2 kernel written in Bass

```python
import numpy as np
import jax
import jax.numpy as jnp

def _softmax(x, axis=-1):
    return jax.nn.softmax(x, axis=axis)

def _gelu(x):
    return jax.nn.gelu(x, approximate=True)

def _silu(x):
    return jax.nn.silu(x)

def _sigmoid(x):
    return jax.nn.sigmoid(x)

def _layernorm(x, axis=-1, eps=1e-05):
    m = jnp.mean(x, axis=axis, keepdims=True)
    v = jnp.var(x, axis=axis, keepdims=True)
    return (x - m) / jnp.sqrt(v + eps)

def _scatter_add(tgt, idx, src, axis=0):
    return tgt.at[idx].add(src)

def _segment_sum(src, seg, n):
    return jax.ops.segment_sum(src, seg, n)
kernel_name = 'mk_gnn_resnorm_d4_gnn_r64_943dc3'

def setup_inputs(seed: int=0):
    np.random.seed(seed)
    _w = jnp.asarray

    def _rec_inputs():
        import jax
        import jax.numpy as jnp
        _gk = jax.random.key(seed)
        x = -8.776e-05 + 1 * jax.random.normal(jax.random.fold_in(_gk, 1), (10000, 512), jnp.float32)
        src = jax.random.randint(jax.random.fold_in(_gk, 2), (2500,), 0, 10000, jnp.int32)
        dst = jnp.minimum((10000 * jax.random.uniform(jax.random.fold_in(_gk, 3), (2500,)) ** 2.0).astype(jnp.int32), 9999)
        _o = jnp.argsort(dst, stable=True)
        src = src[_o]
        dst = dst[_o]
        edge_attr_32 = jax.random.uniform(jax.random.fold_in(_gk, 12), (2500, 32), jnp.float32, 0.0, 1)
        edge_attr_4 = 0.000937891 + 0.999965 * jax.random.normal(jax.random.fold_in(_gk, 13), (2500, 4), jnp.float32)
        edge_weight = jax.random.uniform(jax.random.fold_in(_gk, 15), (2500,), jnp.float32, 0.0, 0.999994)
        return (x, src, dst, edge_attr_32, edge_attr_4, edge_weight)
    x, src, dst, edge_attr_32, edge_attr_4, edge_weight = _rec_inputs()

    def _L0_gnn_setup():
        import jax, jax.numpy as jnp
        import numpy as np
        N_NODES = 10000
        D_IN = 512
        D_HID = 512
        D_OUT = 512
        N_EDGES = 2500

        def sage_conv(x, edge_index, W_l, b_l, W_r):
            src, dst = (edge_index[0], edge_index[1])
            msgs = x[src]
            agg = jax.ops.segment_sum(msgs, dst, num_segments=x.shape[0])
            cnt = jax.ops.segment_sum(jnp.ones((msgs.shape[0],), x.dtype), dst, num_segments=x.shape[0])
            agg = agg / jnp.maximum(cnt, 1.0)[:, None]
            return agg @ W_l.T + b_l + x @ W_r.T
        key = jax.random.key(seed)
        ks = jax.random.split(key, 8)
        s = lambda d: 1.0 / np.sqrt(d)
        x = jax.random.normal(ks[0], (N_NODES, D_IN), dtype=jnp.float32)
        edge_index = jax.random.randint(ks[1], (2, N_EDGES), 0, N_NODES, dtype=jnp.int64)
        W1_l = jax.random.uniform(ks[2], (D_HID, D_IN), jnp.float32, -s(D_IN), s(D_IN))
        b1 = jax.random.uniform(ks[3], (D_HID,), jnp.float32, -s(D_IN), s(D_IN))
        W1_r = jax.random.uniform(ks[4], (D_HID, D_IN), jnp.float32, -s(D_IN), s(D_IN))
        W2_l = jax.random.uniform(ks[5], (D_OUT, D_HID), jnp.float32, -s(D_HID), s(D_HID))
        b2 = jax.random.uniform(ks[6], (D_OUT,), jnp.float32, -s(D_HID), s(D_HID))
        W2_r = jax.random.uniform(ks[7], (D_OUT, D_HID), jnp.float32, -s(D_HID), s(D_HID))
        return {'x': x, 'edge_index': edge_index, 'W1_l': W1_l, 'b1': b1, 'W1_r': W1_r, 'W2_l': W2_l, 'b2': b2, 'W2_r': W2_r}
    _L0_gnn_all = _L0_gnn_setup()
    _L0_gnn_in = {k: v for k, v in _L0_gnn_all.items() if k in ('W1_l', 'b1', 'W1_r', 'W2_l', 'b2', 'W2_r')}
    del _L0_gnn_all

    def _L1_gnn_setup():
        import jax, jax.numpy as jnp
        import numpy as np
        N = 256
        D = 512
        NNZ = 2560
        NUM_ITERS = 10
        key = jax.random.key(seed)
        k1, k2, k3, k4 = jax.random.split(key, 4)
        x = jax.random.normal(k1, (N, D), dtype=jnp.float32)
        edge_val = jax.random.uniform(k2, (NNZ,), dtype=jnp.float32)
        edge_row = jnp.sort(jax.random.randint(k3, (NNZ,), 0, N, dtype=jnp.int32))
        edge_col = jax.random.randint(k4, (NNZ,), 0, N, dtype=jnp.int32)
        alpha = jnp.zeros((1,), dtype=jnp.float32)
        beta = jnp.zeros((1,), dtype=jnp.float32)
        sigma = jnp.ones((1,), dtype=jnp.float32)
        return {'x': x, 'alpha': alpha, 'beta': beta, 'sigma': sigma, 'edge_val': edge_val, 'edge_row': edge_row, 'edge_col': edge_col, 'num_iters': NUM_ITERS}
    _L1_gnn_all = _L1_gnn_setup()
    _L1_gnn_in = {k: v for k, v in _L1_gnn_all.items() if k in ('alpha', 'beta', 'sigma')}
    del _L1_gnn_all

    def _L2_gnn_setup():
        import jax, jax.numpy as jnp
        import numpy as np
        N, E, DM, H, DFF = (20000, 10000, 512, 8, 32)
        DK = DM // H

        def _layernorm(x, g, b, eps=1e-05):
            mu = jnp.mean(x, axis=-1, keepdims=True)
            var = jnp.mean(jnp.square(x - mu), axis=-1, keepdims=True)
            return (x - mu) * jax.lax.rsqrt(var + eps) * g + b
        key = jax.random.key(seed)
        ks = jax.random.split(key, 12)
        s = 0.02
        h = jax.random.normal(ks[0], (N, DM), dtype=jnp.float32)
        src = jax.random.randint(ks[1], (E,), 0, N, dtype=jnp.int32)
        dst = jnp.sort(jax.random.randint(ks[2], (E,), 0, N, dtype=jnp.int32))
        return {'h': h, 'src': src, 'dst': dst, 'Wq': jax.random.normal(ks[3], (DM, DM), dtype=jnp.float32) * s, 'Wk': jax.random.normal(ks[4], (DM, DM), dtype=jnp.float32) * s, 'Wv': jax.random.normal(ks[5], (DM, DM), dtype=jnp.float32) * s, 'Wo': jax.random.normal(ks[6], (DM, DM), dtype=jnp.float32) * s, 'ln1_g': jnp.ones((DM,), jnp.float32), 'ln1_b': jnp.zeros((DM,), jnp.float32), 'ln2_g': jnp.ones((DM,), jnp.float32), 'ln2_b': jnp.zeros((DM,), jnp.float32), 'W1': jax.random.normal(ks[7], (DM, DFF), dtype=jnp.float32) * s, 'b1': jnp.zeros((DFF,), jnp.float32), 'W2': jax.random.normal(ks[8], (DFF, DM), dtype=jnp.float32) * s, 'b2': jnp.zeros((DM,), jnp.float32)}
    _L2_gnn_all = _L2_gnn_setup()
    _L2_gnn_in = {k: v for k, v in _L2_gnn_all.items() if k in ('Wq', 'Wk', 'Wv', 'Wo', 'ln1_g', 'ln1_b', 'ln2_g', 'ln2_b', 'W1', 'b1', 'W2', 'b2')}
    del _L2_gnn_all

    def _L3_gnn_setup():
        import jax, jax.numpy as jnp
        import numpy as np
        import math
        N, E = (20000, 3125)
        MUL = 128
        D = MUL + 3 * MUL
        EDGE_ATTR = 32
        HID = 32
        LOG2 = math.log(2.0)

        def ssp(x):
            return jax.nn.softplus(x) - LOG2

        def split_irreps(x):
            return (x[:, :MUL], x[:, MUL:].reshape(x.shape[0], MUL, 3))

        def merge_irreps(x0, x1):
            return jnp.concatenate([x0, x1.reshape(x1.shape[0], MUL * 3)], axis=-1)

        def irrep_linear(x, W0, b0, W1):
            x0, x1 = split_irreps(x)
            y0 = x0 @ W0 + b0
            y1 = jnp.einsum('nuc,uv->nvc', x1, W1)
            return merge_irreps(y0, y1)
        key = jax.random.key(seed)
        ks = iter(jax.random.split(key, 32))

        def randn(shape, scale=1.0):
            return (scale * jax.random.normal(next(ks), shape)).astype(jnp.float32)
        inp = {'x': randn((N, D)), 'edge_sh': randn((E, 4)), 'edge_attr': jax.random.uniform(next(ks), (E, EDGE_ATTR), dtype=jnp.float32), 'edge_index': jax.random.randint(next(ks), (2, E), 0, N, dtype=jnp.int32), 'W_pre0': randn((MUL, MUL), MUL ** (-0.5)), 'b_pre0': jnp.zeros((MUL,), jnp.float32), 'W_pre1': randn((MUL, MUL), MUL ** (-0.5)), 'W_nd0': randn((MUL, MUL), MUL ** (-0.5)), 'b_nd0': jnp.zeros((MUL,), jnp.float32), 'W_nd1': randn((MUL, MUL), MUL ** (-0.5)), 'W_g1': randn((2 * MUL, 2 * MUL), (2 * MUL) ** (-0.5)), 'b_g1': jnp.zeros((2 * MUL,), jnp.float32), 'W_g2': randn((2 * MUL, 2 * MUL), (2 * MUL) ** (-0.5)), 'b_g2': jnp.zeros((2 * MUL,), jnp.float32), 'W_f1': randn((EDGE_ATTR, HID), EDGE_ATTR ** (-0.5)), 'W_f2': randn((HID, 4 * MUL), HID ** (-0.5)), 'W_s1': randn((3 * MUL, HID), (3 * MUL) ** (-0.5)), 'W_s2': randn((HID, 4 * MUL), HID ** (-0.5)), 'W_o0': randn((MUL, MUL), MUL ** (-0.5)), 'b_o0': jnp.zeros((MUL,), jnp.float32), 'W_o1': randn((MUL, MUL), MUL ** (-0.5))}
        return inp
    _L3_gnn_all = _L3_gnn_setup()
    _L3_gnn_in = {k: v for k, v in _L3_gnn_all.items() if k in ('W_pre0', 'b_pre0', 'W_pre1', 'W_nd0', 'b_nd0', 'W_nd1', 'W_g1', 'b_g1', 'W_g2', 'b_g2', 'W_f1', 'W_f2', 'W_s1', 'W_s2', 'W_o0', 'b_o0', 'W_o1')}
    del _L3_gnn_all
    return {'x': x, 'src': src, 'dst': dst, 'edge_attr_32': edge_attr_32, 'edge_attr_4': edge_attr_4, 'edge_weight': edge_weight, 'L0_gnn_W1_l': _L0_gnn_in['W1_l'], 'L0_gnn_b1': _L0_gnn_in['b1'], 'L0_gnn_W1_r': _L0_gnn_in['W1_r'], 'L0_gnn_W2_l': _L0_gnn_in['W2_l'], 'L0_gnn_b2': _L0_gnn_in['b2'], 'L0_gnn_W2_r': _L0_gnn_in['W2_r'], 'L1_gnn_alpha': _L1_gnn_in['alpha'], 'L1_gnn_beta': _L1_gnn_in['beta'], 'L1_gnn_sigma': _L1_gnn_in['sigma'], 'L2_gnn_Wq': _L2_gnn_in['Wq'], 'L2_gnn_Wk': _L2_gnn_in['Wk'], 'L2_gnn_Wv': _L2_gnn_in['Wv'], 'L2_gnn_Wo': _L2_gnn_in['Wo'], 'L2_gnn_ln1_g': _L2_gnn_in['ln1_g'], 'L2_gnn_ln1_b': _L2_gnn_in['ln1_b'], 'L2_gnn_ln2_g': _L2_gnn_in['ln2_g'], 'L2_gnn_ln2_b': _L2_gnn_in['ln2_b'], 'L2_gnn_W1': _L2_gnn_in['W1'], 'L2_gnn_b1': _L2_gnn_in['b1'], 'L2_gnn_W2': _L2_gnn_in['W2'], 'L2_gnn_b2': _L2_gnn_in['b2'], 'L3_gnn_W_pre0': _L3_gnn_in['W_pre0'], 'L3_gnn_b_pre0': _L3_gnn_in['b_pre0'], 'L3_gnn_W_pre1': _L3_gnn_in['W_pre1'], 'L3_gnn_W_nd0': _L3_gnn_in['W_nd0'], 'L3_gnn_b_nd0': _L3_gnn_in['b_nd0'], 'L3_gnn_W_nd1': _L3_gnn_in['W_nd1'], 'L3_gnn_W_g1': _L3_gnn_in['W_g1'], 'L3_gnn_b_g1': _L3_gnn_in['b_g1'], 'L3_gnn_W_g2': _L3_gnn_in['W_g2'], 'L3_gnn_b_g2': _L3_gnn_in['b_g2'], 'L3_gnn_W_f1': _L3_gnn_in['W_f1'], 'L3_gnn_W_f2': _L3_gnn_in['W_f2'], 'L3_gnn_W_s1': _L3_gnn_in['W_s1'], 'L3_gnn_W_s2': _L3_gnn_in['W_s2'], 'L3_gnn_W_o0': _L3_gnn_in['W_o0'], 'L3_gnn_b_o0': _L3_gnn_in['b_o0'], 'L3_gnn_W_o1': _L3_gnn_in['W_o1']}

def reference(x, src, dst, edge_attr_32, edge_attr_4, edge_weight, L0_gnn_W1_l, L0_gnn_b1, L0_gnn_W1_r, L0_gnn_W2_l, L0_gnn_b2, L0_gnn_W2_r, L1_gnn_alpha, L1_gnn_beta, L1_gnn_sigma, L2_gnn_Wq, L2_gnn_Wk, L2_gnn_Wv, L2_gnn_Wo, L2_gnn_ln1_g, L2_gnn_ln1_b, L2_gnn_ln2_g, L2_gnn_ln2_b, L2_gnn_W1, L2_gnn_b1, L2_gnn_W2, L2_gnn_b2, L3_gnn_W_pre0, L3_gnn_b_pre0, L3_gnn_W_pre1, L3_gnn_W_nd0, L3_gnn_b_nd0, L3_gnn_W_nd1, L3_gnn_W_g1, L3_gnn_b_g1, L3_gnn_W_g2, L3_gnn_b_g2, L3_gnn_W_f1, L3_gnn_W_f2, L3_gnn_W_s1, L3_gnn_W_s2, L3_gnn_W_o0, L3_gnn_b_o0, L3_gnn_W_o1):
    import jax
    import jax.numpy as jnp

    def _L0_gnn_ref(x, edge_index, W1_l, b1, W1_r, W2_l, b2, W2_r):
        import jax, jax.numpy as jnp
        import numpy as np
        N_NODES = 10000
        D_IN = 512
        D_HID = 512
        D_OUT = 512
        N_EDGES = 2500

        def sage_conv(x, edge_index, W_l, b_l, W_r):
            src, dst = (edge_index[0], edge_index[1])
            msgs = x[src]
            agg = jax.ops.segment_sum(msgs, dst, num_segments=x.shape[0])
            cnt = jax.ops.segment_sum(jnp.ones((msgs.shape[0],), x.dtype), dst, num_segments=x.shape[0])
            agg = agg / jnp.maximum(cnt, 1.0)[:, None]
            return agg @ W_l.T + b_l + x @ W_r.T
        h = jax.nn.relu(sage_conv(x, edge_index, W1_l, b1, W1_r))
        return sage_conv(h, edge_index, W2_l, b2, W2_r)

    def _L1_gnn_ref(x, alpha, beta, sigma, edge_val, edge_row, edge_col, num_iters):
        import jax, jax.numpy as jnp
        import numpy as np
        N = 256
        D = 512
        NNZ = 2560
        NUM_ITERS = 10
        n = x.shape[0]
        xn = x * jax.lax.rsqrt(jnp.maximum(jnp.sum(x * x, axis=1, keepdims=True), 1e-12))
        sim_e = jnp.sum(xn[edge_row] * xn[edge_col], axis=-1)
        sim_e = jnp.where(edge_row == edge_col, 0.0, sim_e)
        s = jnp.exp(sigma[0])
        sigma_sq = 2.0 * s * s
        sim_e = jnp.exp(sim_e / (2.0 * sigma_sq))
        sup = edge_val * sim_e
        normalize = jax.ops.segment_sum(sup, edge_row, num_segments=n)
        a = jnp.exp(alpha[0])
        b = jnp.exp(beta[0])
        denom = b + normalize[:, None] * a + a

        def step(out, _):
            Ax = jax.ops.segment_sum(sup[:, None] * out[edge_col], edge_row, num_segments=n)
            out = (x * b + (Ax + out) * a) / denom
            return (out, None)
        out, _ = jax.lax.scan(step, x, None, length=num_iters)
        return out

    def _L2_gnn_ref(h, src, dst, Wq, Wk, Wv, Wo, ln1_g, ln1_b, ln2_g, ln2_b, W1, b1, W2, b2):
        import jax, jax.numpy as jnp
        import numpy as np
        N, E, DM, H, DFF = (20000, 10000, 512, 8, 32)
        DK = DM // H

        def _layernorm(x, g, b, eps=1e-05):
            mu = jnp.mean(x, axis=-1, keepdims=True)
            var = jnp.mean(jnp.square(x - mu), axis=-1, keepdims=True)
            return (x - mu) * jax.lax.rsqrt(var + eps) * g + b
        n = h.shape[0]
        q = (h @ Wq).reshape(n, H, DK)
        k = (h @ Wk).reshape(n, H, DK)
        v = (h @ Wv).reshape(n, H, DK)
        e = jnp.einsum('ehd,ehd->eh', k[src], q[dst]) / np.sqrt(DK).astype(np.float32)
        m = jax.ops.segment_max(e, dst, num_segments=n)
        ex = jnp.exp(e - m[dst])
        z = jax.ops.segment_sum(ex, dst, num_segments=n)
        attn = ex / z[dst]
        a = jax.ops.segment_sum(attn[:, :, None] * v[src], dst, num_segments=n)
        a = a.reshape(n, DM)
        o = a @ Wo
        x = _layernorm(h + o, ln1_g, ln1_b)
        f = jax.nn.relu(x @ W1 + b1) @ W2 + b2
        return _layernorm(x + f, ln2_g, ln2_b)

    def _L3_gnn_ref(x, edge_sh, edge_attr, edge_index, W_pre0, b_pre0, W_pre1, W_nd0, b_nd0, W_nd1, W_g1, b_g1, W_g2, b_g2, W_f1, W_f2, W_s1, W_s2, W_o0, b_o0, W_o1):
        import jax, jax.numpy as jnp
        import numpy as np
        import math
        N, E = (20000, 3125)
        MUL = 128
        D = MUL + 3 * MUL
        EDGE_ATTR = 32
        HID = 32
        LOG2 = math.log(2.0)

        def ssp(x):
            return jax.nn.softplus(x) - LOG2

        def split_irreps(x):
            return (x[:, :MUL], x[:, MUL:].reshape(x.shape[0], MUL, 3))

        def merge_irreps(x0, x1):
            return jnp.concatenate([x0, x1.reshape(x1.shape[0], MUL * 3)], axis=-1)

        def irrep_linear(x, W0, b0, W1):
            x0, x1 = split_irreps(x)
            y0 = x0 @ W0 + b0
            y1 = jnp.einsum('nuc,uv->nvc', x1, W1)
            return merge_irreps(y0, y1)
        edge_dst, edge_src = (edge_index[0], edge_index[1])
        old_x = x
        pre = irrep_linear(x, W_pre0, b_pre0, W_pre1)
        p0, p1 = split_irreps(pre)
        pd0 = p0[edge_dst]
        ip1 = jnp.einsum('eum,eum->eu', p1[edge_dst], p1[edge_src]) / 3.0
        s0 = jnp.concatenate([pd0, pd0, ip1], axis=-1)
        x0, x1 = split_irreps(x)
        n1 = jnp.sqrt(jnp.sum(x1 * x1, axis=-1) / 3.0)
        g = jax.nn.silu(jnp.concatenate([x0, n1], -1) @ W_g1 + b_g1) @ W_g2 + b_g2
        xg = merge_irreps(g[:, :MUL], x1 * g[:, MUL:, None])
        x = irrep_linear(xg, W_nd0, b_nd0, W_nd1)
        self_x = x
        w = ssp(edge_attr @ W_f1) @ W_f2 * (ssp(s0 @ W_s1) @ W_s2)
        w1, w2, w3, w4 = jnp.split(w, 4, axis=-1)
        x0e, x1e = split_irreps(x[edge_src])
        sh0, sh1 = (edge_sh[:, 0], edge_sh[:, 1:4])
        out0 = w1 * x0e * sh0[:, None] + w4 * (jnp.einsum('eum,em->eu', x1e, sh1) / jnp.sqrt(3.0))
        out1 = w2[:, :, None] * x0e[:, :, None] * sh1[:, None, :] + w3[:, :, None] * x1e * sh0[:, None, None]
        edge_feat = merge_irreps(out0, out1)
        out = jax.ops.segment_sum(edge_feat, edge_dst, num_segments=old_x.shape[0])
        out = out + self_x
        out = irrep_linear(out, W_o0, b_o0, W_o1)
        return out + old_x
    edge_index = jnp.stack([src, dst])
    x = _layernorm(x + _L0_gnn_ref(x, edge_index, L0_gnn_W1_l, L0_gnn_b1, L0_gnn_W1_r, L0_gnn_W2_l, L0_gnn_b2, L0_gnn_W2_r), axis=-1)
    x = _layernorm(x + _L1_gnn_ref(x, L1_gnn_alpha, L1_gnn_beta, L1_gnn_sigma, edge_weight, src, dst, 10), axis=-1)
    x = _layernorm(x + _L2_gnn_ref(x, src, dst, L2_gnn_Wq, L2_gnn_Wk, L2_gnn_Wv, L2_gnn_Wo, L2_gnn_ln1_g, L2_gnn_ln1_b, L2_gnn_ln2_g, L2_gnn_ln2_b, L2_gnn_W1, L2_gnn_b1, L2_gnn_W2, L2_gnn_b2), axis=-1)
    x = _layernorm(x + _L3_gnn_ref(x, edge_attr_4, edge_attr_32, edge_index, L3_gnn_W_pre0, L3_gnn_b_pre0, L3_gnn_W_pre1, L3_gnn_W_nd0, L3_gnn_b_nd0, L3_gnn_W_nd1, L3_gnn_W_g1, L3_gnn_b_g1, L3_gnn_W_g2, L3_gnn_b_g2, L3_gnn_W_f1, L3_gnn_W_f2, L3_gnn_W_s1, L3_gnn_W_s2, L3_gnn_W_o0, L3_gnn_b_o0, L3_gnn_W_o1), axis=-1)
    return x

_drawn_inputs = setup_inputs


def setup_inputs(seed=0):
    import zlib

    import numpy as np

    out = dict(_drawn_inputs(seed))
    spreads = {'L2_gnn_ln1_g': (1.0, 0.2),
     'L2_gnn_ln1_b': (0.0, 0.1),
     'L2_gnn_ln2_g': (1.0, 0.2),
     'L2_gnn_ln2_b': (0.0, 0.1),
     'L2_gnn_b1': (0.0, 0.8),
     'L2_gnn_b2': (0.0, 0.1),
     'L3_gnn_b_pre0': (0.0, 2.0),
     'L3_gnn_b_nd0': (0.0, 0.36),
     'L3_gnn_b_g1': (0.0, 0.1),
     'L3_gnn_b_g2': (0.0, 0.1),
     'L3_gnn_b_o0': (0.0, 0.335)}
    factors = {'edge_attr_32': 3.93,
     'L0_gnn_b1': 5.313,
     'L2_gnn_Wq': 8.0,
     'L2_gnn_Wk': 8.0,
     'L2_gnn_W1': 3.777,
     'L2_gnn_W2': 3.091,
     'L3_gnn_W_pre1': 5.351}
    for name, (base, spread) in spreads.items():
        noise = np.random.default_rng([zlib.crc32(name.encode()), seed]).standard_normal(out[name].shape)
        drawn = base * np.exp(spread * noise) if base else spread * noise
        out[name] = jnp.asarray(drawn.astype(out[name].dtype))
    for name, factor in factors.items():
        out[name] = (out[name] * factor).astype(out[name].dtype)
    return out
```

```python
import concourse.bass as bass
from concourse import mybir
from contextlib import ExitStack

N, E, D = 10000, 2500, 512
P = 125
TG = 4
GR = P * TG
NG = N // GR
KC = D // 128
HI = 112
EPS = 1e-5
F32, I32 = mybir.dt.float32, mybir.dt.int32
ALU, ACT, AX = mybir.AluOpType, mybir.ActivationFunctionType, mybir.AxisListType

C_L0B1, C_LN1G, C_LN1B, C_L2B1, C_BG1, C_BG2, C_BND, C_BPRE, C_END = 0, 4, 8, 12, 13, 15, 17, 18, 19
R_L0B2, R_LN1G, R_LN1B, R_L2B2, R_LN2G, R_LN2B, R_L3, R_END = range(8)
W_G1, W_G2, W_ND0, W_ND1, W_O0, W_O1, W_PRE0, W_PRE1, W_S1, W_L2A, W_END = \
    0, 512, 1024, 1152, 1280, 1408, 1536, 1664, 1792, 1888, 2016
V_L2B, V_F2, V_S2, V_F1, V_END = 0, 512, 1024, 1536, 1568
ET = E // P
EG = ET // TG
NB = 2 * ET
H, DK = 8, D // 8
ITERS = 10
Q_DST, Q_SRC, Q_W, Q_DSC, Q_SH, Q_EA, Q_SSC, Q_CNT, Q_DUP, Q_SI, Q_DI, Q_RS, Q_YI, Q_XD, Q_END = \
    0, 1, 2, 3, 4, 8, 40, 41, 42, 43, 44, 45, 46, 47, 48
FAR = 1 << 20
NEG = -1e30
LN2 = 0.6931471805599453


def gnn_kernel(nc, x, cols, rows, wsmall, w32, ident_in, w_r1, w_r2, w_l1, w_l2, w_q, w_k, w_v, w_o,
               keys, key_cols, rec_in, tri_in, mask_in, abs_in, out):
    ctx = ExitStack()
    with ctx:
        def sb(name, shape, dt=F32):
            return ctx.enter_context(nc.sbuf_tensor(name, shape, dt))

        def sem(name):
            return ctx.enter_context(nc.semaphore(name))

        bank = [ctx.enter_context(nc.psum_tensor(f"bank{i}", [128, 512], F32)) for i in range(8)]

        ident = sb("ident", [128, 128])
        colv = sb("colv", [128, C_END])
        rowv = sb("rowv", [P, R_END, D])
        ws = sb("ws", [128, W_END])
        w32s = sb("w32s", [32, V_END])
        AR = 38100
        arena = sb("arena", [128, AR])

        def at(off, shape, parts=128, dt=F32):
            n = 1
            for v in shape:
                n *= v
            assert off + n <= AR, (off, shape)
            ap = arena[0:parts, off:off + n]
            if dt != F32:
                ap = ap.bitcast(dt)
            if len(shape) == 2:
                ap = ap.rearrange("p (a b) -> p a b", b=shape[1])
            return ap

        G4 = TG * D
        W1r, W2r = at(0, [KC, D]), at(2048, [KC, D])
        X = [at(4096 + G4 * i, [TG, D], P) for i in range(2)]
        Z = at(8192, [TG, D], P)
        T = [at(10240 + G4 * i, [TG, D], P) for i in range(2)]
        U = at(14336, [TG, D], P)
        X3 = [at(16384 + G4 * i, [TG, D], P) for i in range(2)]
        O = at(20480, [TG, D], P)
        xT, hT, tT = at(22528, [KC, GR]), at(24528, [KC, GR]), at(26528, [KC, GR])
        x3T = at(28528, [KC, GR])
        xgT, ndT = at(30528, [KC, GR]), at(32528, [KC, GR])
        sq = xgT[:, 1:4, :]
        g1T = at(34528, [2, GR])
        f1T, n1T, gateT = at(35528, [GR], 32), at(36028, [GR]), at(36528, [GR])
        st = sb("st", [P, 4, TG, 6])
        n_even = sb("n_even", [P, 4, 1])
        mv = sb("mv", [P, 4, TG, 2])
        dd = sb("dd", [P, 2, TG])
        sr = sb("sr", [P, 4, 2, TG])
        rs = sb("rs", [P, 4, TG])
        nb = sb("nb", [P, 4, TG])
        q2 = [sb(f"q2_{i}", [P, TG]) for i in range(2)]

        s_w = sem("weights_in")
        A = {k: sem("A_" + k) for k in
             "x_in0 x_in1 xb xT_ps xT_sb hT_ps hT_sb out_ps z bn ag sc rt rc t".split()}
        B = {k: sem("B_" + k) for k in
             "tT_ps tT_sb f1_ps f1_sb f_ps tg tgb z bn ag sc rt rc u ug ub z3 bn3 ag3 sc3 rt3 rc3 x3".split()}
        C = {k: sem("C_" + k) for k in
             "xT_ps xT_sb sq sqs n1 g1_ps g1_sb g2_ps g2_sb xg nd_ps nd_sb o_ps o bn ag sc rt rc y out".split()}

        def wcol(a, n):
            return ws[:, a:a + n]

        def row(r, n=D):
            return rowv[:, r, 0:n]

        def vec3(ap):
            return ap.rearrange("p (u c) -> p c u", c=3)

        block = ctx.enter_context(nc.Block())

        def grows(dram, g):
            return dram[bass.ds(g * GR, GR), :].rearrange("(t p) d -> p t d", p=P)

        def sp_in(sp, n, par):
            if not (isinstance(n, int) and n < 2):
                sp.wait_ge(A["xT_ps"], 4 * n - 4)
                sp.wait_ge(A["xb"], 4 * n - 4)
            src = grows(x, n)
            sp.dma_start(X[par][0:HI], src[0:HI]).then_inc(A[f"x_in{par}"], 16)
            sp.dma_start(X[par][HI:P], src[HI:P]).then_inc(A[f"x_in{par}"], 16)

        def sp_out(sp, n):
            sp.wait_ge(C["y"], 4 * n + 4)
            dst = grows(out, n)
            sp.dma_start(dst[0:HI], O[0:HI]).then_inc(C["out"], 16)
            sp.dma_start(dst[HI:P], O[HI:P]).then_inc(C["out"], 16)

        def pe_A(pe, n, par):
            pe.wait_ge(A[f"x_in{par}"], 16 * n + 32 - 16 * par)
            for k in range(KC):
                if k >= 2:
                    pe.wait_ge(A["xT_sb"], 4 * n + k - 1)
                for j in range(TG):
                    i = nc.tensor.transpose(bank[k % 2][:, j * P:(j + 1) * P],
                                            X[par][:, j, k * 128:(k + 1) * 128], ident[0:P, 0:P])
                i.then_inc(A["xT_ps"], 1)
            pe.wait_ge(A["xT_sb"], 4 * n + 4)
            for m in range(KC):
                if m >= 2:
                    pe.wait_ge(A["hT_sb"], 4 * n + m - 1)
                for k in range(KC):
                    i = nc.tensor.matmul(bank[2 + m % 2][:, 0:GR], W1r[:, k, m * 128:(m + 1) * 128],
                                         xT[:, k, :], start=k == 0, stop=k == KC - 1)
                i.then_inc(A["hT_ps"], 1)
            pe.wait_ge(A["hT_sb"], 4 * n + 4)
            for j in range(TG):
                if j >= 2:
                    pe.wait_ge(A["z"], 4 * n + j - 1)
                for k in range(KC):
                    i = nc.tensor.matmul(bank[4 + j % 2][0:P, :], hT[:, k, j * P:(j + 1) * P],
                                         W2r[:, k, :], start=k == 0, stop=k == KC - 1)
                i.then_inc(A["out_ps"], 1)

        def pe_B(pe, n, par):
            pe.wait_ge(B_in, 4 * n + 4)
            for k in range(KC):
                if k >= 2:
                    pe.wait_ge(B["tT_sb"], 4 * n + k - 1)
                for j in range(TG):
                    i = nc.tensor.transpose(bank[k % 2][:, j * P:(j + 1) * P],
                                            T[par][:, j, k * 128:(k + 1) * 128], ident[0:P, 0:P])
                i.then_inc(B["tT_ps"], 1)
            pe.wait_ge(B["tT_sb"], 4 * n + 4)
            for k in range(KC):
                i = nc.tensor.matmul(bank[2][0:32, 0:GR], wcol(W_L2A + 32 * k, 32), tT[:, k, :],
                                     start=k == 0, stop=k == KC - 1)
            i.then_inc(B["f1_ps"], 1)
            pe.wait_ge(B["f1_sb"], n + 1)
            for j in range(TG):
                if j >= 2:
                    pe.wait_ge(B["z"], 4 * n + j - 1)
                elif not (isinstance(n, int) and n == 0):
                    pe.wait_ge(B["z"], 4 * n + j - 1)
                nc.tensor.matmul(bank[6 + j % 2][0:P, :], f1T[:, j * P:(j + 1) * P],
                                 w32s[:, V_L2B:V_L2B + D], start=True, stop=True).then_inc(B["f_ps"], 1)

        def pe_C(pe, n, par):
            pe.wait_ge(B["x3"], 4 * n + 4)
            for k in range(KC):
                if k >= 2:
                    pe.wait_ge(C["xT_sb"], 4 * n + k - 1)
                for j in range(TG):
                    src = X3[par][:, j, 0:128] if k == 0 else vec3(X3[par][:, j, 128:D])[:, k - 1, :]
                    i = nc.tensor.transpose(bank[k % 2][:, j * P:(j + 1) * P], src, ident[0:P, 0:P])
                i.then_inc(C["xT_ps"], 1)
            pe.wait_ge(C["n1"], n + 1)
            for m in range(2):
                nc.tensor.matmul(bank[2 + m][:, 0:GR], wcol(W_G1 + 128 * m, 128), x3T[:, 0, :],
                                 start=True, stop=False)
                nc.tensor.matmul(bank[2 + m][:, 0:GR], wcol(W_G1 + 256 + 128 * m, 128), n1T[:, :],
                                 start=False, stop=True).then_inc(C["g1_ps"], 1)
            pe.wait_ge(C["g1_sb"], 2 * n + 2)
            for m in (1, 0):
                nc.tensor.matmul(bank[m][:, 0:GR], wcol(W_G2 + 128 * m, 128), g1T[:, 0, :],
                                 start=True, stop=False)
                nc.tensor.matmul(bank[m][:, 0:GR], wcol(W_G2 + 256 + 128 * m, 128), g1T[:, 1, :],
                                 start=False, stop=True).then_inc(C["g2_ps"], 1)
            pe.wait_ge(C["g2_sb"], 2 * n + 2)
            for k in range(KC):
                if k >= 1:
                    pe.wait_ge(C["xg"], 3 * n + k)
                if k >= 2:
                    pe.wait_ge(C["nd_sb"], 4 * n + k - 1)
                nc.tensor.matmul(bank[2 + k % 2][:, 0:GR], wcol(W_ND1 if k else W_ND0, 128), xgT[:, k, :],
                                 start=True, stop=True).then_inc(C["nd_ps"], 1)
            pe.wait_ge(C["nd_sb"], 4 * n + 4)
            for j in range(TG):
                if j >= 2:
                    pe.wait_ge(C["o"], 4 * n + j - 1)
                for k in range(KC):
                    i = nc.tensor.matmul(bank[4 + j % 2][0:P, k * 128:(k + 1) * 128],
                                         ndT[:, k, j * P:(j + 1) * P], wcol(W_O1 if k else W_O0, 128),
                                         start=k == 0, stop=k == KC - 1)
                i.then_inc(C["o_ps"], 1)

        def act_A1(act, n):
            for k in range(KC):
                act.wait_ge(A["xT_ps"], 4 * n + k + 1)
                if k == 0 and not (isinstance(n, int) and n == 0):
                    act.wait_ge(A["hT_ps"], 4 * n)
                nc.scalar.activation(xT[:, k, :], bank[k % 2][:, 0:GR], ACT.Identity).then_inc(A["xT_sb"], 1)
            for m in range(KC):
                act.wait_ge(A["hT_ps"], 4 * n + m + 1)
                if m == 0 and not (isinstance(n, int) and n == 0):
                    act.wait_ge(A["out_ps"], 4 * n)
                nc.scalar.activation(hT[:, m, :], bank[2 + m % 2][:, 0:GR], ACT.Relu,
                                     bias=colv[:, C_L0B1 + m:C_L0B1 + m + 1]).then_inc(A["hT_sb"], 1)

        def act_A2(act, n, par):
            act.wait_ge(A["sc"], 4 * n + 4)
            nc.scalar.activation(sr[:, 0, :, :], sr[:, 0, :, :], ACT.Sqrt).then_inc(A["rt"], 1)
            act.wait_ge(A["rc"], 3 * n + 3)
            if not (isinstance(n, int) and n < 2):
                act.wait_ge(B["z3"], 4 * n - 4)
            for j in range(TG):
                nc.scalar.activation(T[par][:, j, :], Z[:, j, :], ACT.Identity, scale=rs[:, 0, j:j + 1],
                                     bias=nb[:, 0, j:j + 1]).then_inc(A["t"], 1)

        def act_B1(act, n):
            for k in range(KC):
                act.wait_ge(B["tT_ps"], 4 * n + k + 1)
                if k == 0 and not (isinstance(n, int) and n == 0):
                    act.wait_ge(B["f1_ps"], n)
                nc.scalar.activation(tT[:, k, :], bank[k % 2][:, 0:GR], ACT.Identity,
                                     scale=colv[:, C_LN1G + k:C_LN1G + k + 1],
                                     bias=colv[:, C_LN1B + k:C_LN1B + k + 1]).then_inc(B["tT_sb"], 1)
            act.wait_ge(B["f1_ps"], n + 1)
            if not (isinstance(n, int) and n == 0):
                act.wait_ge(B["f_ps"], 4 * n)
            nc.scalar.activation(f1T[:, :], bank[2][0:32, 0:GR], ACT.Relu,
                                 bias=colv[0:32, C_L2B1:C_L2B1 + 1]).then_inc(B["f1_sb"], 1)

        def act_B2(act, n, par):
            act.wait_ge(B["sc"], n + 1)
            nc.scalar.activation(sr[:, 1, 0, :], sr[:, 1, 0, :], ACT.Sqrt).then_inc(B["rt"], 1)
            act.wait_ge(B["rc"], 2 * n + 2)
            for j in range(TG):
                nc.scalar.activation(U[:, j, :], U[:, j, :], ACT.Identity, scale=rs[:, 1, j:j + 1],
                                     bias=nb[:, 1, j:j + 1]).then_inc(B["u"], 1)
            act.wait_ge(B["sc3"], n + 1)
            nc.scalar.activation(sr[:, 2, 0, :], sr[:, 2, 0, :], ACT.Sqrt).then_inc(B["rt3"], 1)
            act.wait_ge(B["rc3"], 2 * n + 2)
            if not (isinstance(n, int) and n < 2):
                act.wait_ge(C["o"], 4 * n - 4)
            for j in range(TG):
                nc.scalar.activation(X3[par][:, j, :], U[:, j, :], ACT.Identity, scale=rs[:, 2, j:j + 1],
                                     bias=nb[:, 2, j:j + 1]).then_inc(B["x3"], 1)

        def act_C1(act, n):
            for k in range(KC):
                act.wait_ge(C["xT_ps"], 4 * n + k + 1)
                if k == 0 and not (isinstance(n, int) and n == 0):
                    act.wait_ge(C["g1_ps"], 2 * n)
                    act.wait_ge(C["xg"], 3 * n)
                nc.scalar.activation(x3T[:, k, :], bank[k % 2][:, 0:GR], ACT.Identity).then_inc(C["xT_sb"], 1)
            act.wait_ge(C["sqs"], 2 * n + 2)
            nc.scalar.activation(n1T[:, :], sq[:, 0, :], ACT.Sqrt, scale=1.0 / 3.0).then_inc(C["n1"], 1)
            for m in range(2):
                act.wait_ge(C["g1_ps"], 2 * n + m + 1)
                nc.scalar.activation(g1T[:, m, :], bank[2 + m][:, 0:GR], ACT.Silu,
                                     bias=colv[:, C_BG1 + m:C_BG1 + m + 1]).then_inc(C["g1_sb"], 1)
            for i, (m, dst) in enumerate(((1, gateT[:, :]), (0, xgT[:, 0, :]))):
                act.wait_ge(C["g2_ps"], 2 * n + i + 1)
                if m == 0 and not (isinstance(n, int) and n == 0):
                    act.wait_ge(C["nd_ps"], 4 * n)
                nc.scalar.activation(dst, bank[m][:, 0:GR], ACT.Identity,
                                     bias=colv[:, C_BG2 + m:C_BG2 + m + 1]).then_inc(C["g2_sb"], 1)
            for k in range(KC):
                act.wait_ge(C["nd_ps"], 4 * n + k + 1)
                if k == 0 and not (isinstance(n, int) and n == 0):
                    act.wait_ge(C["o_ps"], 4 * n)
                if k == 0:
                    nc.scalar.activation(ndT[:, k, :], bank[2][:, 0:GR], ACT.Identity,
                                         bias=colv[:, C_BND:C_BND + 1]).then_inc(C["nd_sb"], 1)
                else:
                    nc.scalar.activation(ndT[:, k, :], bank[2 + k % 2][:, 0:GR],
                                         ACT.Identity).then_inc(C["nd_sb"], 1)

        def act_C2(act, n):
            act.wait_ge(C["sc"], n + 1)
            nc.scalar.activation(sr[:, 3, 0, :], sr[:, 3, 0, :], ACT.Sqrt).then_inc(C["rt"], 1)
            act.wait_ge(C["rc"], 2 * n + 2)
            for j in range(TG):
                nc.scalar.activation(O[:, j, :], O[:, j, :], ACT.Identity, scale=rs[:, 3, j:j + 1],
                                     bias=nb[:, 3, j:j + 1]).then_inc(C["y"], 1)

        def dve_stats(dve, S, bn, ag, z, n, q, src):
            for j in range(TG):
                dve.wait_ge(S[z], 4 * n + j + 1)
                nc.vector.bn_stats(st[:, q, j, :], src[:, j, :]).then_inc(S[bn], 1)
            dve.wait_ge(S[bn], 4 * n + 4)
            nc.vector.tensor_copy(n_even[:, q, :], st[:, q, 0, 0:1]).then_inc(S[ag], 1)
            for j in range(TG):
                nc.vector.bn_aggr(mv[:, q, j, :], st[:, q, j, :]).then_inc(S[ag], 1)
            dve.wait_ge(S[ag], 5 * n + 5)

        def dve_norm(dve, S, sc, rt, rc, n, q):
            nc.vector.tensor_scalar_add(sr[:, q, 0, :], mv[:, q, :, 1], EPS).then_inc(S[sc], 1)
            dve.wait_ge(S[rt], n + 1)
            nc.vector.reciprocal(rs[:, q, :], sr[:, q, 0, :]).then_inc(S[rc], 1)
            dve.wait_ge(S[rc], 2 * n + 1)
            nc.vector.scalar_tensor_tensor(nb[:, q, :], mv[:, q, :, 0], -1.0, rs[:, q, :], ALU.mult,
                                           ALU.mult).then_inc(S[rc], 1)

        def dve_A(dve, n, par):
            for j in range(TG):
                dve.wait_ge(A["xb"], 4 * n + j + 1)
                dve.wait_ge(A["out_ps"], 4 * n + j + 1)
                nc.vector.tensor_tensor(Z[:, j, :], Z[:, j, :], bank[4 + j % 2][0:P, :],
                                        ALU.add).then_inc(A["z"], 1)
            if not (isinstance(n, int) and n == 0):
                dve.wait_ge(A["t"], 4 * n)
            dve_stats(dve, A, "bn", "ag", "z", n, 0, Z)
            var = mv[:, 0, :, 1]
            nc.vector.tensor_scalar(dd[:, 0, :], var, 4.0 + EPS, EPS * EPS, ALU.mult,
                                    ALU.add).then_inc(A["sc"], 1)
            dve.wait_ge(A["sc"], 4 * n + 1)
            nc.vector.scalar_tensor_tensor(sr[:, 0, 0, :], dd[:, 0, :], EPS / 4, var, ALU.mult,
                                           ALU.add).then_inc(A["sc"], 1)
            nc.vector.reciprocal(dd[:, 1, :], dd[:, 0, :]).then_inc(A["sc"], 1)
            dve.wait_ge(A["sc"], 4 * n + 3)
            nc.vector.scalar_tensor_tensor(sr[:, 0, 1, :], dd[:, 1, :], 4.0, sr[:, 0, 0, :], ALU.mult,
                                           ALU.mult).then_inc(A["sc"], 1)
            dve.wait_ge(A["rt"], n + 1)
            nc.vector.reciprocal(rs[:, 0, :], sr[:, 0, 0, :]).then_inc(A["rc"], 1)
            nc.vector.tensor_copy(q2[par][:, :], sr[:, 0, 1, :]).then_inc(A["rc"], 1)
            dve.wait_ge(A["rc"], 3 * n + 1)
            nc.vector.scalar_tensor_tensor(nb[:, 0, :], mv[:, 0, :, 0], -1.0, rs[:, 0, :], ALU.mult,
                                           ALU.mult).then_inc(A["rc"], 1)

        def dve_B(dve, n, par):
            for j in range(TG):
                dve.wait_ge(B["tgb"], 4 * n + j + 1)
                dve.wait_ge(B["f_ps"], 4 * n + j + 1)
                nc.vector.tensor_tensor(U[:, j, :], U[:, j, :], bank[6 + j % 2][0:P, :],
                                        ALU.add).then_inc(B["z"], 1)
            if not (isinstance(n, int) and n == 0):
                dve.wait_ge(B["u"], 4 * n)
            dve_stats(dve, B, "bn", "ag", "z", n, 1, U)
            dve_norm(dve, B, "sc", "rt", "rc", n, 1)
            for j in range(TG):
                dve.wait_ge(B["ub"], 4 * n + j + 1)
                nc.vector.scalar_tensor_tensor(U[:, j, :], T[par][:, j, :], q2[par][:, j:j + 1], U[:, j, :],
                                               ALU.mult, ALU.add).then_inc(B["z3"], 1)
            dve_stats(dve, B, "bn3", "ag3", "z3", n, 2, U)
            dve_norm(dve, B, "sc3", "rt3", "rc3", n, 2)

        def dve_C(dve, n, par):
            for c in range(3):
                dve.wait_ge(C["xT_sb"], 4 * n + c + 2)
                if c == 0 and not (isinstance(n, int) and n == 0):
                    dve.wait_ge(C["nd_ps"], 4 * n)
                nc.vector.tensor_tensor(sq[:, c, :], x3T[:, c + 1, :], x3T[:, c + 1, :],
                                        ALU.mult).then_inc(C["sq"], 1)
            for c in range(2):
                dve.wait_ge(C["sq"], 3 * n + 2 + c)
                if c:
                    dve.wait_ge(C["sqs"], 2 * n + 1)
                nc.vector.tensor_tensor(sq[:, 0, :], sq[:, 0, :], sq[:, c + 1, :],
                                        ALU.add).then_inc(C["sqs"], 1)
            dve.wait_ge(C["g2_sb"], 2 * n + 1)
            if not (isinstance(n, int) and n == 0):
                dve.wait_ge(C["nd_ps"], 4 * n)
            for c in range(3):
                nc.vector.tensor_tensor(xgT[:, c + 1, :], x3T[:, c + 1, :], gateT[:, :],
                                        ALU.mult).then_inc(C["xg"], 1)

        def dve_C2(dve, n, par):
            if not (isinstance(n, int) and n == 0):
                dve.wait_ge(C["out"], 32 * n)
            for j in range(TG):
                dve.wait_ge(C["o_ps"], 4 * n + j + 1)
                b = bank[4 + j % 2]
                nc.vector.scalar_tensor_tensor(vec3(O[:, j, 128:D]), vec3(X3[par][:, j, 128:D]), 2.0,
                                               b[0:P, 128:D].rearrange("p (c u) -> p c u", c=3),
                                               ALU.mult, ALU.add)
                nc.vector.scalar_tensor_tensor(O[:, j, 0:128], X3[par][:, j, 0:128], 2.0, b[0:P, 0:128],
                                               ALU.mult, ALU.add).then_inc(C["o"], 1)
            for j in range(TG):
                dve.wait_ge(C["o"], 4 * n + j + 1)
                nc.vector.tensor_tensor(O[:, j, 0:128], O[:, j, 0:128], row(R_L3, 128),
                                        ALU.add).then_inc(C["ob"], 1)
            dve_stats(dve, C, "bn", "ag", "ob", n, 3, O)
            dve_norm(dve, C, "sc", "rt", "rc", n, 3)
        C["ob"] = sem("C_ob")
        B_in = A["t"]

        def pool_A(pool, n, par):
            pool.wait_ge(A[f"x_in{par}"], 16 * n + 32 - 16 * par)
            if not (isinstance(n, int) and n == 0):
                pool.wait_ge(A["t"], 4 * n)
            for j in range(TG):
                nc.gpsimd.tensor_tensor(Z[:, j, :], X[par][:, j, :], row(R_L0B2), ALU.add).then_inc(A["xb"], 1)

        def pool_B1(pool, n, par):
            if not (isinstance(n, int) and n == 0):
                pool.wait_ge(B["x3"], 4 * n)
            for j in range(TG):
                pool.wait_ge(B_in, 4 * n + j + 1)
                nc.gpsimd.tensor_tensor(U[:, j, :], T[par][:, j, :], row(R_LN1G), ALU.mult).then_inc(B["tg"], 1)
            for j in range(TG):
                pool.wait_ge(B["tg"], 4 * n + j + 1)
                nc.gpsimd.tensor_tensor(U[:, j, :], U[:, j, :], row(R_LN1B), ALU.add).then_inc(B["tgb"], 1)

        def pool_B2(pool, n, par):
            for j in range(TG):
                pool.wait_ge(B["u"], 4 * n + j + 1)
                nc.gpsimd.tensor_tensor(U[:, j, :], U[:, j, :], row(R_LN2G), ALU.mult).then_inc(B["ug"], 1)
            for j in range(TG):
                pool.wait_ge(B["ug"], 4 * n + j + 1)
                nc.gpsimd.tensor_tensor(U[:, j, :], U[:, j, :], row(R_LN2B), ALU.add).then_inc(B["ub"], 1)

        T_ps, T_sb, R_ps, R_sb, B_ps, B_sb = (sem(k) for k in "T_ps T_sb R_ps R_sb B_ps B_sb".split())
        dstep, astep = sem("vector_step"), sem("scalar_step")
        L_sc, L_rt, L_y = sem("norm_variance"), sem("norm_root"), sem("norm_rows")
        phase_end = sem("phase_end")
        keys_in, rec_done, rec_put, rec_back = (sem(k) for k in "keys_in rec_done rec_put rec_back".split())

        rows_in = {q: [sem(f"rows_in_{q}{g}") for g in range(EG)] for q in ("gather_a", "gather_b", "load")}

        class Arrival:
            def __init__(self, s, base):
                self.s, self.base = s, base

            def full(self, n):
                return self.s, n + self.base

        def per_group(q, base):
            return [Arrival(s, base) for s in rows_in[{"a": "gather_a", "b": "gather_b", "h": "load"}[q]]]

        Hd, X1d, X2d, X3d = (nc.dram_tensor(f"{n}_table", (2 * E, D), F32).ap() for n in ("h", "x1", "x2", "x3"))
        Yd = nc.dram_tensor("y_table", (E, D), F32).ap()
        PDd = nc.dram_tensor("part_rows", (E, D), F32).ap()
        RDd = nc.dram_tensor("records_by_dst", (E, Q_END), F32).ap()
        RSd = nc.dram_tensor("records_by_src", (E, Q_END), F32).ap()

        class Counts:
            def __init__(self):
                self.t = self.r = self.b = self.ln = self.y = self.d = self.a = self.ph = 0

        def end_phase(eng, c):
            eng.drain().then_inc(phase_end, 1)
            c.ph += 1
            eng.wait_ge(phase_end, 4 * c.ph)

        def gcols(ap2, g):
            return ap2[:, g * TG:(g + 1) * TG]

        rec = at(0, [ET, Q_END], P)
        kfc = at(17000, [2 * ET], P)
        cnts = at(17100, [2 * 6 * ET], P).rearrange("p (q a t) -> p q a t", q=2, a=6)
        rank_i = at(17400, [2, ET], P, I32)
        own = at(17500, [6, ET], P)
        RD = sb("RD", [P, ET, Q_END])
        RSs = sb("RSs", [P, ET, 3])
        bk = sb("bk", [NB, 2])
        bkm = sb("bkm", [NB, 2, ET])
        mask = sb("mask", [NB, ET])
        idd = sb("idd", [P, 7, ET], I32)
        ids = sb("ids", [P, 3, ET], I32)
        Sd = sb("Sd", [P, ET, P])
        Md = sb("Md", [NB, ET, P])
        Bd = sb("Bd", [P, NB * ET])
        abv = sb("abv", [P, 3])
        v20 = sb("v20", [P, 12, ET])
        lst = sb("lst", [P, TG, 6])
        lmv = sb("lmv", [P, TG, 2])
        lsr = sb("lsr", [P, TG])
        lrs = sb("lrs", [P, TG])
        s_end = sem("edge_constants")

        def b3(ap, n):
            return ap.unsqueeze(2).broadcast_to([ap.shape[0], ap.shape[1], n])

        def spread(ap, n):
            return ap.unsqueeze(1).broadcast_to([ap.shape[0], n, ap.shape[1]])

        def t_open(pe, c):
            if c.t >= 4:
                pe.wait_ge(T_sb, c.t - 3)
            c.t += 1
            return bank[(c.t - 1) % 4]

        def r_open(pe, c):
            if c.r >= 2:
                pe.wait_ge(R_sb, c.r - 1)
            c.r += 1
            return bank[4 + (c.r - 1) % 2]

        def b_open(pe, c):
            if c.b:
                pe.wait_ge(B_sb, c.b)
            c.b += 1
            return bank[7]

        def pe_transpose_rows(pe, c, rows4, interleaved=False):
            for k in range(KC):
                b = t_open(pe, c)
                for j in range(TG):
                    if interleaved and k:
                        src = vec3(rows4[:, j, 128:D])[:, k - 1, :]
                    else:
                        src = rows4[:, j, k * 128:(k + 1) * 128]
                    i = nc.tensor.transpose(b[:, j * P:(j + 1) * P], src, ident[0:P, 0:P])
                i.then_inc(T_ps, 1)

        def pe_transpose_back(pe, c, fT):
            for j in range(TG):
                b = r_open(pe, c)
                for k in range(KC):
                    i = nc.tensor.transpose(b[0:P, k * 128:(k + 1) * 128], fT[:, k, j * P:(j + 1) * P],
                                            ident[:, :])
                i.then_inc(R_ps, 1)

        def pe_boundaries(pe, c, B, V, n, ready=None):
            b = b_open(pe, c)
            for t in range(ET):
                if ready is not None and t % TG == 0:
                    pe.wait_ge(*ready(t // TG))
                i = nc.tensor.matmul(b[0:NB, 0:n], B[:, t * NB:(t + 1) * NB], V(t), start=t == 0,
                                     stop=t == ET - 1)
            i.then_inc(B_ps, 1)

        def pe_segment_T(pe, c, b, S, M, V, bf, g, k, fresh):
            for j in range(TG):
                t = TG * g + j
                nc.tensor.matmul(b[:, j * P:(j + 1) * P], V[:, t, k * 128:(k + 1) * 128], S[:, t, :],
                                 start=fresh and j == 0, stop=False)
                i = nc.tensor.matmul(b[:, j * P:(j + 1) * P], bf[0:NB, k * 128:(k + 1) * 128], M[:, t, :],
                                     start=False, stop=j == TG - 1)
            return i

        def pe_segment_narrow(pe, c, S, M, V, bf, n):
            b = r_open(pe, c)
            for t in range(ET):
                nc.tensor.matmul(b[0:P, t * n:(t + 1) * n], S[:, t, :], V(t), start=t == 0, stop=False)
                i = nc.tensor.matmul(b[0:P, t * n:(t + 1) * n], M[:, t, :], bf[0:NB, 0:n], start=False,
                                     stop=t == ET - 1)
            i.then_inc(R_ps, 1)

        def pe_rows_out(pe, c, pairs, n=D):
            for j in range(TG):
                b = r_open(pe, c)
                last = len(pairs) * KC - 1
                for q, (fT, W) in enumerate(pairs):
                    for k in range(KC):
                        i = nc.tensor.matmul(b[0:P, 0:n], fT[:, k, j * P:(j + 1) * P], W[:, k, :],
                                             start=q * KC + k == 0, stop=q * KC + k == last)
                i.then_inc(R_ps, 1)

        def act_evac(act, c, dst, src_rows=128, n=GR, func=ACT.Identity, **kw):
            act.wait_ge(T_ps, c.t + 1)
            c.t += 1
            nc.scalar.activation(dst, bank[(c.t - 1) % 4][0:src_rows, 0:n], func, **kw).then_inc(T_sb, 1)

        def act_root(act, c):
            act.wait_ge(L_sc, c.ln + 1)
            c.ln += 1
            nc.scalar.activation(lsr[:, :], lsr[:, :], ACT.Sqrt).then_inc(L_rt, 1)

        def link(dve, c, ins):
            ins.then_inc(dstep, 1)
            c.d += 1
            dve.wait_ge(dstep, c.d)

        def dve_evac(dve, c, f):
            dve.wait_ge(R_ps, c.r + 1)
            c.r += 1
            f(bank[4 + (c.r - 1) % 2]).then_inc(R_sb, 1)

        def dve_b_evac(dve, c, dst, n):
            dve.wait_ge(B_ps, c.b + 1)
            c.b += 1
            nc.vector.tensor_copy(dst, bank[7][0:NB, 0:n]).then_inc(B_sb, 1)

        def dve_ln(dve, c, rows4, doubled=False):
            for j in range(TG):
                i = nc.vector.bn_stats(lst[:, j, :], rows4[:, j, :])
            link(dve, c, i)
            for j in range(TG):
                i = nc.vector.bn_aggr(lmv[:, j, :], lst[:, j, :])
            link(dve, c, i)
            nc.vector.tensor_scalar(lsr[:, :], lmv[:, :, 1], 4.0 if doubled else 1.0, EPS, ALU.mult,
                                    ALU.add).then_inc(L_sc, 1)
            c.ln += 1
            dve.wait_ge(L_rt, c.ln)
            link(dve, c, nc.vector.reciprocal(lrs[:, :], lsr[:, :]))
            if doubled:
                link(dve, c, nc.vector.tensor_scalar_mul(lrs[:, :], lrs[:, :], 2.0))
            for j in range(TG):
                nc.vector.tensor_scalar(rows4[:, j, :], rows4[:, j, :], lmv[:, j, 0:1], lrs[:, j:j + 1],
                                        ALU.subtract, ALU.mult).then_inc(L_y, 1)
            c.y += TG
            dve.wait_ge(L_y, c.y)

        def gather(dst, table, idx, s, limit=None):
            nc.gpsimd.indirect_dma_start(out=dst, out_offset=None, in_=table,
                                         in_offset=bass.IndirectOffsetOnAxis(ap=idx, axis=0),
                                         bounds_check=limit, oob_is_err=limit is None).then_inc(s.s, 16)

        def store(sp, table, base, g, rows4, s):
            dst = grp(table[base:base + E, :], g)
            sp.dma_start(dst[0:HI], rows4[0:HI]).then_inc(s, 16)
            sp.dma_start(dst[HI:P], rows4[HI:P]).then_inc(s, 16)

        def load(sp, rows4, table, base, g, s):
            src = grp(table[base:base + E, :], g)
            sp.dma_start(rows4[0:HI], src[0:HI]).then_inc(s.s, 16)
            sp.dma_start(rows4[HI:P], src[HI:P]).then_inc(s.s, 16)

        def scatter(table, idx, src, s, limit=N - 1):
            nc.gpsimd.indirect_dma_start(out=table, out_offset=bass.IndirectOffsetOnAxis(ap=idx, axis=0),
                                         in_=src, in_offset=None, bounds_check=limit,
                                         oob_is_err=False).then_inc(s, 16)

        KI = at(1000, [2, E], P, I32)
        KF = at(6000, [2, E], P)
        junk = at(11000, [E], P)
        tri = at(13500, [P], P)
        ones = sb("ones", [P, P])
        diag = at(14000, [ET, P], P)
        kci = at(17700, [2 * ET], P, I32)

        def sp_records(sp, c):
            sp.wait_ge(C["out"], 32 * NG)
            for q in range(2):
                sp.dma_start(KI[:, q, :], keys[q].partition_broadcast(P)).then_inc(keys_in, 16)
            sp.dma_start(kci, key_cols).then_inc(keys_in, 16)
            sp.dma_start(rec[:, :, :], rec_in.rearrange("(t p) q -> p t q", p=P)).then_inc(keys_in, 16)
            sp.dma_start(tri, tri_in).then_inc(keys_in, 16)
            sp.dma_start(mask[:, :], mask_in).then_inc(keys_in, 16)
            sp.dma_start(abv[:, :], abs_in[0].partition_broadcast(P)).then_inc(keys_in, 16)
            sp.wait_ge(rec_put, 16 * 2 * ET)
            dv = RDd.rearrange("(t p) q -> p t q", p=P)
            sv = RSd.rearrange("(t p) q -> p t q", p=P)
            sp.dma_start(RD[:, :, :], dv).then_inc(rec_back, 16)
            sp.dma_start(rec[:, :, :], sv).then_inc(rec_back, 16)
            with nc.allow_non_contiguous_dma(reason="one key of each boundary record"):
                for q, (v, col) in enumerate(((dv, Q_DST), (sv, Q_SRC))):
                    sp.dma_start(bk[0:ET, q:q + 1], v[0, :, col:col + 1]).then_inc(rec_back, 16)
                    sp.dma_start(bk[ET:NB, q:q + 1], v[P - 1, :, col:col + 1]).then_inc(rec_back, 16)

        def dve_records(dve, c):
            dve.wait_ge(keys_in, 16 * 7)
            nc.vector.tensor_copy(KF[:, :, :], KI[:, :, :])
            link(dve, c, nc.vector.tensor_copy(kfc, kci))
            link(dve, c, nc.vector.memset(cnts[:, :, :, :], 0.0))
            for q in range(2):
                for t in range(ET):
                    me = kfc[:, q * ET + t:q * ET + t + 1]
                    todo = [(0, ALU.is_lt, 0, E)] + ([(1, ALU.is_equal, 0, t * P)] if t else []) \
                        + [(3, ALU.is_le, 0, E), (4, ALU.is_lt, 0, E), (5, ALU.is_le, 0, E)]
                    for a, op, lo, hi in todo:
                        link(dve, c, nc.vector.tensor_scalar(junk[:, 0:hi - lo],
                                                             KF[:, 1 - q if a > 3 else q, lo:hi], me, None,
                                                             op, ALU.add, accum_out=cnts[:, q, a, t:t + 1]))
                    link(dve, c, nc.vector.scalar_tensor_tensor(
                        junk[:, 0:P], KF[:, q, t * P:(t + 1) * P], me, tri, ALU.is_equal, ALU.mult,
                        accum_out=cnts[:, q, 2, t:t + 1]))
            dup = v20[:, 0:2, :]
            link(dve, c, nc.vector.tensor_tensor(dup, cnts[:, :, 1, :], cnts[:, :, 2, :], ALU.add))
            link(dve, c, nc.vector.tensor_tensor(v20[:, 2:4, :], cnts[:, :, 0, :], dup, ALU.add))
            link(dve, c, nc.vector.tensor_copy(rank_i[:, :, :], v20[:, 2:4, :]))
            link(dve, c, nc.vector.tensor_tensor(own[:, 0:2, :], cnts[:, :, 5, :], cnts[:, :, 4, :], ALU.subtract))
            link(dve, c, nc.vector.tensor_scalar_min(own[:, 0:2, :], own[:, 0:2, :], 1.0))
            link(dve, c, nc.vector.tensor_scalar_add(own[:, 2, :], v20[:, 2, :], float(E)))
            link(dve, c, nc.vector.tensor_tensor(own[:, 3, :], cnts[:, 0, 4, :], own[:, 2, :], ALU.subtract))
            link(dve, c, nc.vector.tensor_tensor(own[:, 3, :], own[:, 3, :], own[:, 0, :], ALU.mult))
            link(dve, c, nc.vector.tensor_tensor(own[:, 3, :], own[:, 3, :], own[:, 2, :], ALU.add))
            link(dve, c, nc.vector.scalar_tensor_tensor(own[:, 4, :], cnts[:, 1, 4, :], float(E), v20[:, 2, :],
                                                        ALU.add, ALU.subtract))
            link(dve, c, nc.vector.tensor_tensor(own[:, 4, :], own[:, 4, :], own[:, 1, :], ALU.mult))
            link(dve, c, nc.vector.tensor_tensor(own[:, 4, :], own[:, 4, :], v20[:, 2, :], ALU.add))
            link(dve, c, nc.vector.tensor_scalar(own[:, 5, :], own[:, 0, :], -float(FAR), float(FAR), ALU.mult,
                                                 ALU.add))
            link(dve, c, nc.vector.tensor_tensor(own[:, 5, :], own[:, 5, :], cnts[:, 0, 4, :], ALU.add))
            link(dve, c, nc.vector.tensor_scalar(v20[:, 4:6, :], dup, 1.0, float(FAR), ALU.min, ALU.mult))
            link(dve, c, nc.vector.tensor_tensor(v20[:, 6:8, :], v20[:, 4:6, :],
                                                 kfc.rearrange("p (q t) -> p q t", q=2), ALU.add))
            for col, src in ((Q_DST, kfc[:, 0:ET]), (Q_SRC, kfc[:, ET:2 * ET]), (Q_DSC, v20[:, 6, :]),
                             (Q_SSC, v20[:, 7, :]), (Q_DUP, v20[:, 0, :]), (Q_RS, v20[:, 3, :]),
                             (Q_XD, own[:, 2, :]), (Q_DI, own[:, 3, :]), (Q_SI, own[:, 4, :]),
                             (Q_YI, own[:, 5, :])):
                nc.vector.tensor_copy(rec[:, :, col], src)
            nc.vector.tensor_tensor(rec[:, :, Q_CNT], cnts[:, 0, 3, :], cnts[:, 0, 0, :],
                                    ALU.subtract).then_inc(rec_done, 1)
            dve.wait_ge(rec_back, 16 * 6)
            for k, col in enumerate((Q_DST, Q_SRC, Q_DSC, Q_SSC, Q_SI, Q_DI, Q_RS)):
                nc.vector.tensor_copy(idd[:, k, :], RD[:, :, col])
            for k, col in enumerate((Q_XD, Q_SI, Q_YI)):
                nc.vector.tensor_copy(ids[:, k, :], rec[:, :, col])
            for k, col in enumerate((Q_DST, Q_SRC, Q_W)):
                i = nc.vector.tensor_copy(RSs[:, :, k], rec[:, :, col])
            i.then_inc(rec_done, 1)
            nc.vector.memset(ones[:, :], 1.0)
            nc.vector.tensor_scalar_add(bk[:, :], bk[:, :], 1.0)
            link(dve, c, nc.vector.memset(Bd[:, :], 0.0))
            for q in range(2):
                i = nc.vector.tensor_scalar(bkm[:, q, :], mask[:, :], bk[:, q:q + 1], None, ALU.mult)
            link(dve, c, i)
            link(dve, c, nc.vector.tensor_scalar_add(bkm[:, :, :], bkm[:, :, :], -1.0))

        def dve_build(dve, c, q, key, S, M, dg):
            dve.wait_ge(dstep, c.d)
            nc.vector.tensor_tensor(dg[:, :, :], spread(ident[0:P, 0:P], ET), b3(key, P), ALU.mult).then_inc(s_end, 1)
            for g in range(EG):
                kt = gcols(key, g)
                dve.wait_ge(R_ps, c.r + 1)
                b = bank[4 + c.r % 2]
                c.r += 1
                row = b[0:P, 0:GR].rearrange("p (t f) -> p t f", f=P)
                nc.vector.tensor_tensor(S[:, g * TG:(g + 1) * TG, :], row, b3(kt, P), ALU.is_equal)
                nc.vector.tensor_tensor(M[:, g * TG:(g + 1) * TG, :],
                                        b[0:NB, 0:GR].rearrange("p (t f) -> p t f", f=P),
                                        b3(gcols(bkm[:, q, :], g), P), ALU.is_equal).then_inc(R_sb, 1)
            dve.wait_ge(R_sb, c.r)

        def pe_build(pe, c, dg, n):
            pe.wait_ge(s_end, n)
            for g in range(EG):
                b = r_open(pe, c)
                nc.tensor.matmul(b[0:P, 0:GR], ones[:, :], dg[:, g * TG:(g + 1) * TG, :].rearrange("p t f -> p (t f)"),
                                 start=True, stop=True).then_inc(R_ps, 1)

        def dve_boundary_cols(dve, c, B, S, done):
            nc.vector.tensor_copy(B[:, 0:(ET - 1) * (NB + 1) + 1:NB + 1], S[:, :, 0])
            nc.vector.tensor_copy(B[:, ET:ET + (ET - 1) * (NB + 1) + 1:NB + 1], S[:, :, P - 1]).then_inc(done, 1)

        def pool_records(pool, c):
            pool.wait_ge(rec_done, 1)
            for q, table in enumerate((RDd, RSd)):
                for t in range(ET):
                    scatter(table, rank_i[:, q, t:t + 1], rec[:, t, :], rec_put, E - 1)
            pool.wait_ge(rec_done, 2)

        W1l, W2l = at(4096, [KC, D]), at(6144, [KC, D])
        V0 = at(8192, [ET, D], P)
        SN = at(18432, [ET, P], P)
        BN = at(20932, [NB * ET], P)
        BF0 = at(21732, [D], NB)
        XD0 = [at(22244, [TG, D], P), at(24292, [TG, D], P)]
        ZZ0 = at(26340, [TG, D], P)
        HR0 = at(28388, [TG, D], P)
        XT0, HT0, AT0 = at(30436, [KC, GR]), at(32436, [KC, GR]), at(34436, [KC, GR])
        w0_in = sem("layer0_weights_in")
        e0_x, e0_xd, e0_h, e0_pd = per_group("a", 0), per_group("b", 0), per_group("a", 64), per_group("h", 0)
        h_put, x1_put, pd_put, bn0 = sem("h_put"), sem("x1_put"), sem("pd_put"), sem("mean_weights")
        pd_sem = sem("part_rows_ready")

        def grp(dram, g):
            return dram[g * GR:(g + 1) * GR, :].rearrange("(t p) d -> p t d", p=P)

        def sp_L0(sp, c):
            sp.wait_ge(phase_end, 4 * c.ph)
            for dst, src in ((W1r, w_r1), (W2r, w_r2), (W1l, w_l1), (W2l, w_l2)):
                sp.dma_start(dst, src).then_inc(w0_in, 16)
            for g in range(EG):
                c.r += TG
                sp.wait_ge(R_sb, c.r)
                store(sp, Hd, 0, g, HR0, h_put)
                c.r += TG
                c.y += TG
                sp.wait_ge(L_y, c.y)
                store(sp, X1d, 0, g, ZZ0, x1_put)
            for g in range(EG):
                c.r += TG
                sp.wait_ge(R_sb, c.r)
                store(sp, Hd, E, g, HR0, h_put)
                c.r += TG
                sp.wait_ge(pd_sem, g + 1)
                store(sp, PDd, 0, g, ZZ0, pd_put)
            sp.wait_ge(pd_put, 32 * EG)
            for g in range(2):
                sp.wait_ge(R_sb, c.r)
                load(sp, XD0[g], PDd, 0, g, e0_pd[g])
            for g in range(EG):
                c.r += TG
                c.y += TG
                sp.wait_ge(L_y, c.y)
                store(sp, X1d, E, g, ZZ0, x1_put)
                if g + 2 < EG:
                    load(sp, XD0[g % 2], PDd, 0, g + 2, e0_pd[g + 2])
            sp.wait_ge(x1_put, 2 * 32 * EG)

        def sp_L1(sp, c):
            for g in range(EG):
                load(sp, CR[:, g * TG:(g + 1) * TG, :], X1d, E, g, e1_b[g])
            for g in range(EG):
                c.y += TG
                sp.wait_ge(L_y, c.y)
                store(sp, X2d, E, g, CR[:, g * TG:(g + 1) * TG, :], x2_put)
            c.r += EG + 1 + ET

            def step(i):
                for g in range(EG):
                    if isinstance(i, int) and i == 1:
                        sp.wait_ge(y_rdy, TG * (g + 1))
                    else:
                        sp.wait_ge(R_sb, i * ET + (c.r - 2 * ET + TG * (g + 1)))
                    store(sp, Yd, 0, g, Y[:, g * TG:(g + 1) * TG, :], y_put)
            step(1)
            with sp.Fori(2, ITERS) as i:
                step(i)
            c.r += ET * (ITERS - 1)
            for g in range(EG):
                c.y += TG
                sp.wait_ge(L_y, c.y)
                store(sp, X2d, 0, g, Y[:, g * TG:(g + 1) * TG, :], x2_put)
            sp.wait_ge(x2_put, 2 * 32 * EG)

        def pool_L0(pool, c):
            for t in range(ET):
                gather(V0[:, t, :], x, idd[:, 1, t:t + 1], e0_x[t // TG])
            for g in range(2):
                for j in range(TG):
                    gather(XD0[g][:, j, :], x, idd[:, 0, TG * g + j:TG * g + j + 1], e0_xd[g])
            c.r += 2 * TG * EG
            for g in range(EG):
                if g >= 2:
                    pool.wait_ge(R_sb, c.r - TG * 2)
                    for j in range(TG):
                        gather(XD0[g % 2][:, j, :], x, idd[:, 0, TG * g + j:TG * g + j + 1], e0_xd[g])
                c.r += 2 * TG
            pool.wait_ge(h_put, 2 * 32 * EG)
            pool.wait_ge(T_sb, c.t + 8 * EG + 12 * EG)
            for t in range(ET):
                gather(V0[:, t, :], Hd, idd[:, 4, t:t + 1], e0_h[t // TG])
            c.r += TG * EG
            c.t += 8 * EG + 12 * EG + 4 * EG
            c.y += 2 * TG * EG
            pool.wait_ge(x1_put, 2 * 32 * EG)

        def pe_L0(pe, c):
            pe.wait_ge(w0_in, 16 * 4)
            for g in range(EG):
                pe.wait_ge(*e0_x[g].full(16 * TG))
                pe_transpose_rows(pe, c, V0[:, g * TG:(g + 1) * TG, :])
                pe.wait_ge(T_sb, c.t)
                for m in range(KC):
                    b = t_open(pe, c)
                    for k in range(KC):
                        i = nc.tensor.matmul(b[:, 0:GR], W1r[:, k, m * 128:(m + 1) * 128], XT0[:, k, :],
                                             start=k == 0, stop=k == KC - 1)
                    i.then_inc(T_ps, 1)
                pe.wait_ge(T_sb, c.t)
                pe_transpose_back(pe, c, HT0)
                pe_rows_out(pe, c, [(HT0, W2r)])
            pe.wait_ge(bn0, 1)
            pe_boundaries(pe, c, BN, lambda t: V0[:, t, :], D)
            for g in range(EG):
                pe.wait_ge(*e0_xd[g].full(16 * TG))
                pe_transpose_rows(pe, c, XD0[g % 2])
                pe.wait_ge(B_sb, c.b)
                for k in range(KC):
                    b = t_open(pe, c)
                    pe_segment_T(pe, c, b, SN, Md, V0, BF0, g, k, True).then_inc(T_ps, 1)
                pe.wait_ge(T_sb, c.t)
                for m in range(KC):
                    b = t_open(pe, c)
                    for q, (fT, W) in enumerate(((XT0, W1r), (AT0, W1l))):
                        for k in range(KC):
                            i = nc.tensor.matmul(b[:, 0:GR], W[:, k, m * 128:(m + 1) * 128], fT[:, k, :],
                                                 start=q + k == 0, stop=q == 1 and k == KC - 1)
                    i.then_inc(T_ps, 1)
                pe.wait_ge(T_sb, c.t)
                pe_transpose_back(pe, c, HT0)
                pe_rows_out(pe, c, [(HT0, W2r)])
            pe_boundaries(pe, c, BN, lambda t: V0[:, t, :], D, lambda g: e0_h[g].full(16 * TG))
            pe.wait_ge(B_sb, c.b)
            for g in range(EG):
                for k in range(KC):
                    b = t_open(pe, c)
                    pe_segment_T(pe, c, b, SN, Md, V0, BF0, g, k, True).then_inc(T_ps, 1)
                pe.wait_ge(T_sb, c.t)
                pe_rows_out(pe, c, [(AT0, W2l)])

        def act_L0(act, c):
            for loop in range(2):
                for g in range(EG):
                    for k in range(KC):
                        act_evac(act, c, XT0[:, k, :])
                    if loop == 1:
                        for k in range(KC):
                            act_evac(act, c, AT0[:, k, :])
                    if c.r:
                        act.wait_ge(R_ps, c.r)
                    for m in range(KC):
                        act_evac(act, c, HT0[:, m, :], func=ACT.Relu, bias=colv[:, C_L0B1 + m:C_L0B1 + m + 1])
                    if loop == 0:
                        act_root(act, c)
                    c.r += 2 * TG
            for g in range(EG):
                act.wait_ge(R_ps, c.r)
                for k in range(KC):
                    act_evac(act, c, AT0[:, k, :])
                act_root(act, c)
                c.r += TG

        def dve_L0(dve, c):
            link(dve, c, nc.vector.reciprocal(v20[:, 8, :], RD[:, :, Q_CNT]))
            link(dve, c, nc.vector.tensor_tensor(SN[:, :, :], Sd[:, :, :], b3(v20[:, 8, :], P), ALU.mult))
            link(dve, c, nc.vector.memset(BN, 0.0))
            dve_boundary_cols(dve, c, BN, SN, bn0)
            dve.wait_ge(bn0, 1)
            b2row = spread(row(R_L0B2), TG)
            for loop in range(2):
                for g in range(EG):
                    res = V0[:, g * TG:(g + 1) * TG, :] if loop == 0 else XD0[g % 2]
                    if loop == 0:
                        dve.wait_ge(*e0_x[g].full(16 * TG))
                    else:
                        dve.wait_ge(*e0_xd[g].full(16 * TG))
                    if loop or g:
                        dve.wait_ge(h_put, 32 * (EG * loop + g))
                    for j in range(TG):
                        dve_evac(dve, c, lambda b: nc.vector.tensor_copy(HR0[:, j, :], b[0:P, :]))
                    if loop == 0 and g:
                        dve.wait_ge(x1_put, 32 * g)
                    if loop == 1:
                        dve.wait_ge(x1_put, 32 * EG)
                        if g:
                            dve.wait_ge(pd_put, 32 * g)
                    for j in range(TG):
                        dve_evac(dve, c, lambda b: nc.vector.tensor_tensor(ZZ0[:, j, :], res[:, j, :],
                                                                           b[0:P, :], ALU.add))
                    dve.wait_ge(R_sb, c.r)
                    i = nc.vector.tensor_tensor(ZZ0, ZZ0, b2row, ALU.add)
                    if loop == 1:
                        i.then_inc(pd_sem, 1)
                    else:
                        link(dve, c, i)
                        dve_ln(dve, c, ZZ0)
                dve_b_evac(dve, c, BF0, D)
            dve.wait_ge(pd_put, 32 * EG)
            for g in range(EG):
                dve.wait_ge(*e0_pd[g].full(32))
                if g:
                    dve.wait_ge(x1_put, 32 * (EG + g))
                for j in range(TG):
                    dve_evac(dve, c, lambda b: nc.vector.tensor_tensor(ZZ0[:, j, :], XD0[g % 2][:, j, :],
                                                                       b[0:P, :], ALU.add))
                dve.wait_ge(R_sb, c.r)
                dve_ln(dve, c, ZZ0)

        Ss, Ms = at(0, [ET, P], P), at(2500, [ET, P], NB)
        BW = at(5000, [NB * ET], P)
        BF1 = at(5800, [D], NB)
        V1, Y, CR = at(6312, [ET, D], P), at(16552, [ET, D], P), at(26792, [ET, D], P)
        J1 = at(37032, [2, D], P)
        diag1 = at(16552, [ET, P], P)
        e1_b, e1_v, e1_x, e1_y, e1_f = (per_group(*q) for q in (
            ("h", 32), ("a", 128), ("b", 64), ("a", 192), ("b", 128)))
        x2_put, y_put = sem("x2_put"), sem("y_put")
        sc1, sc1a = sem("layer1_scalars"), sem("layer1_scalars_act")
        sup_rdy, w1_rdy, zr, y_rdy = sem("sup_ready"), sem("weights1_ready"), sem("zero_rows"), sem("y_ready")
        SUP, NN, RR, NRR, SD, SSQ, DSQ, TMP = (v20[:, k, :] for k in range(8))

        def pool_L1(pool, c):
            for t in range(ET):
                gather(V1[:, t, :], X1d, ids[:, 0, t:t + 1], e1_v[t // TG])
            pool.wait_ge(R_sb, c.r + EG)
            for t in range(ET):
                gather(Y[:, t, :], X1d, ids[:, 1, t:t + 1], e1_x[t // TG])
            c.r += EG + 1 + ET
            c.y += ET
            pool.wait_ge(zr, 1)
            for i in range(1, ITERS):
                pool.wait_ge(y_put, i * (32 * EG))
                pool.wait_ge(R_sb, i * ET + (c.r - ET))
                for t in range(ET):
                    gather(V1[:, t, :], Yd, ids[:, 2, t:t + 1], e1_y[t // TG], E - 1)
            c.r += ET * (ITERS - 1)
            pool.wait_ge(R_sb, c.r)
            for t in range(ET):
                gather(CR[:, t, :], X1d, ids[:, 1, t:t + 1], e1_f[t // TG])
            c.y += ET
            pool.wait_ge(x2_put, 2 * 32 * EG)

        def pe_segment_rows(pe, c, V, ring):
            for t in range(ET):
                b = ring(t)
                nc.tensor.matmul(b[0:P, :], Ss[:, t, :], V[:, t, :], start=True, stop=False)
                nc.tensor.matmul(b[0:P, :], Ms[:, t, :], BF1[:, :], start=False, stop=True).then_inc(R_ps, 1)

        def pe_L1(pe, c):
            pe_build(pe, c, diag1, 2)
            pe.wait_ge(sup_rdy, 1)
            pe_boundaries(pe, c, BW, lambda t: SUP[:, t:t + 1], 1)
            pe.wait_ge(B_sb, c.b)
            pe_segment_narrow(pe, c, Ss, Ms, lambda t: SUP[:, t:t + 1], BF1, 1)
            pe.wait_ge(w1_rdy, 2)
            pe_boundaries(pe, c, BW, lambda t: V1[:, t, :], D)
            pe.wait_ge(B_sb, c.b)
            pe_segment_rows(pe, c, V1, lambda t: r_open(pe, c))
            r0, b0 = c.r, c.b
            assert ET % 2 == 0

            def step(i):
                def ring(t):
                    pe.wait_ge(R_sb, i * ET + (r0 - ET + t - 1))
                    return bank[4 + (r0 + t) % 2]
                pe.wait_ge(B_sb, i + (b0 - 1))
                for t in range(ET):
                    if t % TG == 0:
                        pe.wait_ge(*e1_y[t // TG].full(i * (16 * TG)))
                    q = nc.tensor.matmul(bank[7][0:NB, :], BW[:, t * NB:(t + 1) * NB], V1[:, t, :],
                                         start=t == 0, stop=t == ET - 1)
                q.then_inc(B_ps, 1)
                pe.wait_ge(B_sb, i + b0)
                pe_segment_rows(pe, c, V1, ring)
            step(1)
            with pe.Fori(2, ITERS) as i:
                step(i)
            c.r = r0 + ET * (ITERS - 1)
            c.b = b0 + ITERS - 1

        def act_L1(act, c):
            for g in range(EG):
                act_root(act, c)
            act.wait_ge(sc1, 1)
            nc.scalar.activation(v20[:, 5:7, :], v20[:, 5:7, :], ACT.Sqrt).then_inc(sc1a, 1)
            nc.scalar.activation(abv[:, :], abv[:, :], ACT.Exp).then_inc(sc1a, 1)
            act.wait_ge(sc1, 2)
            nc.scalar.activation(SD, SD, ACT.Exp).then_inc(sc1a, 1)
            for g in range(EG):
                act_root(act, c)

        def dve_L1(dve, c):
            dve_build(dve, c, 1, RSs[:, :, 1], Ss, Ms, diag1)
            link(dve, c, nc.vector.memset(BW, 0.0))
            dve_boundary_cols(dve, c, BW, Ss, w1_rdy)
            dve.wait_ge(w1_rdy, 1)
            for g in range(EG):
                dve.wait_ge(*e1_b[g].full(32))
                dve_ln(dve, c, CR[:, g * TG:(g + 1) * TG, :], doubled=True)
            for t in range(ET):
                if t % TG == 0:
                    dve.wait_ge(*e1_v[t // TG].full(16 * TG))
                    dve.wait_ge(*e1_x[t // TG].full(16 * TG))
                for k, (p, q) in enumerate(((Y, V1), (Y, Y), (V1, V1))):
                    link(dve, c, nc.vector.scalar_tensor_tensor(
                        J1[:, k % 2, :], p[:, t, :], 1.0, q[:, t, :], ALU.mult, ALU.mult,
                        accum_out=v20[:, 4 + k, t:t + 1]))
            nc.vector.tensor_scalar_max(v20[:, 5:7, :], v20[:, 5:7, :], 1e-12).then_inc(sc1, 1)
            dve.wait_ge(sc1a, 2)
            link(dve, c, nc.vector.reciprocal(v20[:, 5:7, :], v20[:, 5:7, :]))
            link(dve, c, nc.vector.tensor_tensor(SD, SD, SSQ, ALU.mult))
            link(dve, c, nc.vector.tensor_tensor(SD, SD, DSQ, ALU.mult))
            link(dve, c, nc.vector.tensor_tensor(TMP, RSs[:, :, 0], RSs[:, :, 1], ALU.not_equal))
            link(dve, c, nc.vector.tensor_tensor(SD, SD, TMP, ALU.mult))
            sg = v20[:, 8, 0:1]
            link(dve, c, nc.vector.tensor_tensor(sg, abv[:, 2:3], abv[:, 2:3], ALU.mult))
            link(dve, c, nc.vector.tensor_scalar_mul(sg, sg, 4.0))
            link(dve, c, nc.vector.reciprocal(sg, sg))
            nc.vector.tensor_scalar(SD, SD, sg, None, ALU.mult).then_inc(sc1, 1)
            dve.wait_ge(sc1a, 3)
            nc.vector.tensor_tensor(SUP, SD, RSs[:, :, 2], ALU.mult).then_inc(sup_rdy, 1)
            dve_b_evac(dve, c, BF1[:, 0:1], 1)
            dve_evac(dve, c, lambda b: nc.vector.tensor_copy(NN, b[0:P, 0:ET]))
            dve.wait_ge(R_sb, c.r)
            al, be = abv[:, 0:1], abv[:, 1:2]
            link(dve, c, nc.vector.tensor_scalar(RR, NN, al, be, ALU.mult, ALU.add))
            link(dve, c, nc.vector.tensor_scalar(RR, RR, al, None, ALU.add))
            link(dve, c, nc.vector.reciprocal(RR, RR))
            link(dve, c, nc.vector.tensor_scalar(RR, RR, al, None, ALU.mult))
            link(dve, c, nc.vector.scalar_tensor_tensor(NRR, RR, -1.0, NN, ALU.mult, ALU.mult))
            link(dve, c, nc.vector.tensor_tensor(TMP, SUP, RR, ALU.mult))
            link(dve, c, nc.vector.tensor_tensor(Ss[:, :, :], Ss[:, :, :], b3(TMP, P), ALU.mult))
            dve_boundary_cols(dve, c, BW, Ss, w1_rdy)
            dve.wait_ge(w1_rdy, 2)
            dve_b_evac(dve, c, BF1, D)
            dve.wait_ge(x2_put, 32 * EG)
            for t in range(ET):
                dve_evac(dve, c, lambda b: nc.vector.scalar_tensor_tensor(
                    CR[:, t, :], Y[:, t, :], NRR[:, t:t + 1], b[0:P, :], ALU.mult, ALU.add))
            dve.wait_ge(R_sb, c.r)
            for t in range(ET):
                nc.vector.tensor_copy(Y[:, t, :], CR[:, t, :]).then_inc(y_rdy, 1)
            dve.wait_ge(y_rdy, ET)
            for t in range(0, ET, TG):
                i = nc.vector.memset(V1[:, t:t + TG, :], 0.0)
            i.then_inc(zr, 1)
            r0, b0 = c.r, c.b
            pre = sem("y_before_sums")

            def step(i):
                dve.wait_ge(y_put, i * (32 * EG))
                for t in range(ET):
                    nc.vector.scalar_tensor_tensor(Y[:, t, :], Y[:, t, :], RR[:, t:t + 1], CR[:, t, :],
                                                   ALU.mult, ALU.add).then_inc(pre, 1)
                dve.wait_ge(B_ps, i + b0)
                nc.vector.tensor_copy(BF1, bank[7][0:NB, :]).then_inc(B_sb, 1)
                dve.wait_ge(pre, i * ET)
                for t in range(ET):
                    dve.wait_ge(R_ps, i * ET + (r0 - ET + t + 1))
                    nc.vector.tensor_tensor(Y[:, t, :], Y[:, t, :], bank[4 + (r0 + t) % 2][0:P, :],
                                            ALU.add).then_inc(R_sb, 1)
                dve.wait_ge(R_sb, i * ET + r0)
            step(1)
            with dve.Fori(2, ITERS) as i:
                step(i)
            c.r, c.b = r0 + ET * (ITERS - 1), b0 + ITERS - 1
            for g in range(EG):
                dve.wait_ge(*e1_f[g].full(16 * TG))
                Yg = Y[:, g * TG:(g + 1) * TG, :]
                link(dve, c, nc.vector.scalar_tensor_tensor(
                    Yg.rearrange("p t d -> p (t d)"), CR[:, g * TG:(g + 1) * TG, :].rearrange("p t d -> p (t d)"),
                    2.0, Yg.rearrange("p t d -> p (t d)"), ALU.mult, ALU.add))
                dve_ln(dve, c, Yg)

        WQ, WK, WV, WO = (at(2048 * k, [KC, D]) for k in range(4))
        V2 = at(8192, [ET, D], P)
        BF2 = at(18432, [D], NB)
        XS2, XD2, KQ2, T2, U2 = (at(18944 + G4 * k, [TG, D], P) for k in range(5))
        XT2, YT2, TT2 = (at(29184 + 2000 * k, [KC, GR]) for k in range(3))
        F1T2 = at(35184, [GR], 32)
        eT, negT, FT = (at(18944 + 2500 * k, [E], H) for k in range(3))
        EE, EN, EX, FC = (at(35684 + ET * H * k, [ET, H], P) for k in range(4))
        w2_in, q_rdy, e_rdy, f_rdy, ft_rdy = (sem(k) for k in "w2_in q_ready e_ready fc_ready ft_ready".split())
        ex_in, ex_rdy, at_rdy, x3_put, bd_rdy = (sem(k) for k in "ex_in ex_ready attn_ready x3_put bd_ready".split())
        A_L1 = 192 + 64 * (ITERS - 1)
        x2_s, x2_d, x2_d2 = per_group("a", A_L1), per_group("b", 192), per_group("b", 256)

        def sp_L2(sp, c):
            sp.wait_ge(phase_end, 4 * c.ph)
            for dst, src in ((WQ, w_q), (WK, w_k), (WV, w_v), (WO, w_o)):
                sp.dma_start(dst, src).then_inc(w2_in, 16)
            for q in range(2):
                for g in range(EG):
                    c.y += 3 * TG
                    sp.wait_ge(L_y, c.y)
                    store(sp, X3d, q * E, g, U2, x3_put)
            sp.wait_ge(x3_put, 2 * 32 * EG)

        def sp_L3(sp, c):
            sp.wait_ge(phase_end, 4 * c.ph)
            sp.dma_start(RD[:, :, :], RSd.rearrange("(t p) q -> p t q", p=P)).then_inc(rec_back, 16)

        def pe_ffn(pe, c, rows, TT, F1T):
            pe_transpose_rows(pe, c, rows)
            pe.wait_ge(T_sb, c.t)
            b = t_open(pe, c)
            for k in range(KC):
                i = nc.tensor.matmul(b[0:32, 0:GR], wcol(W_L2A + 32 * k, 32), TT[:, k, :], start=k == 0,
                                     stop=k == KC - 1)
            i.then_inc(T_ps, 1)
            pe.wait_ge(T_sb, c.t)
            for j in range(TG):
                b = r_open(pe, c)
                nc.tensor.matmul(b[0:P, :], F1T[:, j * P:(j + 1) * P], w32s[:, V_L2B:V_L2B + D], start=True,
                                 stop=True).then_inc(R_ps, 1)

        def act_ffn(act, c, TT, F1T):
            for k in range(KC):
                act_evac(act, c, TT[:, k, :], scale=colv[:, C_LN1G + k:C_LN1G + k + 1],
                         bias=colv[:, C_LN1B + k:C_LN1B + k + 1])
            act.wait_ge(R_ps, c.r)
            act_evac(act, c, F1T[:, :], src_rows=32, func=ACT.Relu, bias=colv[0:32, C_L2B1:C_L2B1 + 1])
            c.r += TG
            act_root(act, c)
            act_root(act, c)

        def dve_ffn(dve, c, Tn, Un, res):
            link(dve, c, nc.vector.tensor_tensor(Un, Tn, spread(row(R_LN1G), TG), ALU.mult))
            link(dve, c, nc.vector.tensor_tensor(Un, Un, spread(row(R_LN1B), TG), ALU.add))
            for j in range(TG):
                dve_evac(dve, c, lambda b: nc.vector.tensor_tensor(Un[:, j, :], Un[:, j, :], b[0:P, :], ALU.add))
            dve.wait_ge(R_sb, c.r)
            dve_ln(dve, c, Un)
            link(dve, c, nc.vector.tensor_tensor(Un, Un, spread(row(R_LN2G), TG), ALU.mult))
            link(dve, c, nc.vector.tensor_tensor(Un, Un, spread(row(R_LN2B), TG), ALU.add))
            link(dve, c, nc.vector.tensor_tensor(Un, Un, res, ALU.add))
            dve_ln(dve, c, Un)

        def pool_L2(pool, c):
            for g in range(EG):
                pool.wait_ge(L_y, c.y)
                for j in range(TG):
                    t = TG * g + j
                    gather(XS2[:, j, :], X2d, idd[:, 6, t:t + 1], x2_s[g])
                for j in range(TG):
                    t = TG * g + j
                    gather(XD2[:, j, :], X2d, idd[:, 5, t:t + 1], x2_d[g])
                c.r += 4 * TG
                c.y += 3 * TG
            c.r += 2 * EG + 1 + 1 + 1
            pool.wait_ge(R_sb, c.r)
            for g in range(EG):
                pool.wait_ge(L_y, c.y)
                for j in range(TG):
                    t = TG * g + j
                    gather(XD2[:, j, :], X2d, idd[:, 5, t:t + 1], x2_d2[g])
                c.r += 2 * TG
                c.y += 3 * TG
            pool.wait_ge(x3_put, 2 * 32 * EG)

        def pe_L2(pe, c):
            c.y = 4 * ET
            pe.wait_ge(w2_in, 16 * 4)
            for g in range(EG):
                pe.wait_ge(*x2_s[g].full(16 * TG))
                pe_transpose_rows(pe, c, XS2)
                pe.wait_ge(*x2_d[g].full(16 * TG))
                pe_transpose_rows(pe, c, XD2)
                pe.wait_ge(T_sb, c.t)
                for j in range(TG):
                    for fT, W in ((YT2, WQ), (XT2, WK), (XT2, WV)):
                        b = r_open(pe, c)
                        for k in range(KC):
                            i = nc.tensor.matmul(b[0:P, :], fT[:, k, j * P:(j + 1) * P], W[:, k, :],
                                                 start=k == 0, stop=k == KC - 1)
                        i.then_inc(R_ps, 1)
                c.y += TG
                pe.wait_ge(L_y, c.y)
                pe_ffn(pe, c, T2, TT2, F1T2)
                c.y += 2 * TG
            pe.wait_ge(e_rdy, 1)
            for src in (EE, EN):
                for g in range(EG):
                    b = r_open(pe, c)
                    for j in range(TG):
                        i = nc.tensor.transpose(b[0:H, j * P:(j + 1) * P], src[:, TG * g + j, :], ident[0:P, 0:P])
                    i.then_inc(R_ps, 1)
            pe.wait_ge(ft_rdy, 1)
            b = r_open(pe, c)
            for t in range(ET):
                i = nc.tensor.transpose(b[0:P, t * H:(t + 1) * H], FT[:, t * P:(t + 1) * P], ident[0:H, 0:H])
            i.then_inc(R_ps, 1)
            for done, src in ((f_rdy, FC), (ex_rdy, EX)):
                pe.wait_ge(done, 1)
                pe_boundaries(pe, c, Bd[:, :], lambda t: src[:, t, :], H)
                pe.wait_ge(B_sb, c.b)
                pe_segment_narrow(pe, c, Sd, Md, lambda t: src[:, t, :], BF2, H)
            pe.wait_ge(at_rdy, 1)
            pe_boundaries(pe, c, Bd[:, :], lambda t: V2[:, t, :], D)
            pe.wait_ge(B_sb, c.b)
            for g in range(EG):
                for k in range(KC):
                    b = t_open(pe, c)
                    pe_segment_T(pe, c, b, Sd, Md, V2, BF2, g, k, True).then_inc(T_ps, 1)
                pe.wait_ge(T_sb, c.t)
                pe_rows_out(pe, c, [(XT2, WO)])
                c.y += TG
                pe.wait_ge(L_y, c.y)
                pe_ffn(pe, c, T2, TT2, F1T2)
                c.y += 2 * TG

        def act_L2(act, c):
            c.r += EG + 1 + ET * ITERS
            for g in range(EG):
                act.wait_ge(R_ps, c.r)
                for fT in (XT2, YT2):
                    for k in range(KC):
                        act_evac(act, c, fT[:, k, :])
                act_root(act, c)
                c.r += 3 * TG
                act_ffn(act, c, TT2, F1T2)
            act.wait_ge(ex_in, 1)
            nc.scalar.activation(EX[:, :, :], EX[:, :, :], ACT.Exp).then_inc(ex_rdy, 1)
            c.r += 2 * EG + 3
            for g in range(EG):
                act.wait_ge(R_ps, c.r)
                for k in range(KC):
                    act_evac(act, c, XT2[:, k, :])
                c.r += TG
                act_root(act, c)
                act_ffn(act, c, TT2, F1T2)

        def dve_L2(dve, c):
            for g in range(EG):
                dve.wait_ge(*x2_s[g].full(16 * TG))
                for j in range(TG):
                    t = TG * g + j
                    dve_evac(dve, c, lambda b: nc.vector.tensor_copy(KQ2[:, j, :], b[0:P, :]))
                    dve.wait_ge(R_sb, c.r)
                    dve_evac(dve, c, lambda b: nc.vector.tensor_tensor(KQ2[:, j, :], KQ2[:, j, :], b[0:P, :],
                                                                       ALU.mult))
                    dve_evac(dve, c, lambda b: nc.vector.tensor_copy(V2[:, t, :], b[0:P, :]))
                dve.wait_ge(R_sb, c.r)
                for j in range(TG):
                    i = nc.vector.tensor_reduce(EE[:, TG * g + j, :],
                                                KQ2[:, j, :].rearrange("p (h d) -> p h d", h=H), AX.X, ALU.add)
                link(dve, c, i)
                link(dve, c, nc.vector.tensor_copy(T2, XS2))
                dve_ln(dve, c, T2)
                if g:
                    dve.wait_ge(x3_put, 32 * g)
                dve_ffn(dve, c, T2, U2, XS2)
            start = v20[:, 9, :]
            link(dve, c, nc.vector.tensor_scalar(start, RD[:, :, Q_DSC], float(FAR), NEG, ALU.is_lt, ALU.mult))
            nc.vector.tensor_copy(EN[:, :, :], b3(start, H)).then_inc(e_rdy, 1)
            for dst, f in ((eT, 0.125), (negT, 1.0)):
                assert DK == 64
                for g in range(EG):
                    dve_evac(dve, c, lambda b: nc.vector.tensor_scalar_mul(dst[:, g * GR:(g + 1) * GR],
                                                                           b[0:H, 0:GR], f))
            dve.wait_ge(R_sb, c.r)
            nc.vector.tensor_tensor_scan(FT, negT, eT, NEG, ALU.add, ALU.max).then_inc(ft_rdy, 1)
            last = v20[:, 10, :]
            link(dve, c, nc.vector.tensor_scalar_add(last, RD[:, :, Q_DUP], 1.0))
            link(dve, c, nc.vector.tensor_tensor(last, last, RD[:, :, Q_CNT], ALU.is_equal))
            dve_evac(dve, c, lambda b: nc.vector.tensor_tensor(
                FC[:, :, :], b[0:P, 0:ET * H].rearrange("p (t h) -> p t h", h=H), b3(last, H), ALU.mult))
            dve.wait_ge(R_sb, c.r)
            link(dve, c, nc.vector.memset(Bd[:, :], 0.0))
            dve_boundary_cols(dve, c, Bd, Sd, f_rdy)
            dve_b_evac(dve, c, BF2[:, 0:H], H)
            dve.wait_ge(R_ps, c.r + 1)
            bmax = bank[4 + c.r % 2][0:P, 0:ET * H].rearrange("p (t h) -> p t h", h=H)
            c.r += 1
            nc.vector.scalar_tensor_tensor(EX[:, :, :], EE[:, :, :], 0.125, bmax, ALU.mult,
                                           ALU.subtract).then_inc(R_sb, 1)
            dve.wait_ge(R_sb, c.r)
            nc.vector.memset(lst[:, :, :], 0.0).then_inc(ex_in, 1)
            dve_b_evac(dve, c, BF2[:, 0:H], H)
            dve_evac(dve, c, lambda b: nc.vector.reciprocal(
                FC[:, :, :], b[0:P, 0:ET * H].rearrange("p (t h) -> p t h", h=H)))
            dve.wait_ge(R_sb, c.r)
            link(dve, c, nc.vector.tensor_tensor(EX[:, :, :], EX[:, :, :], FC[:, :, :], ALU.mult))
            for t in range(ET):
                vt = V2[:, t, :].rearrange("p (h d) -> p h d", h=H)
                i = nc.vector.tensor_tensor(vt, vt, b3(EX[:, t, :], DK), ALU.mult)
            i.then_inc(at_rdy, 1)
            dve_b_evac(dve, c, BF2, D)
            dve.wait_ge(x3_put, 32 * EG)
            for g in range(EG):
                dve.wait_ge(*x2_d2[g].full(16 * TG))
                for j in range(TG):
                    dve_evac(dve, c, lambda b: nc.vector.tensor_tensor(T2[:, j, :], XD2[:, j, :], b[0:P, :],
                                                                       ALU.add))
                dve.wait_ge(R_sb, c.r)
                dve_ln(dve, c, T2)
                if g:
                    dve.wait_ge(x3_put, 32 * (EG + g))
                dve_ffn(dve, c, T2, U2, XD2)

        diag3 = at(0, [ET, P], P)
        V3 = at(0, [ET, D], P)
        BF3 = at(10240, [D], NB)
        XS3, XD3, SR3, WA3 = (at(10752 + G4 * k, [TG, D], P) for k in range(4))
        PST, PDT, XG3, ND3 = (at(18944 + 2000 * k, [KC, GR]) for k in range(4))
        XST, XDT = (at(26944 + 2000 * k, [KC, GR]) for k in range(2))
        O3 = at(30944, [TG, D], P)
        G1T = at(32992, [2, GR])
        GT3, N1T3, IPT = (at(33992 + GR * k, [GR]) for k in range(3))
        SQ3 = XG3[:, 1:4, :]
        EAT, SX, SA, FS, SS = (at(35492 + GR * k, [GR], 32) for k in range(5))
        x3_s, x3_d, x3_d2 = per_group("a", A_L1 + 64), per_group("b", 320), per_group("b", 384)
        n1_in, n1_rdy, xg_rdy, ip_rdy, sp_in3, sp_rdy, v3_rdy = (sem(k) for k in
            "n1_in n1_ready xg_ready ip_ready softplus_in softplus_ready v3_ready".split())
        out_put = sem("out_put")

        def pool_L3(pool, c):
            pool.wait_ge(rec_done, 3)
            for g in range(EG):
                if g:
                    pool.wait_ge(L_y, c.y)
                for k, (dst, s) in enumerate(((XS3, x3_s), (XD3, x3_d))):
                    for j in range(TG):
                        t = TG * g + j
                        gather(dst[:, j, :], X3d, idd[:, 1 - k, t:t + 1], s[g])
                for j in range(TG):
                    pool.wait_ge(L_y, c.y + j + 1)
                    scatter(out, idd[:, 2, TG * g + j:TG * g + j + 1], O3[:, j, :], out_put)
                c.y += TG
            pool.wait_ge(out_put, 16 * ET)
            for g in range(EG):
                pool.wait_ge(L_y, c.y)
                for j in range(TG):
                    t = TG * g + j
                    gather(XD3[:, j, :], X3d, idd[:, 0, t:t + 1], x3_d2[g])
                for j in range(TG):
                    pool.wait_ge(L_y, c.y + j + 1)
                    scatter(out, idd[:, 3, TG * g + j:TG * g + j + 1], O3[:, j, :], out_put)
                c.y += TG
            pool.wait_ge(out_put, 2 * 16 * ET)

        def pe_one(pe, c, rows, n, pairs):
            b = t_open(pe, c)
            for q, (W, fT) in enumerate(pairs):
                i = nc.tensor.matmul(b[0:rows, 0:n], W, fT, start=q == 0, stop=q == len(pairs) - 1)
            i.then_inc(T_ps, 1)

        def pe_gate(pe, c, fT, n):
            pe.wait_ge(n1_rdy, n)
            for m in range(2):
                pe_one(pe, c, 128, GR, [(wcol(W_G1 + 128 * m, 128), fT[:, 0, :]),
                                        (wcol(W_G1 + 256 + 128 * m, 128), N1T3)])
            pe.wait_ge(T_sb, c.t)
            for m in range(2):
                pe_one(pe, c, 128, GR, [(wcol(W_G2 + 128 * m, 128), G1T[:, 0, :]),
                                        (wcol(W_G2 + 256 + 128 * m, 128), G1T[:, 1, :])])
            pe.wait_ge(xg_rdy, n)

        def act_gate(act, c, fT, n):
            for k in range(KC):
                act_evac(act, c, fT[:, k, :])
            act.wait_ge(n1_in, n)
            nc.scalar.activation(N1T3, SQ3[:, 0, :], ACT.Sqrt, scale=1.0 / 3.0).then_inc(n1_rdy, 1)
            for m in range(2):
                act_evac(act, c, G1T[:, m, :], func=ACT.Silu, bias=colv[:, C_BG1 + m:C_BG1 + m + 1])
            for m, dst in enumerate((XG3[:, 0, :], GT3)):
                act_evac(act, c, dst, bias=colv[:, C_BG2 + m:C_BG2 + m + 1])

        def dve_gate(dve, c, fT, n, t0):
            dve.wait_ge(T_sb, t0)
            for k in range(3):
                i = nc.vector.tensor_tensor(SQ3[:, k, :], fT[:, k + 1, :], fT[:, k + 1, :], ALU.mult)
            link(dve, c, i)
            link(dve, c, nc.vector.tensor_tensor(SQ3[:, 0, :], SQ3[:, 0, :], SQ3[:, 1, :], ALU.add))
            nc.vector.tensor_tensor(SQ3[:, 0, :], SQ3[:, 0, :], SQ3[:, 2, :], ALU.add).then_inc(n1_in, 1)
            dve.wait_ge(T_sb, t0 + 4)
            for k in range(3):
                i = nc.vector.tensor_tensor(XG3[:, k + 1, :], fT[:, k + 1, :], GT3, ALU.mult)
            i.then_inc(xg_rdy, 1)

        def dve_last(dve, c, rows):
            for j in range(TG):
                dve.wait_ge(R_ps, c.r + 1)
                b = bank[4 + c.r % 2]
                c.r += 1
                nc.vector.scalar_tensor_tensor(vec3(O3[:, j, 128:D]), vec3(rows[:, j, 128:D]), 2.0,
                                               b[0:P, 128:D].rearrange("p (c u) -> p c u", c=3),
                                               ALU.mult, ALU.add)
                nc.vector.scalar_tensor_tensor(O3[:, j, 0:128], rows[:, j, 0:128], 2.0, b[0:P, 0:128],
                                               ALU.mult, ALU.add).then_inc(R_sb, 1)
            dve.wait_ge(R_sb, c.r)
            link(dve, c, nc.vector.tensor_tensor(O3[:, :, 0:128], O3[:, :, 0:128], spread(row(R_L3, 128), TG),
                                                 ALU.add))
            dve_ln(dve, c, O3)

        def pe_last(pe, c, fT):
            for j in range(TG):
                b = r_open(pe, c)
                for k in range(KC):
                    i = nc.tensor.matmul(b[0:P, k * 128:(k + 1) * 128], fT[:, k, j * P:(j + 1) * P],
                                         wcol(W_O1 if k else W_O0, 128), start=k == 0, stop=k == KC - 1)
                i.then_inc(R_ps, 1)

        def pe_L3(pe, c):
            pe_build(pe, c, diag3, 3)
            for g in range(EG):
                pe.wait_ge(*x3_s[g].full(16 * TG))
                pe_transpose_rows(pe, c, XS3, True)
                pe_gate(pe, c, XST, g + 1)
                for k in range(KC):
                    pe_one(pe, c, 128, GR, [(wcol(W_ND1 if k else W_ND0, 128), XG3[:, k, :])])
                for j in range(TG):
                    b = r_open(pe, c)
                    for k in range(KC):
                        i = nc.tensor.matmul(b[0:P, k * 128:(k + 1) * 128], XG3[:, k, j * P:(j + 1) * P],
                                             wcol(W_ND1 if k else W_ND0, 128), start=k == 0, stop=k == KC - 1)
                    i.then_inc(R_ps, 1)
                pe.wait_ge(*x3_d[g].full(16 * TG))
                pe_transpose_rows(pe, c, XD3, True)
                pe.wait_ge(T_sb, c.t)
                for k in range(KC):
                    pe_one(pe, c, 128, GR, [(wcol(W_PRE1 if k else W_PRE0, 128), XDT[:, k, :])])
                for k in range(1, KC):
                    pe_one(pe, c, 128, GR, [(wcol(W_PRE1, 128), XST[:, k, :])])
                b = t_open(pe, c)
                for j in range(TG):
                    i = nc.tensor.transpose(b[0:32, j * P:(j + 1) * P], RD[:, TG * g + j, Q_EA:Q_SSC],
                                            ident[0:P, 0:P])
                i.then_inc(T_ps, 1)
                pe.wait_ge(T_sb, c.t)
                pe_one(pe, c, 32, GR, [(w32s[:, V_F1:V_F1 + 32], EAT)])
                pe.wait_ge(ip_rdy, g + 1)
                pe_one(pe, c, 32, GR, [(wcol(W_S1, 32), PDT[:, 0, :]), (wcol(W_S1 + 32, 32), PDT[:, 0, :]),
                                       (wcol(W_S1 + 64, 32), IPT)])
                pe.wait_ge(sp_rdy, 2 * g + 2)
                for j in range(TG):
                    for src, w in ((FS, V_F2), (SS, V_S2)):
                        b = r_open(pe, c)
                        nc.tensor.matmul(b[0:P, :], src[:, j * P:(j + 1) * P], w32s[:, w:w + D], start=True,
                                         stop=True).then_inc(R_ps, 1)
                pe_last(pe, c, ND3)
            pe.wait_ge(v3_rdy, EG)
            pe_boundaries(pe, c, Bd[:, :], lambda t: V3[:, t, :], D)
            pe.wait_ge(B_sb, c.b)
            for g in range(EG):
                pe.wait_ge(*x3_d2[g].full(16 * TG))
                pe_transpose_rows(pe, c, XD3, True)
                pe_gate(pe, c, XDT, EG + g + 1)
                for k in range(KC):
                    b = t_open(pe, c)
                    nc.tensor.matmul(b[:, 0:GR], wcol(W_ND1 if k else W_ND0, 128), XG3[:, k, :], start=True,
                                     stop=False)
                    pe_segment_T(pe, c, b, Sd, Md, V3, BF3, g, k, False).then_inc(T_ps, 1)
                pe.wait_ge(T_sb, c.t)
                pe_last(pe, c, ND3)

        def act_nd(act, c):
            act_evac(act, c, ND3[:, 0, :], bias=colv[:, C_BND:C_BND + 1])
            for k in range(1, KC):
                act_evac(act, c, ND3[:, k, :])

        def act_softplus(act, c):
            act.wait_ge(T_ps, c.t + 1)
            c.t += 1
            b = bank[(c.t - 1) % 4][0:32, 0:GR]
            nc.scalar.activation(SX, b, ACT.Identity)
            nc.scalar.activation(SA, b, ACT.Abs).then_inc(T_sb, 1)
            act.wait_ge(T_sb, c.t)
            nc.scalar.activation(SA, SA, ACT.Exp, scale=-1.0).then_inc(astep, 1)
            c.a += 1
            act.wait_ge(astep, c.a)
            nc.scalar.activation(SA, SA, ACT.Ln, bias=1.0).then_inc(sp_in3, 1)

        def act_L3(act, c):
            c.r += EG
            for g in range(EG):
                act.wait_ge(R_ps, c.r)
                act_gate(act, c, XST, g + 1)
                act_nd(act, c)
                for k in range(KC):
                    act_evac(act, c, XDT[:, k, :])
                act_evac(act, c, PDT[:, 0, :], bias=colv[:, C_BPRE:C_BPRE + 1])
                for k in range(1, KC):
                    act_evac(act, c, PDT[:, k, :])
                for k in range(1, KC):
                    act_evac(act, c, PST[:, k, :], scale=1.0 / 3.0)
                act_evac(act, c, EAT, src_rows=32)
                if g:
                    act.wait_ge(sp_rdy, 2 * g)
                act_softplus(act, c)
                act.wait_ge(sp_rdy, 2 * g + 1)
                act_softplus(act, c)
                act_root(act, c)
                c.r += TG + 2 * TG + TG
            for g in range(EG):
                act.wait_ge(R_ps, c.r)
                act_gate(act, c, XDT, EG + g + 1)
                act_nd(act, c)
                act_root(act, c)
                c.r += TG

        def dve_L3(dve, c):
            t0 = EG * (8 + 12 + 4) + EG * (13 + 9)
            dve.wait_ge(rec_back, 16 * 7)
            for k, col in enumerate((Q_SI, Q_XD, Q_DSC, Q_SSC)):
                i = nc.vector.tensor_copy(idd[:, k, :], RD[:, :, col])
            i.then_inc(rec_done, 1)
            dve.wait_ge(rec_done, 3)
            dve_build(dve, c, 1, RD[:, :, Q_SRC], Sd, Md, diag3)
            link(dve, c, nc.vector.memset(Bd[:, :], 0.0))
            dve_boundary_cols(dve, c, Bd, Sd, bd_rdy)
            dve.wait_ge(bd_rdy, 1)
            for g in range(EG):
                dve_gate(dve, c, XST, g + 1, t0 + 4)
                for j in range(TG):
                    dve_evac(dve, c, lambda b: nc.vector.tensor_copy(SR3[:, j, :], b[0:P, :]))
                dve.wait_ge(R_sb, c.r)
                link(dve, c, nc.vector.tensor_tensor(
                    SR3[:, :, 0:128], SR3[:, :, 0:128], spread(rowv[:, R_L3, 128:256], TG), ALU.add))
                dve.wait_ge(T_sb, t0 + 23)
                for k in range(1, KC):
                    i = nc.vector.tensor_tensor(PST[:, k, :], PST[:, k, :], PDT[:, k, :], ALU.mult)
                link(dve, c, i)
                link(dve, c, nc.vector.tensor_tensor(PST[:, 1, :], PST[:, 1, :], PST[:, 2, :], ALU.add))
                nc.vector.tensor_tensor(IPT, PST[:, 1, :], PST[:, 3, :], ALU.add).then_inc(ip_rdy, 1)
                for k, dst in enumerate((FS, SS)):
                    dve.wait_ge(sp_in3, 2 * g + k + 1)
                    link(dve, c, nc.vector.scalar_tensor_tensor(dst, SX, 0.0, SA, ALU.max, ALU.add))
                    nc.vector.tensor_scalar_add(dst, dst, -LN2).then_inc(sp_rdy, 1)
                for j in range(TG):
                    dve_evac(dve, c, lambda b: nc.vector.tensor_copy(WA3[:, j, :], b[0:P, :]))
                    dve.wait_ge(R_sb, c.r)
                    dve_evac(dve, c, lambda b: nc.vector.tensor_tensor(WA3[:, j, :], WA3[:, j, :], b[0:P, :],
                                                                       ALU.mult))
                dve.wait_ge(R_sb, c.r)
                if g:
                    dve.wait_ge(out_put, 64 * g)
                for j in range(TG):
                    t = TG * g + j
                    w = [WA3[:, j, 128 * k:128 * (k + 1)] for k in range(4)]
                    sh = [RD[:, t, Q_SH + k:Q_SH + k + 1] for k in range(4)]
                    x0, x1 = SR3[:, j, 0:128], [SR3[:, j, 128 * k:128 * (k + 1)] for k in (1, 2, 3)]
                    o = [V3[:, t, 128 * k:128 * (k + 1)] for k in range(4)]
                    tmp = O3[:, 0, :]
                    S1, S2, S3 = tmp[:, 0:128], tmp[:, 128:256], O3[:, 1, 128:D]
                    link(dve, c, nc.vector.tensor_scalar(S1, x1[0], sh[1], None, ALU.mult))
                    link(dve, c, nc.vector.scalar_tensor_tensor(S1, x1[1], sh[2], S1, ALU.mult, ALU.add))
                    link(dve, c, nc.vector.scalar_tensor_tensor(S1, x1[2], sh[3], S1, ALU.mult, ALU.add))
                    nc.vector.scalar_tensor_tensor(S1, S1, 3.0 ** -0.5, w[3], ALU.mult, ALU.mult)
                    nc.vector.scalar_tensor_tensor(S2, x0, sh[0], w[0], ALU.mult, ALU.mult)
                    for k in range(3):
                        nc.vector.scalar_tensor_tensor(o[k + 1], x0, sh[k + 1], w[1], ALU.mult, ALU.mult)
                    link(dve, c, nc.vector.scalar_tensor_tensor(
                        S3.rearrange("p (c u) -> p c u", c=3), SR3[:, j, 128:D].rearrange("p (c u) -> p c u", c=3),
                        sh[0], spread(w[2], 3), ALU.mult, ALU.mult))
                    nc.vector.tensor_tensor(o[0], S1, S2, ALU.add)
                    link(dve, c, nc.vector.tensor_tensor(V3[:, t, 128:D], V3[:, t, 128:D], S3, ALU.add))
                nc.vector.memset(lst[:, :, :], 0.0).then_inc(v3_rdy, 1)
                dve_last(dve, c, XS3)
                t0 += 26
            c.t = t0
            dve_b_evac(dve, c, BF3, D)
            for g in range(EG):
                dve.wait_ge(out_put, 64 * (EG + g))
                dve_gate(dve, c, XDT, EG + g + 1, c.t + 4)
                c.t += 12
                dve_last(dve, c, XD3)

        def node_steps(eng, step):
            step(0, 0)
            step(1, 1)
            with eng.Fori(1, NG // 2) as i:
                step(i * 2, 0)
                step(i * 2 + 1, 1)
            step(NG, 0)
            step(NG + 1, 1)

        def has(g, lag):
            return not isinstance(g, int) or 0 <= g - lag < NG

        @block.sync
        def _(sp):
            for dst, src in ((ident, ident_in), (colv, cols), (ws, wsmall), (w32s, w32), (W1r, w_r1),
                             (W2r, w_r2)):
                sp.dma_start(dst[:], src).then_inc(s_w, 16)
            sp.dma_start(rowv[:, :, :], rows.partition_broadcast(P)).then_inc(s_w, 16)

            def step(g, par):
                if has(g, 0):
                    sp_in(sp, g, par)
                if has(g, 3):
                    sp_out(sp, g - 3)
            sp_in(sp, 0, 0)
            sp_in(sp, 1, 1)
            with sp.Fori(1, NG // 2) as i:
                sp_in(sp, i * 2, 0)
                if True:
                    sp_out(sp, i * 2 - 2)
                sp_in(sp, i * 2 + 1, 1)
                sp_out(sp, i * 2 - 1)
            sp_out(sp, NG - 2)
            sp_out(sp, NG - 1)
            c = Counts()
            sp_records(sp, c)
            c.ph, c.r = 1, EG
            sp_L0(sp, c)
            c.ph = 2
            sp.wait_ge(phase_end, 4 * c.ph)
            sp_L1(sp, c)
            c.ph = 3
            sp_L2(sp, c)
            c.ph = 4
            sp_L3(sp, c)

        @block.tensor
        def _(pe):
            pe.wait_ge(s_w, 16 * 7)

            def step(g, par):
                if has(g, 0):
                    if not (isinstance(g, int) and g < 3):
                        pe.wait_ge(C["o"], 4 * (g - 2))
                    pe_A(pe, g, par)
                if has(g, 1):
                    pe_B(pe, g - 1, 1 - par)
                if has(g, 2):
                    pe.wait_ge(A["z"], 4 * (g + 1) if not isinstance(g, int) else 4 * min(g + 1, NG))
                    pe_C(pe, g - 2, par)
            node_steps(pe, step)
            c = Counts()
            pe_build(pe, c, diag, 1)
            end_phase(pe, c)
            pe_L0(pe, c)
            end_phase(pe, c)
            pe_L1(pe, c)
            end_phase(pe, c)
            pe_L2(pe, c)
            end_phase(pe, c)
            pe_L3(pe, c)

        @block.scalar
        def _(act):
            act.wait_ge(s_w, 16 * 7)

            def step(g, par):
                if has(g, 0):
                    act_A1(act, g)
                if has(g, 1):
                    act_B1(act, g - 1)
                if has(g, 0):
                    act_A2(act, g, par)
                if has(g, 1):
                    act_B2(act, g - 1, 1 - par)
                if has(g, 2):
                    act_C1(act, g - 2)
                    act_C2(act, g - 2)
            node_steps(act, step)
            c = Counts()
            c.r = EG
            end_phase(act, c)
            act_L0(act, c)
            end_phase(act, c)
            act_L1(act, c)
            end_phase(act, c)
            act_L2(act, c)
            end_phase(act, c)
            act_L3(act, c)

        @block.vector
        def _(dve):
            dve.wait_ge(s_w, 16 * 7)

            def step(g, par):
                if has(g, 0):
                    dve_A(dve, g, par)
                if has(g, 1):
                    dve_B(dve, g - 1, 1 - par)
                if has(g, 2):
                    dve_C(dve, g - 2, par)
                    dve_C2(dve, g - 2, par)
            node_steps(dve, step)
            c = Counts()
            dve_records(dve, c)
            dve_build(dve, c, 0, RD[:, :, Q_DST], Sd, Md, diag)
            end_phase(dve, c)
            dve_L0(dve, c)
            end_phase(dve, c)
            dve_L1(dve, c)
            end_phase(dve, c)
            dve_L2(dve, c)
            end_phase(dve, c)
            dve_L3(dve, c)

        @block.gpsimd
        def _(pool):
            pool.wait_ge(s_w, 16 * 7)
            nc.gpsimd.tensor_tensor(row(R_LN1B), row(R_LN1B), row(R_L2B2), ALU.add).then_inc(s_w, 16)
            pool.wait_ge(s_w, 16 * 8)

            def step(g, par):
                if has(g, 0):
                    pool_A(pool, g, par)
                if has(g, 1):
                    pool_B1(pool, g - 1, 1 - par)
                    pool_B2(pool, g - 1, 1 - par)
            node_steps(pool, step)
            c = Counts()
            pool_records(pool, c)
            c.r = EG
            end_phase(pool, c)
            pool_L0(pool, c)
            end_phase(pool, c)
            pool_L1(pool, c)
            end_phase(pool, c)
            pool_L2(pool, c)
            end_phase(pool, c)
            pool_L3(pool, c)


def kernel(**inputs):
    import numpy as np
    import concourse.bacc as bacc
    from concourse.bass_utils import run_bass_kernel_spmd

    a = {k: np.asarray(v) for k, v in inputs.items()}
    f32 = np.float32

    def colsof(v):
        return v.reshape(-1, 128).T

    def chunks(w):
        return np.ascontiguousarray(w.reshape(w.shape[0] // 128, 128, -1).transpose(1, 0, 2))

    def flat(w):
        return chunks(w).reshape(128, -1)

    cols = np.zeros((128, C_END), f32)
    cols[:, C_L0B1:C_LN1G] = colsof(a["L0_gnn_b1"])
    cols[:, C_LN1G:C_LN1B] = colsof(a["L2_gnn_ln1_g"])
    cols[:, C_LN1B:C_L2B1] = colsof(a["L2_gnn_ln1_b"])
    cols[0:32, C_L2B1] = a["L2_gnn_b1"]
    cols[:, C_BG1:C_BG2] = colsof(a["L3_gnn_b_g1"])
    cols[:, C_BG2:C_BND] = colsof(a["L3_gnn_b_g2"])
    cols[:, C_BND] = a["L3_gnn_b_nd0"]
    cols[:, C_BPRE] = a["L3_gnn_b_pre0"]
    rows = np.zeros((R_END, D), f32)
    for r, k in ((R_L0B2, "L0_gnn_b2"), (R_LN1G, "L2_gnn_ln1_g"), (R_LN1B, "L2_gnn_ln1_b"),
                 (R_L2B2, "L2_gnn_b2"), (R_LN2G, "L2_gnn_ln2_g"), (R_LN2B, "L2_gnn_ln2_b")):
        rows[r] = a[k]
    rows[R_L3, 0:128] = a["L3_gnn_b_o0"]
    rows[R_L3, 128:256] = a["L3_gnn_b_nd0"]
    rows[R_L3, 256:384] = a["L3_gnn_b_pre0"]
    wsmall = np.concatenate([flat(a["L3_gnn_" + k]) for k in
                             ("W_g1", "W_g2", "W_nd0", "W_nd1", "W_o0", "W_o1", "W_pre0", "W_pre1", "W_s1")]
                            + [flat(a["L2_gnn_W1"])], axis=1)
    w32 = np.concatenate([a["L2_gnn_W2"], a["L3_gnn_W_f2"], a["L3_gnn_W_s2"], a["L3_gnn_W_f1"]], axis=1)
    rec = np.zeros((E, Q_END), f32)
    rec[:, Q_W] = a["edge_weight"]
    rec[:, Q_SH:Q_EA] = a["edge_attr_4"]
    rec[:, Q_EA:Q_SSC] = a["edge_attr_32"]
    t = np.arange(ET)
    mask = np.concatenate([t[:, None] > t[None, :], t[:, None] < t[None, :]]).astype(f32)
    arrays = {"x": a["x"], "cols": cols, "rows": rows, "wsmall": wsmall, "w32": w32,
              "ident_in": np.eye(128, dtype=f32),
              "w_r1": chunks(a["L0_gnn_W1_r"].T), "w_r2": chunks(a["L0_gnn_W2_r"].T),
              "w_l1": chunks(a["L0_gnn_W1_l"].T), "w_l2": chunks(a["L0_gnn_W2_l"].T),
              "w_q": chunks(a["L2_gnn_Wq"]), "w_k": chunks(a["L2_gnn_Wk"]),
              "w_v": chunks(a["L2_gnn_Wv"]), "w_o": chunks(a["L2_gnn_Wo"]),
              "keys": np.stack([a["dst"], a["src"]]),
              "key_cols": np.concatenate([a["dst"].reshape(ET, P).T, a["src"].reshape(ET, P).T], axis=1),
              "rec_in": rec, "tri_in": np.triu(np.ones((P, P), f32), 1).T.copy(), "mask_in": mask,
              "abs_in": np.concatenate([a["L1_gnn_alpha"], a["L1_gnn_beta"], a["L1_gnn_sigma"]])[None, :]}
    nc = bacc.Bacc("TRN2", target_bir_lowering=False, num_devices=1)
    args = [nc.dram_tensor(k, v.shape, mybir.dt.from_np(v.dtype), kind="ExternalInput").ap()
            for k, v in arrays.items()]
    out = nc.dram_tensor("out", (N, D), F32, kind="ExternalOutput").ap()
    gnn_kernel(nc, *args, out)
    r = run_bass_kernel_spmd(nc, [{k: np.ascontiguousarray(v) for k, v in arrays.items()}], core_ids=[0])
    return r.results[0]["out"]
```

```python
import concourse.bass as bass
from concourse import mybir
from contextlib import ExitStack

N, E, D = 10000, 2500, 512
P = 125
TG = 4
GR = P * TG
NG = N // GR
KC = D // 128
HI = 112
EPS = 1e-5
F32, I32 = mybir.dt.float32, mybir.dt.int32
ALU, ACT, AX = mybir.AluOpType, mybir.ActivationFunctionType, mybir.AxisListType

C_L0B1, C_LN1G, C_LN1B, C_L2B1, C_BG1, C_BG2, C_BND, C_BPRE, C_END = 0, 4, 8, 12, 13, 15, 17, 18, 19
R_L0B2, R_LN1G, R_LN2G, R_LN2B, R_L3, R_END = range(6)
W_G1, W_G2, W_ND0, W_ND1, W_O0, W_O1, W_PRE0, W_PRE1, W_S1, W_L2A, W_END = \
    0, 512, 1024, 1152, 1280, 1408, 1536, 1664, 1792, 1888, 2016
V_L2B, V_F2, V_S2, V_F1, V_END = 0, 512, 1024, 1536, 1568
ET = E // P
EG = ET // TG
NB = 2 * ET
H, DK = 8, D // 8
ITERS = 10
Q_DST, Q_SRC, Q_W, Q_DSC, Q_SH, Q_EA, Q_SSC, Q_CNT, Q_DUP, Q_SI, Q_DI, Q_RS, Q_YI, Q_XD, Q_END = \
    0, 1, 2, 3, 4, 8, 40, 41, 42, 43, 44, 45, 46, 47, 48
FAR = 1 << 20
NEG = -1e30
LN2 = 0.6931471805599453


def gnn_kernel(nc, x, cols, rows, wsmall, w32, ident_in, w_r1, w_r2, w_l1, w_l2, w_q, w_k, w_v, w_o,
               keys, key_cols, rec_in, earlier_in, mask_in, abs_in, out):
    ctx = ExitStack()
    with ctx:
        def sb(name, shape, dt=F32):
            return ctx.enter_context(nc.sbuf_tensor(name, shape, dt))

        def sem(name):
            return ctx.enter_context(nc.semaphore(name))

        bank = [ctx.enter_context(nc.psum_tensor(f"bank{i}", [128, 512], F32)) for i in range(8)]

        ident = sb("ident", [128, 128])
        colv = sb("colv", [128, C_END])
        rowv = sb("rowv", [P, R_END, D])
        ws = sb("ws", [128, W_END])
        w32s = sb("w32s", [34, V_END])
        AR = 38400
        arena = sb("arena", [128, AR])

        def at(off, shape, parts=128, dt=F32):
            n = 1
            for v in shape:
                n *= v
            assert off + n <= AR, (off, shape)
            ap = arena[0:parts, off:off + n]
            if dt != F32:
                ap = ap.bitcast(dt)
            if len(shape) == 2:
                ap = ap.rearrange("p (a b) -> p a b", b=shape[1])
            return ap

        G4 = TG * D
        W1r, W2r = at(0, [KC, D]), at(2048, [KC, D])
        X = [at(4096 + G4 * i, [TG, D], P) for i in range(2)]
        Z = at(8192, [TG, D], P)
        T = [at(10240 + G4 * i, [TG, D], P) for i in range(2)]
        U = at(14336, [TG, D], P)
        X3 = [at(16384 + G4 * i, [TG, D], P) for i in range(2)]
        O = at(20480, [TG, D], P)
        xT, hT, tT = at(22528, [KC, GR]), at(24528, [KC, GR]), at(26528, [KC, GR])
        x3T = at(28528, [KC, GR])
        xgT, ndT = at(30528, [KC, GR]), at(32528, [KC, GR])
        sq = xgT[:, 1:4, :]
        g1T = at(34528, [2, GR])
        f1T, n1T, gateT = at(35528, [GR], 34), at(36028, [GR]), at(36528, [GR])
        st = sb("st", [P, 4, TG, 6])
        n_even = sb("n_even", [P, 4, 1])
        mv = sb("mv", [P, 4, TG, 2])
        dd = sb("dd", [P, 2, TG])
        sr = sb("sr", [P, 4, 2, TG])
        rs = sb("rs", [P, 4, TG])
        nb = sb("nb", [P, 4, TG])
        q2 = [sb(f"q2_{i}", [P, TG]) for i in range(2)]

        s_w = sem("weights_in")
        A = {k: sem("A_" + k) for k in
             "x_in0 x_in1 xb z bn ag sc rt rc t".split()}
        B = {k: sem("B_" + k) for k in
             "tg z bn ag sc rt rc u ug ub z3 bn3 ag3 sc3 rt3 rc3 x3".split()}
        C = {k: sem("C_" + k) for k in
             "sq sqs n1 xg o bn ag sc rt rc y out".split()}

        def wcol(a, n):
            return ws[:, a:a + n]

        def row(r, n=D):
            return rowv[:, r, 0:n]

        def b3(ap, n):
            return ap.unsqueeze(2).broadcast_to([ap.shape[0], ap.shape[1], n])

        def spread(ap, n):
            return ap.unsqueeze(1).broadcast_to([ap.shape[0], n, ap.shape[1]])

        def vec3(ap):
            return ap.rearrange("p (u c) -> p c u", c=3)

        block = ctx.enter_context(nc.Block())

        def grows(dram, g):
            return dram[bass.ds(g * GR, GR), :].rearrange("(t p) d -> p t d", p=P)

        NT_ps, NT_sb, NR_ps, NR_sb = (sem(k) for k in "NT_ps NT_sb NR_ps NR_sb".split())
        TB, RB = [0, 1, 2, 3, 7], [4, 5, 6]
        PARTS = [("c_x", "C", "t", 4), ("a_x", "A", "t", 4), ("a_h1", "A", "t", 2), ("c_g1", "C", "t", 2),
                 ("a_h2", "A", "t", 2), ("b_t", "B", "t", 4), ("c_g2", "C", "t", 2), ("a_o1", "A", "r", 2),
                 ("b_f1", "B", "t", 1), ("c_nd", "C", "t", 4), ("a_o2", "A", "r", 2), ("b_f", "B", "r", 4),
                 ("c_o", "C", "r", 4)]
        LAG = {"A": 0, "B": 1, "L": 2, "C": 3, "S": 4}
        STEPS = NG + LAG["S"]
        FULL_T = sum(n for _, _, r, n in PARTS if r == "t")
        FULL_R = sum(n for _, _, r, n in PARTS if r == "r")
        assert FULL_T % len(TB) == 0 and FULL_R % len(RB) == 0

        def has(s, stage):
            return not isinstance(s, int) or 0 <= s - LAG[stage] < NG

        class Step:
            def __init__(self, s, k0):
                self.s, self.at = s, {}
                i0 = 0 if isinstance(s, int) else 1
                self.end = dict(k0)
                for part, stage, ring, n in PARTS:
                    self.at[part] = (self.end[ring], ring)
                    if has(s, stage):
                        self.end[ring] += n
                self.shift = {"t": 0, "r": 0}

            def count(self, part, i=0):
                k, ring = self.at[part]
                return self.shift[ring] + (k + i) if not isinstance(self.shift[ring], int) \
                    else self.shift[ring] + k + i

            def bank(self, part, i):
                k, ring = self.at[part]
                ring = TB if ring == "t" else RB
                return bank[ring[(k + i) % len(ring)]]

        def node_steps(eng, step):
            k = {"t": 0, "r": 0}
            for s in range(LAG["S"]):
                st_ = Step(s, k)
                step(st_, s, s % 2)
                k = st_.end
            lo, hi = LAG["S"] // 2, NG // 2
            with eng.Fori(lo, hi) as i:
                kk = k
                for par in range(2):
                    st_ = Step(i * 2 + par, kk)
                    st_.shift = {"t": i * (2 * FULL_T) - 2 * FULL_T * lo, "r": i * (2 * FULL_R) - 2 * FULL_R * lo}
                    step(st_, i * 2 + par, par)
                    kk = st_.end
            n = hi - lo
            k = {"t": k["t"] + 2 * FULL_T * n, "r": k["r"] + 2 * FULL_R * n}
            for s in range(NG, STEPS):
                st_ = Step(s, k)
                step(st_, s, s % 2)
                k = st_.end

        def later(n, least=1):
            return not isinstance(n, int) or n >= least

        def sp_in(sp, n, par):
            if later(n, 2):
                sp.wait_ge(A["t"], 4 * n - 4)
            src = grows(x, n)
            sp.dma_start(X[par][0:HI], src[0:HI]).then_inc(A[f"x_in{par}"], 16)
            sp.dma_start(X[par][HI:P], src[HI:P]).then_inc(A[f"x_in{par}"], 16)

        def sp_out(sp, n):
            sp.wait_ge(C["y"], 4 * n + 4)
            dst = grows(out, n)
            sp.dma_start(dst[0:HI], O[0:HI]).then_inc(C["out"], 16)
            sp.dma_start(dst[HI:P], O[HI:P]).then_inc(C["out"], 16)

        def pe_step(pe, st_, s, par):
            nC = s - LAG["C"]
            hA, hB, hC = has(s, "A"), has(s, "B"), has(s, "C")

            def t_bank(part, i):
                u = st_.count(part, i)
                if not isinstance(u, int) or u >= len(TB):
                    pe.wait_ge(NT_sb, u - (len(TB) - 1))
                return st_.bank(part, i)

            def r_bank(part, i):
                u = st_.count(part, i)
                if not isinstance(u, int) or u >= len(RB):
                    pe.wait_ge(NR_sb, u - (len(RB) - 1))
                return st_.bank(part, i)

            def rows_T(part, rows4, interleaved=False):
                for k in range(KC):
                    b = t_bank(part, k)
                    for j in range(TG):
                        src = vec3(rows4[:, j, 128:D])[:, k - 1, :] if interleaved and k \
                            else rows4[:, j, k * 128:(k + 1) * 128]
                        i = nc.tensor.transpose(b[:, j * P:(j + 1) * P], src, ident[0:P, 0:P])
                    i.then_inc(NT_ps, 1)

            def hidden(part, m0):
                for q in range(2):
                    m = m0 + q
                    b = t_bank(part, q)
                    for k in range(KC):
                        i = nc.tensor.matmul(b[:, 0:GR], W1r[:, k, m * 128:(m + 1) * 128], xT[:, k, :],
                                             start=k == 0, stop=k == KC - 1)
                    i.then_inc(NT_ps, 1)

            def gate(part, w, f0, f1):
                for m in range(2):
                    b = t_bank(part, m)
                    nc.tensor.matmul(b[:, 0:GR], wcol(w + 128 * m, 128), f0, start=True, stop=False)
                    nc.tensor.matmul(b[:, 0:GR], wcol(w + 256 + 128 * m, 128), f1, start=False,
                                     stop=True).then_inc(NT_ps, 1)

            def out_rows(part, j0):
                for q in range(2):
                    j = j0 + q
                    b = r_bank(part, q)
                    for k in range(KC):
                        i = nc.tensor.matmul(b[0:P, :], hT[:, k, j * P:(j + 1) * P], W2r[:, k, :],
                                             start=k == 0, stop=k == KC - 1)
                    i.then_inc(NR_ps, 1)

            if hC:
                pe.wait_ge(B["x3"], 4 * nC + 4)
                rows_T("c_x", X3[1 - par], True)
            if hA:
                pe.wait_ge(A[f"x_in{par}"], 16 * s + (32 - 16 * par))
                rows_T("a_x", X[par])
                pe.wait_ge(NT_sb, st_.count("a_x", 4))
                hidden("a_h1", 0)
            if hC:
                pe.wait_ge(C["n1"], nC + 1)
                gate("c_g1", W_G1, x3T[:, 0, :], n1T[:, :])
            if hA:
                hidden("a_h2", 2)
            if hB:
                pe.wait_ge(A["t"], 4 * s)
                rows_T("b_t", T[1 - par])
            if hC:
                pe.wait_ge(NT_sb, st_.count("c_g1", 2))
                gate("c_g2", W_G2, g1T[:, 0, :], g1T[:, 1, :])
            if hA:
                pe.wait_ge(NT_sb, st_.count("a_h2", 2))
                out_rows("a_o1", 0)
            if hB:
                pe.wait_ge(NT_sb, st_.count("b_t", 4))
                b = t_bank("b_f1", 0)
                for k in range(KC):
                    i = nc.tensor.matmul(b[0:32, 0:GR], wcol(W_L2A + 32 * k, 32), tT[:, k, :],
                                         start=k == 0, stop=k == KC - 1)
                i.then_inc(NT_ps, 1)
            if hC:
                pe.wait_ge(NT_sb, st_.count("c_g2", 2))
                for k in range(KC):
                    if k >= 1:
                        pe.wait_ge(C["xg"], 3 * nC + k)
                    nc.tensor.matmul(t_bank("c_nd", k)[:, 0:GR], wcol(W_ND1 if k else W_ND0, 128), xgT[:, k, :],
                                     start=True, stop=True).then_inc(NT_ps, 1)
            if hA:
                out_rows("a_o2", 2)
            if hB:
                pe.wait_ge(NT_sb, st_.count("b_f1", 1))
                for j in range(TG):
                    nc.tensor.matmul(r_bank("b_f", j)[0:P, :], f1T[:, j * P:(j + 1) * P],
                                     w32s[:, V_L2B:V_L2B + D], start=True, stop=True).then_inc(NR_ps, 1)
            if hC:
                pe.wait_ge(NT_sb, st_.count("c_nd", 4))
                for j in range(TG):
                    b = r_bank("c_o", j)
                    for k in range(KC):
                        i = nc.tensor.matmul(b[0:P, k * 128:(k + 1) * 128], ndT[:, k, j * P:(j + 1) * P],
                                             wcol(W_O1 if k else W_O0, 128), start=k == 0, stop=k == KC - 1)
                    i.then_inc(NR_ps, 1)

        def act_step(act, st_, s, par):
            nB, nL, nC, nS = (s - LAG[k] for k in "BLCS")

            def evac(part, i, dst, parts=128, func=ACT.Identity, **kw):
                act.wait_ge(NT_ps, st_.count(part, i + 1))
                nc.scalar.activation(dst, st_.bank(part, i)[0:parts, 0:GR], func, **kw).then_inc(NT_sb, 1)

            def col(c):
                return colv[:, c:c + 1]

            def hidden(part, m0):
                for q in range(2):
                    evac(part, q, hT[:, m0 + q, :], func=ACT.Relu, bias=col(C_L0B1 + m0 + q))

            def sign_pass(q):
                if has(s, "A"):
                    mine, theirs = ((0, 0), (1, 0), (0, 1))[q]
                    if later(s, 1) or q:
                        act.wait_ge(signs, 3 * s + q)
                    nc.scalar.activation(junk_s, keys_f[theirs], ACT.Sign, bias=key_of(neg_key, mine, s),
                                         accum_out=key_of(sgn, q, s)).then_inc(signs, 1)

            if has(s, "C"):
                if later(nC):
                    act.wait_ge(C["xg"], 3 * nC)
                for k in range(KC):
                    evac("c_x", k, x3T[:, k, :])
            if has(s, "A"):
                for k in range(KC):
                    evac("a_x", k, xT[:, k, :])
            if has(s, "L"):
                act.wait_ge(B["sc"], nL + 1)
                nc.scalar.activation(sr[:, 1, 0, :], sr[:, 1, 0, :], ACT.Sqrt).then_inc(B["rt"], 1)
            if has(s, "B"):
                act.wait_ge(A["rc"], 3 * s)
                if later(s, 3):
                    act.wait_ge(B["z3"], 4 * s - 8)
                for j in range(TG):
                    nc.scalar.activation(T[1 - par][:, j, :], Z[:, j, :], ACT.Identity, scale=rs[:, 0, j:j + 1],
                                         bias=nb[:, 0, j:j + 1]).then_inc(A["t"], 1)
            if has(s, "C"):
                act.wait_ge(C["sqs"], 2 * nC + 2)
                nc.scalar.activation(n1T[:, :], sq[:, 0, :], ACT.Sqrt, scale=1.0 / 3.0).then_inc(C["n1"], 1)
            if has(s, "A"):
                if later(s):
                    act.wait_ge(A["z"], 4 * s)
                hidden("a_h1", 0)
            if has(s, "C"):
                for m in range(2):
                    evac("c_g1", m, g1T[:, m, :], func=ACT.Silu, bias=col(C_BG1 + m))
            if has(s, "L"):
                act.wait_ge(B["rc"], 2 * nL + 2)
                for j in range(TG):
                    nc.scalar.activation(U[:, j, :], U[:, j, :], ACT.Identity, scale=rs[:, 1, j:j + 1],
                                         bias=nb[:, 1, j:j + 1]).then_inc(B["u"], 1)
            if has(s, "A"):
                hidden("a_h2", 2)
            sign_pass(0)
            if has(s, "B"):
                for k in range(KC):
                    evac("b_t", k, tT[:, k, :], scale=col(C_LN1G + k), bias=col(C_LN1B + k))
            if has(s, "C"):
                for m, dst in enumerate((xgT[:, 0, :], gateT[:, :])):
                    evac("c_g2", m, dst, bias=col(C_BG2 + m))
            if has(s, "L"):
                act.wait_ge(B["sc3"], nL + 1)
                nc.scalar.activation(sr[:, 2, 0, :], sr[:, 2, 0, :], ACT.Sqrt).then_inc(B["rt3"], 1)
                act.wait_ge(B["rc3"], 2 * nL + 2)
                if later(nL, 2):
                    act.wait_ge(C["o"], 4 * nL - 4)
                for j in range(TG):
                    nc.scalar.activation(X3[par][:, j, :], U[:, j, :], ACT.Identity, scale=rs[:, 2, j:j + 1],
                                         bias=nb[:, 2, j:j + 1]).then_inc(B["x3"], 1)
            if has(s, "B"):
                if later(s, 2):
                    act.wait_ge(B["z"], 4 * s - 4)
                evac("b_f1", 0, f1T[0:32, :], parts=32, func=ACT.Relu, bias=colv[0:32, C_L2B1:C_L2B1 + 1])
            if has(s, "S"):
                act.wait_ge(C["sc"], nS + 1)
                nc.scalar.activation(sr[:, 3, 0, :], sr[:, 3, 0, :], ACT.Sqrt).then_inc(C["rt"], 1)
                act.wait_ge(C["rc"], 2 * nS + 2)
                for j in range(TG):
                    nc.scalar.activation(O[:, j, :], O[:, j, :], ACT.Identity, scale=rs[:, 3, j:j + 1],
                                         bias=nb[:, 3, j:j + 1]).then_inc(C["y"], 1)
            if has(s, "C"):
                if later(nC):
                    act.wait_ge(C["o"], 4 * nC)
                for k in range(KC):
                    if k:
                        evac("c_nd", k, ndT[:, k, :])
                    else:
                        evac("c_nd", k, ndT[:, k, :], bias=col(C_BND))
            if has(s, "A"):
                act.wait_ge(A["sc"], 4 * s + 4)
                nc.scalar.activation(sr[:, 0, :, :], sr[:, 0, :, :], ACT.Sqrt).then_inc(A["rt"], 1)
            sign_pass(1)
            sign_pass(2)

        def dve_stats(dve, S, bn, ag, z, n, q, src):
            for j in range(TG):
                dve.wait_ge(S[z], 4 * n + j + 1)
                nc.vector.bn_stats(st[:, q, j, :], src[:, j, :]).then_inc(S[bn], 1)
            dve.wait_ge(S[bn], 4 * n + 4)
            nc.vector.tensor_copy(n_even[:, q, :], st[:, q, 0, 0:1]).then_inc(S[ag], 1)
            for j in range(TG):
                nc.vector.bn_aggr(mv[:, q, j, :], st[:, q, j, :]).then_inc(S[ag], 1)
            dve.wait_ge(S[ag], 5 * n + 5)

        def dve_norm(dve, S, sc, rt, rc, n, q):
            nc.vector.tensor_scalar_add(sr[:, q, 0, :], mv[:, q, :, 1], EPS).then_inc(S[sc], 1)
            dve.wait_ge(S[rt], n + 1)
            nc.vector.reciprocal(rs[:, q, :], sr[:, q, 0, :]).then_inc(S[rc], 1)
            dve.wait_ge(S[rc], 2 * n + 1)
            nc.vector.scalar_tensor_tensor(nb[:, q, :], mv[:, q, :, 0], -1.0, rs[:, q, :], ALU.mult,
                                           ALU.mult).then_inc(S[rc], 1)

        def dve_step(dve, st_, s, par):
            nB, nL, nC, nS = (s - LAG[k] for k in "BLCS")

            def count_pass(q):
                if has(s, "A"):
                    dve.wait_ge(counts, 6 * s + q + 1)
                    mine, kind = divmod(q, 3)
                    me, acc = key_of(own_key, mine, s), key_of(cnt3, q, s)
                    if kind == 1:
                        nc.vector.scalar_tensor_tensor(
                            junk_v, keys_f[mine], me, earlier[:, bass.ds(E - s * P, E)], ALU.is_equal, ALU.mult,
                            accum_out=acc).then_inc(counts, 1)
                    else:
                        nc.vector.tensor_scalar(junk_v, keys_f[mine if kind == 0 else 1 - mine], me, None,
                                                ALU.is_lt, ALU.add, accum_out=acc).then_inc(counts, 1)

            def finish(S, sc, rt, rc, n, q):
                dve.wait_ge(S[rt], n + 1)
                nc.vector.reciprocal(rs[:, q, :], sr[:, q, 0, :]).then_inc(S[rc], 1)
                dve.wait_ge(S[rc], 2 * n + 1)
                nc.vector.scalar_tensor_tensor(nb[:, q, :], mv[:, q, :, 0], -1.0, rs[:, q, :], ALU.mult,
                                               ALU.mult).then_inc(S[rc], 1)

            if has(s, "C"):
                for k in range(3):
                    dve.wait_ge(NT_sb, st_.count("c_x", k + 2))
                    nc.vector.tensor_tensor(sq[:, k, :], x3T[:, k + 1, :], x3T[:, k + 1, :],
                                            ALU.mult).then_inc(C["sq"], 1)
            if has(s, "L"):
                finish(B, "sc", "rt", "rc", nL, 1)
            if has(s, "C"):
                for k in range(2):
                    dve.wait_ge(C["sq"], 3 * nC + 2 + k)
                    if k:
                        dve.wait_ge(C["sqs"], 2 * nC + 1)
                    nc.vector.tensor_tensor(sq[:, 0, :], sq[:, 0, :], sq[:, k + 1, :],
                                            ALU.add).then_inc(C["sqs"], 1)
            count_pass(0)
            count_pass(1)
            if has(s, "L"):
                for j in range(TG):
                    dve.wait_ge(B["ub"], 4 * nL + j + 1)
                    nc.vector.scalar_tensor_tensor(U[:, j, :], T[par][:, j, :], q2[par][:, j:j + 1], U[:, j, :],
                                                   ALU.mult, ALU.add).then_inc(B["z3"], 1)
                if later(nL):
                    dve.wait_ge(B["x3"], 4 * nL)
                dve_stats(dve, B, "bn3", "ag3", "z3", nL, 2, U)
                nc.vector.tensor_scalar_add(sr[:, 2, 0, :], mv[:, 2, :, 1], EPS).then_inc(B["sc3"], 1)
            count_pass(2)
            if has(s, "C"):
                dve.wait_ge(NT_sb, st_.count("c_g2", 2))
                for k in range(3):
                    nc.vector.tensor_tensor(xgT[:, k + 1, :], x3T[:, k + 1, :], gateT[:, :],
                                            ALU.mult).then_inc(C["xg"], 1)
            if has(s, "L"):
                finish(B, "sc3", "rt3", "rc3", nL, 2)
            count_pass(3)
            count_pass(4)

            def z_tiles(part, j0):
                for q in range(2):
                    j = j0 + q
                    dve.wait_ge(A["xb"], 4 * s + j + 1)
                    dve.wait_ge(NR_ps, st_.count(part, q + 1))
                    nc.vector.tensor_tensor(Z[:, j, :], Z[:, j, :], st_.bank(part, q)[0:P, :],
                                            ALU.add).then_inc(NR_sb, 1)
                for q in range(2):
                    dve.wait_ge(NR_sb, st_.count(part, q + 1))
                    nc.vector.bn_stats(st[:, 0, j0 + q, :], Z[:, j0 + q, :]).then_inc(A["bn"], 1)
            if has(s, "A"):
                z_tiles("a_o1", 0)
            if has(s, "S"):
                finish(C, "sc", "rt", "rc", nS, 3)
            count_pass(5)
            if has(s, "A"):
                z_tiles("a_o2", 2)
                if later(s):
                    dve.wait_ge(A["t"], 4 * s)
                dve.wait_ge(A["bn"], 4 * s + 4)
                nc.vector.tensor_copy(n_even[:, 0, :], st[:, 0, 0, 0:1]).then_inc(A["z"], 4)
                for j in range(TG):
                    i = nc.vector.bn_aggr(mv[:, 0, j, :], st[:, 0, j, :])
                i.then_inc(A["ag"], 1)
                dve.wait_ge(A["ag"], s + 1)
                var = mv[:, 0, :, 1]
                nc.vector.tensor_scalar(dd[:, 0, :], var, 4.0 + EPS, EPS * EPS, ALU.mult,
                                        ALU.add).then_inc(A["sc"], 1)
                dve.wait_ge(A["sc"], 4 * s + 1)
                nc.vector.scalar_tensor_tensor(sr[:, 0, 0, :], dd[:, 0, :], EPS / 4, var, ALU.mult,
                                               ALU.add).then_inc(A["sc"], 1)
                nc.vector.reciprocal(dd[:, 1, :], dd[:, 0, :]).then_inc(A["sc"], 1)
                dve.wait_ge(A["sc"], 4 * s + 3)
                nc.vector.scalar_tensor_tensor(sr[:, 0, 1, :], dd[:, 1, :], 4.0, sr[:, 0, 0, :], ALU.mult,
                                               ALU.mult).then_inc(A["sc"], 1)

            def last_stats(S, ring_part, n, q, src):
                for j in range(TG):
                    nc.vector.bn_stats(st[:, q, j, :], src[:, j, :]).then_inc(S["bn"], 1)
                dve.wait_ge(S["bn"], 4 * n + 4)
                i = nc.vector.tensor_copy(n_even[:, q, :], st[:, q, 0, 0:1])
                if S is B:
                    i.then_inc(B["z"], 4)
                for j in range(TG):
                    i = nc.vector.bn_aggr(mv[:, q, j, :], st[:, q, j, :])
                i.then_inc(S["ag"], 1)
                dve.wait_ge(S["ag"], n + 1)
                nc.vector.tensor_scalar_add(sr[:, q, 0, :], mv[:, q, :, 1], EPS).then_inc(S["sc"], 1)

            if has(s, "B"):
                for j in range(TG):
                    dve.wait_ge(B["tg"], 4 * nB + j + 1)
                    dve.wait_ge(NR_ps, st_.count("b_f", j + 1))
                    nc.vector.tensor_tensor(U[:, j, :], U[:, j, :], st_.bank("b_f", j)[0:P, :],
                                            ALU.add).then_inc(NR_sb, 1)
                if later(nB):
                    dve.wait_ge(B["u"], 4 * nB)
                dve.wait_ge(NR_sb, st_.count("b_f", 4))
                last_stats(B, "b_f", nB, 1, U)
            if has(s, "A"):
                dve.wait_ge(A["rt"], s + 1)
                nc.vector.reciprocal(rs[:, 0, :], sr[:, 0, 0, :]).then_inc(A["rc"], 1)
                nc.vector.tensor_copy(q2[par][:, :], sr[:, 0, 1, :]).then_inc(A["rc"], 1)
                dve.wait_ge(A["rc"], 3 * s + 1)
                nc.vector.scalar_tensor_tensor(nb[:, 0, :], mv[:, 0, :, 0], -1.0, rs[:, 0, :], ALU.mult,
                                               ALU.mult).then_inc(A["rc"], 1)
            if has(s, "C"):
                if later(nC):
                    dve.wait_ge(C["out"], 32 * nC)
                rows = X3[1 - par]
                for j in range(TG):
                    dve.wait_ge(NR_ps, st_.count("c_o", j + 1))
                    b = st_.bank("c_o", j)
                    nc.vector.scalar_tensor_tensor(vec3(O[:, j, 128:D]), vec3(rows[:, j, 128:D]), 2.0,
                                                   b[0:P, 128:D].rearrange("p (c u) -> p c u", c=3),
                                                   ALU.mult, ALU.add)
                    nc.vector.scalar_tensor_tensor(O[:, j, 0:128], rows[:, j, 0:128], 2.0, b[0:P, 0:128],
                                                   ALU.mult, ALU.add).then_inc(NR_sb, 1)
                dve.wait_ge(NR_sb, st_.count("c_o", 4))
                nc.vector.tensor_tensor(O[:, :, 0:128], O[:, :, 0:128], spread(row(R_L3, 128), TG),
                                        ALU.add).then_inc(C["o"], 4)
            if has(s, "C"):
                dve.wait_ge(C["o"], 4 * nC + 4)
                last_stats(C, "c_o", nC, 3, O)

        def pool_step(pool, st_, s, par):
            nB, nL = s - LAG["B"], s - LAG["L"]
            if has(s, "A"):
                pool.wait_ge(A[f"x_in{par}"], 16 * s + (32 - 16 * par))
                if later(s):
                    pool.wait_ge(A["t"], 4 * s)
                for j in range(TG):
                    nc.gpsimd.tensor_tensor(Z[:, j, :], X[par][:, j, :], row(R_L0B2), ALU.add).then_inc(A["xb"], 1)
            if has(s, "L"):
                for j in range(TG):
                    pool.wait_ge(B["u"], 4 * nL + j + 1)
                    nc.gpsimd.tensor_tensor(U[:, j, :], U[:, j, :], row(R_LN2G), ALU.mult).then_inc(B["ug"], 1)
                for j in range(TG):
                    pool.wait_ge(B["ug"], 4 * nL + j + 1)
                    nc.gpsimd.tensor_tensor(U[:, j, :], U[:, j, :], row(R_LN2B), ALU.add).then_inc(B["ub"], 1)
            if has(s, "B"):
                if later(nB):
                    pool.wait_ge(B["x3"], 4 * nB)
                for j in range(TG):
                    pool.wait_ge(A["t"], 4 * nB + j + 1)
                    nc.gpsimd.tensor_tensor(U[:, j, :], T[1 - par][:, j, :], row(R_LN1G),
                                            ALU.mult).then_inc(B["tg"], 1)

        Sd, Ml, Bd, RD = sb("Sd", [P, ET, P]), sb("Md", [P, ET, P]), sb("Bd", [P, NB * ET]), \
            sb("RD", [P, ET, Q_END])
        Md = Ml[0:NB, :, :]
        keys_f = [m[:, :, :].rearrange("p t f -> p (t f)") for m in (Sd, Ml)]
        junk_v = Bd[:, :].bitcast(mybir.dt.uint8)[:, 0:E]
        junk_s = RD[:, :, :].rearrange("p t q -> p (t q)").bitcast(mybir.dt.int8)[:, 0:E]
        neg_rdy, keys_in = sem("own_keys"), sem("keys_in")

        counts, signs = sem("counts"), sem("signs")
        kfc, neg_key = sb("kfc", [P, 2 * ET]), sb("neg_key", [P, 2 * ET])
        cnt3, sgn = sb("cnt3", [P, 6 * ET]), sb("sgn", [P, 3 * ET])
        own_key = kfc
        earlier = at(37028, [1250], P).bitcast(mybir.dt.uint8)

        def key_of(t_, q, s):
            if isinstance(s, int):
                return t_[:, q * ET + s:q * ET + s + 1]
            return t_[:, bass.ds(s + q * ET, 1)]

        T_ps, T_sb, R_ps, R_sb, B_ps, B_sb = (sem(k) for k in "T_ps T_sb R_ps R_sb B_ps B_sb".split())
        dstep, astep = sem("vector_step"), sem("scalar_step")
        L_sc, L_rt, L_y = sem("norm_variance"), sem("norm_root"), sem("norm_rows")
        phase_end = sem("phase_end")
        rec_done, rec_put, rec_back = (sem(k) for k in "rec_done rec_put rec_back".split())

        rows_in = {q: [sem(f"rows_in_{q}{g}") for g in range(EG)] for q in ("gather_a", "gather_b", "load")}

        class Arrival:
            def __init__(self, s, base):
                self.s, self.base = s, base

            def full(self, n):
                return self.s, n + self.base

        def per_group(q, base):
            return [Arrival(s, base) for s in rows_in[{"a": "gather_a", "b": "gather_b", "h": "load"}[q]]]

        Hd, X1d, X2d, X3d = (nc.dram_tensor(f"{n}_table", (2 * E, D), F32).ap() for n in ("h", "x1", "x2", "x3"))
        Yd = nc.dram_tensor("y_table", (E, D), F32).ap()
        PDd = nc.dram_tensor("part_rows", (E, D), F32).ap()
        RDd = nc.dram_tensor("records_by_dst", (E, Q_END), F32).ap()
        RSd = nc.dram_tensor("records_by_src", (E, Q_END), F32).ap()

        class Counts:
            def __init__(self):
                self.t = self.r = self.b = self.ln = self.y = self.d = self.a = self.ph = 0

        def end_phase(eng, c):
            eng.drain().then_inc(phase_end, 1)
            c.ph += 1
            eng.wait_ge(phase_end, 4 * c.ph)

        def gcols(ap2, g):
            return ap2[:, g * TG:(g + 1) * TG]

        rec = at(0, [ET, Q_END], P)
        cnts = at(17100, [2 * 6 * ET], P).rearrange("p (q a t) -> p q a t", q=2, a=6)
        rank_i = at(17400, [2, ET], P, I32)
        own = at(17500, [6, ET], P)
        RSs = sb("RSs", [P, ET, 3])
        bk = sb("bk", [NB, 2])
        bkm = sb("bkm", [NB, 2, ET])
        mask = sb("mask", [NB, ET])
        idd = sb("idd", [P, 7, ET], I32)
        ids = sb("ids", [P, 3, ET], I32)
        abv = sb("abv", [P, 3])
        v20 = sb("v20", [P, 12, ET])
        lst = sb("lst", [P, TG, 6])
        lmv = sb("lmv", [P, TG, 2])
        lsr = sb("lsr", [P, TG])
        lrs = sb("lrs", [P, TG])
        s_end = sem("edge_constants")

        def t_open(pe, c):
            if c.t >= 4:
                pe.wait_ge(T_sb, c.t - 3)
            c.t += 1
            return bank[(c.t - 1) % 4]

        def r_open(pe, c):
            if c.r >= 2:
                pe.wait_ge(R_sb, c.r - 1)
            c.r += 1
            return bank[4 + (c.r - 1) % 2]

        def b_open(pe, c):
            if c.b:
                pe.wait_ge(B_sb, c.b)
            c.b += 1
            return bank[7]

        def pe_transpose_rows(pe, c, rows4, interleaved=False):
            for k in range(KC):
                b = t_open(pe, c)
                for j in range(TG):
                    if interleaved and k:
                        src = vec3(rows4[:, j, 128:D])[:, k - 1, :]
                    else:
                        src = rows4[:, j, k * 128:(k + 1) * 128]
                    i = nc.tensor.transpose(b[:, j * P:(j + 1) * P], src, ident[0:P, 0:P])
                i.then_inc(T_ps, 1)

        def pe_transpose_back(pe, c, fT):
            for j in range(TG):
                b = r_open(pe, c)
                for k in range(KC):
                    i = nc.tensor.transpose(b[0:P, k * 128:(k + 1) * 128], fT[:, k, j * P:(j + 1) * P],
                                            ident[:, :])
                i.then_inc(R_ps, 1)

        def pe_boundaries(pe, c, B, V, n, ready=None):
            b = b_open(pe, c)
            for t in range(ET):
                if ready is not None and t % TG == 0:
                    pe.wait_ge(*ready(t // TG))
                i = nc.tensor.matmul(b[0:NB, 0:n], B[:, t * NB:(t + 1) * NB], V(t), start=t == 0,
                                     stop=t == ET - 1)
            i.then_inc(B_ps, 1)

        def pe_segment_T(pe, c, b, S, M, V, bf, g, k, fresh):
            for j in range(TG):
                t = TG * g + j
                nc.tensor.matmul(b[:, j * P:(j + 1) * P], V[:, t, k * 128:(k + 1) * 128], S[:, t, :],
                                 start=fresh and j == 0, stop=False)
                i = nc.tensor.matmul(b[:, j * P:(j + 1) * P], bf[0:NB, k * 128:(k + 1) * 128], M[:, t, :],
                                     start=False, stop=j == TG - 1)
            return i

        def pe_segment_narrow(pe, c, S, M, V, bf, n):
            b = r_open(pe, c)
            for t in range(ET):
                nc.tensor.matmul(b[0:P, t * n:(t + 1) * n], S[:, t, :], V(t), start=t == 0, stop=False)
                i = nc.tensor.matmul(b[0:P, t * n:(t + 1) * n], M[:, t, :], bf[0:NB, 0:n], start=False,
                                     stop=t == ET - 1)
            i.then_inc(R_ps, 1)

        def pe_rows_out(pe, c, pairs, n=D):
            for j in range(TG):
                b = r_open(pe, c)
                last = len(pairs) * KC - 1
                for q, (fT, W) in enumerate(pairs):
                    for k in range(KC):
                        i = nc.tensor.matmul(b[0:P, 0:n], fT[:, k, j * P:(j + 1) * P], W[:, k, :],
                                             start=q * KC + k == 0, stop=q * KC + k == last)
                i.then_inc(R_ps, 1)

        def act_evac(act, c, dst, src_rows=128, n=GR, func=ACT.Identity, **kw):
            act.wait_ge(T_ps, c.t + 1)
            c.t += 1
            nc.scalar.activation(dst, bank[(c.t - 1) % 4][0:src_rows, 0:n], func, **kw).then_inc(T_sb, 1)

        def act_root(act, c):
            act.wait_ge(L_sc, c.ln + 1)
            c.ln += 1
            nc.scalar.activation(lsr[:, :], lsr[:, :], ACT.Sqrt).then_inc(L_rt, 1)

        def link(dve, c, ins):
            ins.then_inc(dstep, 1)
            c.d += 1
            dve.wait_ge(dstep, c.d)

        def dve_evac(dve, c, f):
            dve.wait_ge(R_ps, c.r + 1)
            c.r += 1
            f(bank[4 + (c.r - 1) % 2]).then_inc(R_sb, 1)

        def dve_b_evac(dve, c, dst, n):
            dve.wait_ge(B_ps, c.b + 1)
            c.b += 1
            nc.vector.tensor_copy(dst, bank[7][0:NB, 0:n]).then_inc(B_sb, 1)

        def dve_ln_root(dve, c, rows4, doubled=False):
            for j in range(TG):
                i = nc.vector.bn_stats(lst[:, j, :], rows4[:, j, :])
            link(dve, c, i)
            for j in range(TG):
                i = nc.vector.bn_aggr(lmv[:, j, :], lst[:, j, :])
            link(dve, c, i)
            nc.vector.tensor_scalar(lsr[:, :], lmv[:, :, 1], 4.0 if doubled else 1.0, EPS, ALU.mult,
                                    ALU.add).then_inc(L_sc, 1)
            c.ln += 1

        def dve_ln_rows(dve, c, rows4, doubled=False):
            dve.wait_ge(L_rt, c.ln)
            link(dve, c, nc.vector.reciprocal(lrs[:, :], lsr[:, :]))
            if doubled:
                link(dve, c, nc.vector.tensor_scalar_mul(lrs[:, :], lrs[:, :], 2.0))
            for j in range(TG):
                nc.vector.tensor_scalar(rows4[:, j, :], rows4[:, j, :], lmv[:, j, 0:1], lrs[:, j:j + 1],
                                        ALU.subtract, ALU.mult).then_inc(L_y, 1)
            c.y += TG
            dve.wait_ge(L_y, c.y)

        def dve_ln(dve, c, rows4, doubled=False):
            dve_ln_root(dve, c, rows4, doubled)
            dve_ln_rows(dve, c, rows4, doubled)

        def gather(dst, table, idx, s, limit=None):
            nc.gpsimd.indirect_dma_start(out=dst, out_offset=None, in_=table,
                                         in_offset=bass.IndirectOffsetOnAxis(ap=idx, axis=0),
                                         bounds_check=limit, oob_is_err=limit is None).then_inc(s.s, 16)

        def store(sp, table, base, g, rows4, s):
            dst = grp(table[base:base + E, :], g)
            sp.dma_start(dst[0:HI], rows4[0:HI]).then_inc(s, 16)
            sp.dma_start(dst[HI:P], rows4[HI:P]).then_inc(s, 16)

        def load(sp, rows4, table, base, g, s):
            src = grp(table[base:base + E, :], g)
            sp.dma_start(rows4[0:HI], src[0:HI]).then_inc(s.s, 16)
            sp.dma_start(rows4[HI:P], src[HI:P]).then_inc(s.s, 16)

        def scatter(table, idx, src, s, limit=N - 1):
            nc.gpsimd.indirect_dma_start(out=table, out_offset=bass.IndirectOffsetOnAxis(ap=idx, axis=0),
                                         in_=src, in_offset=None, bounds_check=limit,
                                         oob_is_err=False).then_inc(s, 16)

        diag = at(14000, [ET, P], P)
        ones = sb("ones", [P, P])

        def sp_records(sp, c):
            sp.wait_ge(C["out"], 32 * NG)
            sp.dma_start(rec[:, :, :], rec_in.rearrange("(t p) q -> p t q", p=P)).then_inc(keys_in, 16)
            sp.dma_start(mask[:, :], mask_in).then_inc(keys_in, 16)
            sp.dma_start(abv[:, :], abs_in[0].partition_broadcast(P)).then_inc(keys_in, 16)
            sp.wait_ge(rec_put, 16 * 2 * ET)
            dv = RDd.rearrange("(t p) q -> p t q", p=P)
            sv = RSd.rearrange("(t p) q -> p t q", p=P)
            sp.dma_start(RD[:, :, :], dv).then_inc(rec_back, 16)
            sp.dma_start(rec[:, :, :], sv).then_inc(rec_back, 16)
            with nc.allow_non_contiguous_dma(reason="one key of each boundary record"):
                for q, (v, col) in enumerate(((dv, Q_DST), (sv, Q_SRC))):
                    sp.dma_start(bk[0:ET, q:q + 1], v[0, :, col:col + 1]).then_inc(rec_back, 16)
                    sp.dma_start(bk[ET:NB, q:q + 1], v[P - 1, :, col:col + 1]).then_inc(rec_back, 16)

        def dve_records(dve, c):
            dve.wait_ge(keys_in, 16 * 7)
            dve.wait_ge(counts, 6 * ET + 1)
            dve.wait_ge(signs, 3 * ET)
            by = cnt3[:, :].rearrange("p (q a t) -> p q a t", q=2, a=3)
            sg = sgn[:, :].rearrange("p (q t) -> p q t", q=3)
            for k, (q, a, dst) in enumerate(((0, 0, cnts[:, 0, 3, :]), (1, 2, own[:, 1, :]), (0, 2, own[:, 0, :]))):
                link(dve, c, nc.vector.scalar_tensor_tensor(dst, by[:, q, a, :], 2.0, sg[:, k, :], ALU.mult,
                                                            ALU.add))
                link(dve, c, nc.vector.tensor_scalar(dst, dst, -1.0, float(E), ALU.mult, ALU.add))
            dup = v20[:, 0:2, :]
            link(dve, c, nc.vector.tensor_copy(dup, by[:, :, 1, :]))
            link(dve, c, nc.vector.tensor_tensor(v20[:, 2:4, :], by[:, :, 0, :], dup, ALU.add))
            link(dve, c, nc.vector.tensor_copy(rank_i[:, :, :], v20[:, 2:4, :]))
            link(dve, c, nc.vector.tensor_scalar_min(own[:, 0:2, :], own[:, 0:2, :], 1.0))
            link(dve, c, nc.vector.tensor_scalar_add(own[:, 2, :], v20[:, 2, :], float(E)))
            link(dve, c, nc.vector.tensor_tensor(own[:, 3, :], by[:, 0, 2, :], own[:, 2, :], ALU.subtract))
            link(dve, c, nc.vector.tensor_tensor(own[:, 3, :], own[:, 3, :], own[:, 0, :], ALU.mult))
            link(dve, c, nc.vector.tensor_tensor(own[:, 3, :], own[:, 3, :], own[:, 2, :], ALU.add))
            link(dve, c, nc.vector.scalar_tensor_tensor(own[:, 4, :], by[:, 1, 2, :], float(E), v20[:, 2, :],
                                                        ALU.add, ALU.subtract))
            link(dve, c, nc.vector.tensor_tensor(own[:, 4, :], own[:, 4, :], own[:, 1, :], ALU.mult))
            link(dve, c, nc.vector.tensor_tensor(own[:, 4, :], own[:, 4, :], v20[:, 2, :], ALU.add))
            link(dve, c, nc.vector.tensor_scalar(own[:, 5, :], own[:, 0, :], -float(FAR), float(FAR), ALU.mult,
                                                 ALU.add))
            link(dve, c, nc.vector.tensor_tensor(own[:, 5, :], own[:, 5, :], by[:, 0, 2, :], ALU.add))
            link(dve, c, nc.vector.tensor_scalar(v20[:, 4:6, :], dup, 1.0, float(FAR), ALU.min, ALU.mult))
            link(dve, c, nc.vector.tensor_tensor(v20[:, 6:8, :], v20[:, 4:6, :],
                                                 kfc[:, :].rearrange("p (q t) -> p q t", q=2), ALU.add))
            for col, src in ((Q_DST, kfc[:, 0:ET]), (Q_SRC, kfc[:, ET:2 * ET]), (Q_DSC, v20[:, 6, :]),
                             (Q_SSC, v20[:, 7, :]), (Q_DUP, v20[:, 0, :]), (Q_RS, v20[:, 3, :]),
                             (Q_XD, own[:, 2, :]), (Q_DI, own[:, 3, :]), (Q_SI, own[:, 4, :]),
                             (Q_YI, own[:, 5, :])):
                nc.vector.tensor_copy(rec[:, :, col], src)
            nc.vector.tensor_copy(rec[:, :, Q_CNT], cnts[:, 0, 3, :]).then_inc(rec_done, 1)
            dve.wait_ge(rec_back, 16 * 6)
            for k, col in enumerate((Q_DST, Q_SRC, Q_DSC, Q_SSC, Q_SI, Q_DI, Q_RS)):
                nc.vector.tensor_copy(idd[:, k, :], RD[:, :, col])
            for k, col in enumerate((Q_XD, Q_SI, Q_YI)):
                nc.vector.tensor_copy(ids[:, k, :], rec[:, :, col])
            for k, col in enumerate((Q_DST, Q_SRC, Q_W)):
                i = nc.vector.tensor_copy(RSs[:, :, k], rec[:, :, col])
            i.then_inc(rec_done, 1)
            nc.vector.memset(ones[:, :], 1.0)
            nc.vector.tensor_scalar_add(bk[:, :], bk[:, :], 1.0)
            link(dve, c, nc.vector.memset(Bd[:, :], 0.0))
            for q in range(2):
                i = nc.vector.tensor_scalar(bkm[:, q, :], mask[:, :], bk[:, q:q + 1], None, ALU.mult)
            link(dve, c, i)
            link(dve, c, nc.vector.tensor_scalar_add(bkm[:, :, :], bkm[:, :, :], -1.0))

        def dve_build(dve, c, q, key, S, M, dg):
            dve.wait_ge(dstep, c.d)
            nc.vector.tensor_tensor(dg[:, :, :], spread(ident[0:P, 0:P], ET), b3(key, P), ALU.mult).then_inc(s_end, 1)
            for g in range(EG):
                kt = gcols(key, g)
                dve.wait_ge(R_ps, c.r + 1)
                b = bank[4 + c.r % 2]
                c.r += 1
                row = b[0:P, 0:GR].rearrange("p (t f) -> p t f", f=P)
                nc.vector.tensor_tensor(S[:, g * TG:(g + 1) * TG, :], row, b3(kt, P), ALU.is_equal)
                nc.vector.tensor_tensor(M[:, g * TG:(g + 1) * TG, :],
                                        b[0:NB, 0:GR].rearrange("p (t f) -> p t f", f=P),
                                        b3(gcols(bkm[:, q, :], g), P), ALU.is_equal).then_inc(R_sb, 1)
            dve.wait_ge(R_sb, c.r)

        def pe_build(pe, c, dg, n):
            pe.wait_ge(s_end, n)
            for g in range(EG):
                b = r_open(pe, c)
                nc.tensor.matmul(b[0:P, 0:GR], ones[:, :], dg[:, g * TG:(g + 1) * TG, :].rearrange("p t f -> p (t f)"),
                                 start=True, stop=True).then_inc(R_ps, 1)

        def dve_boundary_cols(dve, c, B, S, done):
            nc.vector.tensor_copy(B[:, 0:(ET - 1) * (NB + 1) + 1:NB + 1], S[:, :, 0])
            nc.vector.tensor_copy(B[:, ET:ET + (ET - 1) * (NB + 1) + 1:NB + 1], S[:, :, P - 1]).then_inc(done, 1)

        def pool_records(pool, c):
            pool.wait_ge(rec_done, 1)
            for q, table in enumerate((RDd, RSd)):
                for t in range(ET):
                    scatter(table, rank_i[:, q, t:t + 1], rec[:, t, :], rec_put, E - 1)
            pool.wait_ge(rec_done, 2)

        W1l, W2l = at(4096, [KC, D]), at(6144, [KC, D])
        V0 = at(8192, [ET, D], P)
        SN = at(18432, [ET, P], P)
        BN = at(20932, [NB * ET], P)
        BF0 = at(21732, [D], NB)
        XD0 = [at(22244, [TG, D], P), at(24292, [TG, D], P)]
        ZZ0 = at(26340, [TG, D], P)
        HR0 = at(28388, [TG, D], P)
        XT0, HT0, AT0 = at(30436, [KC, GR]), at(32436, [KC, GR]), at(34436, [KC, GR])
        w0_in = sem("layer0_weights_in")
        e0_x, e0_xd, e0_h, e0_pd = per_group("a", 0), per_group("b", 0), per_group("a", 64), per_group("h", 0)
        h_put, x1_put, pd_put, bn0 = sem("h_put"), sem("x1_put"), sem("pd_put"), sem("mean_weights")
        pd_sem = sem("part_rows_ready")

        def grp(dram, g):
            return dram[g * GR:(g + 1) * GR, :].rearrange("(t p) d -> p t d", p=P)

        def sp_L0(sp, c):
            sp.wait_ge(phase_end, 4 * c.ph)
            for dst, src in ((W1r, w_r1), (W2r, w_r2), (W1l, w_l1), (W2l, w_l2)):
                sp.dma_start(dst, src).then_inc(w0_in, 16)
            for g in range(EG):
                c.r += TG
                sp.wait_ge(R_sb, c.r)
                store(sp, Hd, 0, g, HR0, h_put)
                c.r += TG
                c.y += TG
                sp.wait_ge(L_y, c.y)
                store(sp, X1d, 0, g, ZZ0, x1_put)
            for g in range(EG):
                c.r += TG
                sp.wait_ge(R_sb, c.r)
                store(sp, Hd, E, g, HR0, h_put)
                c.r += TG
                sp.wait_ge(pd_sem, g + 1)
                store(sp, PDd, 0, g, ZZ0, pd_put)
            sp.wait_ge(pd_put, 32 * EG)
            for g in range(2):
                sp.wait_ge(R_sb, c.r)
                load(sp, XD0[g], PDd, 0, g, e0_pd[g])
            for g in range(EG):
                c.r += TG
                c.y += TG
                sp.wait_ge(L_y, c.y)
                store(sp, X1d, E, g, ZZ0, x1_put)
                if g + 2 < EG:
                    load(sp, XD0[g % 2], PDd, 0, g + 2, e0_pd[g + 2])
            sp.wait_ge(x1_put, 2 * 32 * EG)

        def sp_L1(sp, c):
            for g in range(EG):
                load(sp, CR[:, g * TG:(g + 1) * TG, :], X1d, E, g, e1_b[g])
            for g in range(EG):
                c.y += TG
                sp.wait_ge(L_y, c.y)
                store(sp, X2d, E, g, CR[:, g * TG:(g + 1) * TG, :], x2_put)
            c.r += EG + 1 + ET

            def step(i):
                for g in range(EG):
                    if isinstance(i, int) and i == 1:
                        sp.wait_ge(y_rdy, TG * (g + 1))
                    else:
                        sp.wait_ge(R_sb, i * ET + (c.r - 2 * ET + TG * (g + 1)))
                    store(sp, Yd, 0, g, Y[:, g * TG:(g + 1) * TG, :], y_put)
            step(1)
            with sp.Fori(2, ITERS) as i:
                step(i)
            c.r += ET * (ITERS - 1)
            for g in range(EG):
                c.y += TG
                sp.wait_ge(L_y, c.y)
                store(sp, X2d, 0, g, Y[:, g * TG:(g + 1) * TG, :], x2_put)
            sp.wait_ge(x2_put, 2 * 32 * EG)

        def pool_L0(pool, c):
            for t in range(ET):
                gather(V0[:, t, :], x, idd[:, 1, t:t + 1], e0_x[t // TG])
            for g in range(2):
                for j in range(TG):
                    gather(XD0[g][:, j, :], x, idd[:, 0, TG * g + j:TG * g + j + 1], e0_xd[g])
            c.r += 2 * TG * EG
            for g in range(EG):
                if g >= 2:
                    pool.wait_ge(R_sb, c.r - TG * 2)
                    for j in range(TG):
                        gather(XD0[g % 2][:, j, :], x, idd[:, 0, TG * g + j:TG * g + j + 1], e0_xd[g])
                c.r += 2 * TG
            pool.wait_ge(h_put, 2 * 32 * EG)
            pool.wait_ge(T_sb, c.t + 8 * EG + 12 * EG)
            for t in range(ET):
                gather(V0[:, t, :], Hd, idd[:, 4, t:t + 1], e0_h[t // TG])
            c.r += TG * EG
            c.t += 8 * EG + 12 * EG + 4 * EG
            c.y += 2 * TG * EG
            pool.wait_ge(x1_put, 2 * 32 * EG)

        def pe_L0(pe, c):
            pe.wait_ge(w0_in, 16 * 4)
            for g in range(EG):
                pe.wait_ge(*e0_x[g].full(16 * TG))
                pe_transpose_rows(pe, c, V0[:, g * TG:(g + 1) * TG, :])
                pe.wait_ge(T_sb, c.t)
                for m in range(KC):
                    b = t_open(pe, c)
                    for k in range(KC):
                        i = nc.tensor.matmul(b[:, 0:GR], W1r[:, k, m * 128:(m + 1) * 128], XT0[:, k, :],
                                             start=k == 0, stop=k == KC - 1)
                    i.then_inc(T_ps, 1)
                pe.wait_ge(T_sb, c.t)
                pe_transpose_back(pe, c, HT0)
                pe_rows_out(pe, c, [(HT0, W2r)])
            pe.wait_ge(bn0, 1)
            pe_boundaries(pe, c, BN, lambda t: V0[:, t, :], D)
            for g in range(EG):
                pe.wait_ge(*e0_xd[g].full(16 * TG))
                pe_transpose_rows(pe, c, XD0[g % 2])
                pe.wait_ge(B_sb, c.b)
                for k in range(KC):
                    b = t_open(pe, c)
                    pe_segment_T(pe, c, b, SN, Md, V0, BF0, g, k, True).then_inc(T_ps, 1)
                pe.wait_ge(T_sb, c.t)
                for m in range(KC):
                    b = t_open(pe, c)
                    for q, (fT, W) in enumerate(((XT0, W1r), (AT0, W1l))):
                        for k in range(KC):
                            i = nc.tensor.matmul(b[:, 0:GR], W[:, k, m * 128:(m + 1) * 128], fT[:, k, :],
                                                 start=q + k == 0, stop=q == 1 and k == KC - 1)
                    i.then_inc(T_ps, 1)
                pe.wait_ge(T_sb, c.t)
                pe_transpose_back(pe, c, HT0)
                pe_rows_out(pe, c, [(HT0, W2r)])
            pe_boundaries(pe, c, BN, lambda t: V0[:, t, :], D, lambda g: e0_h[g].full(16 * TG))
            pe.wait_ge(B_sb, c.b)
            for g in range(EG):
                for k in range(KC):
                    b = t_open(pe, c)
                    pe_segment_T(pe, c, b, SN, Md, V0, BF0, g, k, True).then_inc(T_ps, 1)
                pe.wait_ge(T_sb, c.t)
                pe_rows_out(pe, c, [(AT0, W2l)])

        def act_L0(act, c):
            for loop in range(2):
                for g in range(EG):
                    for k in range(KC):
                        act_evac(act, c, XT0[:, k, :])
                    if loop == 1:
                        for k in range(KC):
                            act_evac(act, c, AT0[:, k, :])
                    if c.r:
                        act.wait_ge(R_ps, c.r)
                    for m in range(KC):
                        act_evac(act, c, HT0[:, m, :], func=ACT.Relu, bias=colv[:, C_L0B1 + m:C_L0B1 + m + 1])
                    if loop == 0:
                        act_root(act, c)
                    c.r += 2 * TG
            for g in range(EG):
                act.wait_ge(R_ps, c.r)
                for k in range(KC):
                    act_evac(act, c, AT0[:, k, :])
                act_root(act, c)
                c.r += TG

        def dve_L0(dve, c):
            link(dve, c, nc.vector.reciprocal(v20[:, 8, :], RD[:, :, Q_CNT]))
            link(dve, c, nc.vector.tensor_tensor(SN[:, :, :], Sd[:, :, :], b3(v20[:, 8, :], P), ALU.mult))
            link(dve, c, nc.vector.memset(BN, 0.0))
            dve_boundary_cols(dve, c, BN, SN, bn0)
            dve.wait_ge(bn0, 1)
            b2row = spread(row(R_L0B2), TG)
            for loop in range(2):
                for g in range(EG):
                    res = V0[:, g * TG:(g + 1) * TG, :] if loop == 0 else XD0[g % 2]
                    if loop == 0:
                        dve.wait_ge(*e0_x[g].full(16 * TG))
                    else:
                        dve.wait_ge(*e0_xd[g].full(16 * TG))
                    if loop or g:
                        dve.wait_ge(h_put, 32 * (EG * loop + g))
                    for j in range(TG):
                        dve_evac(dve, c, lambda b: nc.vector.tensor_copy(HR0[:, j, :], b[0:P, :]))
                    if loop == 0 and g:
                        dve.wait_ge(x1_put, 32 * g)
                    if loop == 1:
                        dve.wait_ge(x1_put, 32 * EG)
                        if g:
                            dve.wait_ge(pd_put, 32 * g)
                    for j in range(TG):
                        dve_evac(dve, c, lambda b: nc.vector.tensor_tensor(ZZ0[:, j, :], res[:, j, :],
                                                                           b[0:P, :], ALU.add))
                    dve.wait_ge(R_sb, c.r)
                    i = nc.vector.tensor_tensor(ZZ0, ZZ0, b2row, ALU.add)
                    if loop == 1:
                        i.then_inc(pd_sem, 1)
                    else:
                        link(dve, c, i)
                        dve_ln(dve, c, ZZ0)
                dve_b_evac(dve, c, BF0, D)
            dve.wait_ge(pd_put, 32 * EG)
            for g in range(EG):
                dve.wait_ge(*e0_pd[g].full(32))
                if g:
                    dve.wait_ge(x1_put, 32 * (EG + g))
                for j in range(TG):
                    dve_evac(dve, c, lambda b: nc.vector.tensor_tensor(ZZ0[:, j, :], XD0[g % 2][:, j, :],
                                                                       b[0:P, :], ALU.add))
                dve.wait_ge(R_sb, c.r)
                dve_ln(dve, c, ZZ0)

        Ss, Ms = at(0, [ET, P], P), at(2500, [ET, P], NB)
        BW = at(5000, [NB * ET], P)
        BF1 = at(5800, [D], NB)
        V1, Y, CR = at(6312, [ET, D], P), at(16552, [ET, D], P), at(26792, [ET, D], P)
        J1 = at(37032, [2, D], P)
        diag1 = at(16552, [ET, P], P)
        e1_b, e1_v, e1_x, e1_y, e1_f = (per_group(*q) for q in (
            ("h", 32), ("a", 128), ("b", 64), ("a", 192), ("b", 128)))
        x2_put, y_put = sem("x2_put"), sem("y_put")
        sc1, sc1a = sem("layer1_scalars"), sem("layer1_scalars_act")
        sup_rdy, w1_rdy, zr, y_rdy = sem("sup_ready"), sem("weights1_ready"), sem("zero_rows"), sem("y_ready")
        SUP, NN, RR, NRR, SD, SSQ, DSQ, TMP = (v20[:, k, :] for k in range(8))

        def pool_L1(pool, c):
            for t in range(ET):
                gather(V1[:, t, :], X1d, ids[:, 0, t:t + 1], e1_v[t // TG])
            pool.wait_ge(R_sb, c.r + EG)
            for t in range(ET):
                gather(Y[:, t, :], X1d, ids[:, 1, t:t + 1], e1_x[t // TG])
            c.r += EG + 1 + ET
            c.y += ET
            pool.wait_ge(zr, 1)
            for i in range(1, ITERS):
                pool.wait_ge(y_put, i * (32 * EG))
                pool.wait_ge(R_sb, i * ET + (c.r - ET))
                for t in range(ET):
                    gather(V1[:, t, :], Yd, ids[:, 2, t:t + 1], e1_y[t // TG], E - 1)
            c.r += ET * (ITERS - 1)
            pool.wait_ge(R_sb, c.r)
            for t in range(ET):
                gather(CR[:, t, :], X1d, ids[:, 1, t:t + 1], e1_f[t // TG])
            c.y += ET
            pool.wait_ge(x2_put, 2 * 32 * EG)

        def pe_segment_rows(pe, c, V, ring):
            for t in range(ET):
                b = ring(t)
                nc.tensor.matmul(b[0:P, :], Ss[:, t, :], V[:, t, :], start=True, stop=False)
                nc.tensor.matmul(b[0:P, :], Ms[:, t, :], BF1[:, :], start=False, stop=True).then_inc(R_ps, 1)

        def pe_L1(pe, c):
            pe_build(pe, c, diag1, 2)
            pe.wait_ge(sup_rdy, 1)
            pe_boundaries(pe, c, BW, lambda t: SUP[:, t:t + 1], 1)
            pe.wait_ge(B_sb, c.b)
            pe_segment_narrow(pe, c, Ss, Ms, lambda t: SUP[:, t:t + 1], BF1, 1)
            pe.wait_ge(w1_rdy, 2)
            pe_boundaries(pe, c, BW, lambda t: V1[:, t, :], D)
            pe.wait_ge(B_sb, c.b)
            pe_segment_rows(pe, c, V1, lambda t: r_open(pe, c))
            r0, b0 = c.r, c.b
            assert ET % 2 == 0

            def step(i):
                def ring(t):
                    pe.wait_ge(R_sb, i * ET + (r0 - ET + t - 1))
                    return bank[4 + (r0 + t) % 2]
                pe.wait_ge(B_sb, i + (b0 - 1))
                for t in range(ET):
                    if t % TG == 0:
                        pe.wait_ge(*e1_y[t // TG].full(i * (16 * TG)))
                    q = nc.tensor.matmul(bank[7][0:NB, :], BW[:, t * NB:(t + 1) * NB], V1[:, t, :],
                                         start=t == 0, stop=t == ET - 1)
                q.then_inc(B_ps, 1)
                pe.wait_ge(B_sb, i + b0)
                pe_segment_rows(pe, c, V1, ring)
            step(1)
            with pe.Fori(2, ITERS) as i:
                step(i)
            c.r = r0 + ET * (ITERS - 1)
            c.b = b0 + ITERS - 1

        def act_L1(act, c):
            for g in range(EG):
                act_root(act, c)
            act.wait_ge(sc1, 1)
            nc.scalar.activation(v20[:, 5:7, :], v20[:, 5:7, :], ACT.Sqrt).then_inc(sc1a, 1)
            nc.scalar.activation(abv[:, :], abv[:, :], ACT.Exp).then_inc(sc1a, 1)
            act.wait_ge(sc1, 2)
            nc.scalar.activation(SD, SD, ACT.Exp).then_inc(sc1a, 1)
            for g in range(EG):
                act_root(act, c)

        def dve_L1(dve, c):
            dve_build(dve, c, 1, RSs[:, :, 1], Ss, Ms, diag1)
            link(dve, c, nc.vector.memset(BW, 0.0))
            dve_boundary_cols(dve, c, BW, Ss, w1_rdy)
            dve.wait_ge(w1_rdy, 1)
            for g in range(EG):
                dve.wait_ge(*e1_b[g].full(32))
                dve_ln(dve, c, CR[:, g * TG:(g + 1) * TG, :], doubled=True)
            for t in range(ET):
                if t % TG == 0:
                    dve.wait_ge(*e1_v[t // TG].full(16 * TG))
                    dve.wait_ge(*e1_x[t // TG].full(16 * TG))
                for k, (p, q) in enumerate(((Y, V1), (Y, Y), (V1, V1))):
                    link(dve, c, nc.vector.scalar_tensor_tensor(
                        J1[:, k % 2, :], p[:, t, :], 1.0, q[:, t, :], ALU.mult, ALU.mult,
                        accum_out=v20[:, 4 + k, t:t + 1]))
            nc.vector.tensor_scalar_max(v20[:, 5:7, :], v20[:, 5:7, :], 1e-12).then_inc(sc1, 1)
            dve.wait_ge(sc1a, 2)
            link(dve, c, nc.vector.reciprocal(v20[:, 5:7, :], v20[:, 5:7, :]))
            link(dve, c, nc.vector.tensor_tensor(SD, SD, SSQ, ALU.mult))
            link(dve, c, nc.vector.tensor_tensor(SD, SD, DSQ, ALU.mult))
            link(dve, c, nc.vector.tensor_tensor(TMP, RSs[:, :, 0], RSs[:, :, 1], ALU.not_equal))
            link(dve, c, nc.vector.tensor_tensor(SD, SD, TMP, ALU.mult))
            sg = v20[:, 8, 0:1]
            link(dve, c, nc.vector.tensor_tensor(sg, abv[:, 2:3], abv[:, 2:3], ALU.mult))
            link(dve, c, nc.vector.tensor_scalar_mul(sg, sg, 4.0))
            link(dve, c, nc.vector.reciprocal(sg, sg))
            nc.vector.tensor_scalar(SD, SD, sg, None, ALU.mult).then_inc(sc1, 1)
            dve.wait_ge(sc1a, 3)
            nc.vector.tensor_tensor(SUP, SD, RSs[:, :, 2], ALU.mult).then_inc(sup_rdy, 1)
            dve_b_evac(dve, c, BF1[:, 0:1], 1)
            dve_evac(dve, c, lambda b: nc.vector.tensor_copy(NN, b[0:P, 0:ET]))
            dve.wait_ge(R_sb, c.r)
            al, be = abv[:, 0:1], abv[:, 1:2]
            link(dve, c, nc.vector.tensor_scalar(RR, NN, al, be, ALU.mult, ALU.add))
            link(dve, c, nc.vector.tensor_scalar(RR, RR, al, None, ALU.add))
            link(dve, c, nc.vector.reciprocal(RR, RR))
            link(dve, c, nc.vector.tensor_scalar(RR, RR, al, None, ALU.mult))
            link(dve, c, nc.vector.scalar_tensor_tensor(NRR, RR, -1.0, NN, ALU.mult, ALU.mult))
            link(dve, c, nc.vector.tensor_tensor(TMP, SUP, RR, ALU.mult))
            link(dve, c, nc.vector.tensor_tensor(Ss[:, :, :], Ss[:, :, :], b3(TMP, P), ALU.mult))
            dve_boundary_cols(dve, c, BW, Ss, w1_rdy)
            dve.wait_ge(w1_rdy, 2)
            dve_b_evac(dve, c, BF1, D)
            dve.wait_ge(x2_put, 32 * EG)
            for t in range(ET):
                dve_evac(dve, c, lambda b: nc.vector.scalar_tensor_tensor(
                    CR[:, t, :], Y[:, t, :], NRR[:, t:t + 1], b[0:P, :], ALU.mult, ALU.add))
            dve.wait_ge(R_sb, c.r)
            for t in range(ET):
                nc.vector.tensor_copy(Y[:, t, :], CR[:, t, :]).then_inc(y_rdy, 1)
            dve.wait_ge(y_rdy, ET)
            for t in range(0, ET, TG):
                i = nc.vector.memset(V1[:, t:t + TG, :], 0.0)
            i.then_inc(zr, 1)
            r0, b0 = c.r, c.b
            pre = sem("y_before_sums")

            def step(i):
                dve.wait_ge(y_put, i * (32 * EG))
                for t in range(ET):
                    nc.vector.scalar_tensor_tensor(Y[:, t, :], Y[:, t, :], RR[:, t:t + 1], CR[:, t, :],
                                                   ALU.mult, ALU.add).then_inc(pre, 1)
                dve.wait_ge(B_ps, i + b0)
                nc.vector.tensor_copy(BF1, bank[7][0:NB, :]).then_inc(B_sb, 1)
                dve.wait_ge(pre, i * ET)
                for t in range(ET):
                    dve.wait_ge(R_ps, i * ET + (r0 - ET + t + 1))
                    nc.vector.tensor_tensor(Y[:, t, :], Y[:, t, :], bank[4 + (r0 + t) % 2][0:P, :],
                                            ALU.add).then_inc(R_sb, 1)
                dve.wait_ge(R_sb, i * ET + r0)
            step(1)
            with dve.Fori(2, ITERS) as i:
                step(i)
            c.r, c.b = r0 + ET * (ITERS - 1), b0 + ITERS - 1
            for g in range(EG):
                dve.wait_ge(*e1_f[g].full(16 * TG))
                Yg = Y[:, g * TG:(g + 1) * TG, :]
                link(dve, c, nc.vector.scalar_tensor_tensor(
                    Yg.rearrange("p t d -> p (t d)"), CR[:, g * TG:(g + 1) * TG, :].rearrange("p t d -> p (t d)"),
                    2.0, Yg.rearrange("p t d -> p (t d)"), ALU.mult, ALU.add))
                dve_ln(dve, c, Yg)

        WQ, WK, WV, WO = (at(2048 * k, [KC, D]) for k in range(4))
        V2 = at(8192, [ET, D], P)
        BF2 = at(18432, [D], NB)
        XS2a, XD2, KQ2, T2, U2 = (at(18944 + G4 * k, [TG, D], P) for k in range(5))
        XS2 = (XS2a, at(38400 - G4, [TG, D], P))
        XT2, YT2, TT2 = (at(29184 + 2000 * k, [KC, GR]) for k in range(3))
        F1T2 = at(35184, [GR], 34)
        eT, negT, FT = (at(18944 + 2500 * k, [E], H) for k in range(3))
        EE, EN, EX, FC = (at(35684 + ET * H * k, [ET, H], P) for k in range(4))
        w2_in, q_rdy, e_rdy, f_rdy, ft_rdy = (sem(k) for k in "w2_in q_ready e_ready fc_ready ft_ready".split())
        ex_in, ex_rdy, at_rdy, x3_put, bd_rdy = (sem(k) for k in "ex_in ex_ready attn_ready x3_put bd_ready".split())
        A_L1 = 192 + 64 * (ITERS - 1)
        x2_s, x2_d, x2_d2 = per_group("a", A_L1), per_group("b", 192), per_group("b", 256)

        T2_0 = EG * (8 + 12 + 4)
        Y2_0 = 4 * ET

        def y2_first(g):
            return Y2_0 + (3 * TG * g - TG if g else TG)

        def y2_tail(g):
            return Y2_0 + 3 * TG * (g + 1) + (TG if g + 1 < EG else 0)

        def sp_L2(sp, c):
            sp.wait_ge(phase_end, 4 * c.ph)
            for dst, src in ((WQ, w_q), (WK, w_k), (WV, w_v), (WO, w_o)):
                sp.dma_start(dst, src).then_inc(w2_in, 16)
            for g in range(EG):
                sp.wait_ge(L_y, y2_tail(g))
                store(sp, X3d, 0, g, U2, x3_put)
            c.y = y2_tail(EG - 1)
            for g in range(EG):
                c.y += 3 * TG
                sp.wait_ge(L_y, c.y)
                store(sp, X3d, E, g, U2, x3_put)
            sp.wait_ge(x3_put, 2 * 32 * EG)

        def sp_L3(sp, c):
            sp.wait_ge(phase_end, 4 * c.ph)
            sp.dma_start(RD[:, :, :], RSd.rearrange("(t p) q -> p t q", p=P)).then_inc(rec_back, 16)

        def pe_ffn(pe, c, rows, TT, F1T):
            pe_transpose_rows(pe, c, rows)
            pe.wait_ge(T_sb, c.t)
            b = t_open(pe, c)
            for k in range(KC):
                i = nc.tensor.matmul(b[0:32, 0:GR], wcol(W_L2A + 32 * k, 32), TT[:, k, :], start=k == 0,
                                     stop=k == KC - 1)
            i.then_inc(T_ps, 1)
            pe.wait_ge(T_sb, c.t)
            for j in range(TG):
                b = r_open(pe, c)
                nc.tensor.matmul(b[0:P, :], F1T[:, j * P:(j + 1) * P], w32s[:, V_L2B:V_L2B + D], start=True,
                                 stop=True).then_inc(R_ps, 1)

        def act_ffn(act, c, TT, F1T):
            for k in range(KC):
                act_evac(act, c, TT[:, k, :], scale=colv[:, C_LN1G + k:C_LN1G + k + 1],
                         bias=colv[:, C_LN1B + k:C_LN1B + k + 1])
            act.wait_ge(R_ps, c.r)
            act_evac(act, c, F1T[0:32, :], src_rows=32, func=ACT.Relu, bias=colv[0:32, C_L2B1:C_L2B1 + 1])
            c.r += TG

        def dve_ffn_sum(dve, c, Tn, Un):
            link(dve, c, nc.vector.tensor_tensor(Un, Tn, spread(row(R_LN1G), TG), ALU.mult))
            for j in range(TG):
                dve_evac(dve, c, lambda b: nc.vector.tensor_tensor(Un[:, j, :], Un[:, j, :], b[0:P, :], ALU.add))
            dve.wait_ge(R_sb, c.r)

        def dve_ffn_tail(dve, c, Un, res, part):
            if part == 0:
                dve_ln_root(dve, c, Un)
            elif part == 1:
                dve_ln_rows(dve, c, Un)
                link(dve, c, nc.vector.tensor_tensor(Un, Un, spread(row(R_LN2G), TG), ALU.mult))
            elif part == 2:
                link(dve, c, nc.vector.tensor_tensor(Un, Un, spread(row(R_LN2B), TG), ALU.add))
                link(dve, c, nc.vector.tensor_tensor(Un, Un, res, ALU.add))
                dve_ln_root(dve, c, Un)
            else:
                dve_ln_rows(dve, c, Un)

        def pool_L2(pool, c):
            for g in range(EG):
                if g >= 2:
                    c.y = y2_tail(g - 2)
                    pool.wait_ge(L_y, c.y)
                for j in range(TG):
                    t = TG * g + j
                    gather(XS2[g % 2][:, j, :], X2d, idd[:, 6, t:t + 1], x2_s[g])
                if g:
                    pool.wait_ge(T_sb, T2_0 + 13 * (g - 1) + 8)
                for j in range(TG):
                    t = TG * g + j
                    gather(XD2[:, j, :], X2d, idd[:, 5, t:t + 1], x2_d[g])
                c.r += 4 * TG
            c.y = y2_tail(EG - 1)
            c.r += 2 * EG + 1 + 1 + 1
            pool.wait_ge(R_sb, c.r)
            for g in range(EG):
                pool.wait_ge(L_y, c.y)
                for j in range(TG):
                    t = TG * g + j
                    gather(XD2[:, j, :], X2d, idd[:, 5, t:t + 1], x2_d2[g])
                c.r += 2 * TG
                c.y += 3 * TG
            pool.wait_ge(x3_put, 2 * 32 * EG)

        def pe_L2(pe, c):
            pe.wait_ge(w2_in, 16 * 4)
            for g in range(EG):
                pe.wait_ge(*x2_s[g].full(16 * TG))
                pe_transpose_rows(pe, c, XS2[g % 2])
                pe.wait_ge(*x2_d[g].full(16 * TG))
                pe_transpose_rows(pe, c, XD2)
                pe.wait_ge(T_sb, c.t)
                for j in range(TG):
                    for fT, W in ((YT2, WQ), (XT2, WK), (XT2, WV)):
                        b = r_open(pe, c)
                        for k in range(KC):
                            i = nc.tensor.matmul(b[0:P, :], fT[:, k, j * P:(j + 1) * P], W[:, k, :],
                                                 start=k == 0, stop=k == KC - 1)
                        i.then_inc(R_ps, 1)
                pe.wait_ge(L_y, y2_first(g))
                pe_ffn(pe, c, T2, TT2, F1T2)
            c.y = y2_tail(EG - 1)
            pe.wait_ge(e_rdy, 1)
            for src in (EE, EN):
                for g in range(EG):
                    b = r_open(pe, c)
                    for j in range(TG):
                        i = nc.tensor.transpose(b[0:H, j * P:(j + 1) * P], src[:, TG * g + j, :], ident[0:P, 0:P])
                    i.then_inc(R_ps, 1)
            pe.wait_ge(ft_rdy, 1)
            b = r_open(pe, c)
            for t in range(ET):
                i = nc.tensor.transpose(b[0:P, t * H:(t + 1) * H], FT[:, t * P:(t + 1) * P], ident[0:H, 0:H])
            i.then_inc(R_ps, 1)
            for done, src in ((f_rdy, FC), (ex_rdy, EX)):
                pe.wait_ge(done, 1)
                pe_boundaries(pe, c, Bd[:, :], lambda t: src[:, t, :], H)
                pe.wait_ge(B_sb, c.b)
                pe_segment_narrow(pe, c, Sd, Md, lambda t: src[:, t, :], BF2, H)
            pe.wait_ge(at_rdy, 1)
            pe_boundaries(pe, c, Bd[:, :], lambda t: V2[:, t, :], D)
            pe.wait_ge(B_sb, c.b)
            for g in range(EG):
                for k in range(KC):
                    b = t_open(pe, c)
                    pe_segment_T(pe, c, b, Sd, Md, V2, BF2, g, k, True).then_inc(T_ps, 1)
                pe.wait_ge(T_sb, c.t)
                pe_rows_out(pe, c, [(XT2, WO)])
                c.y += TG
                pe.wait_ge(L_y, c.y)
                pe_ffn(pe, c, T2, TT2, F1T2)
                c.y += 2 * TG

        def act_L2(act, c):
            c.r += EG + 1 + ET * ITERS
            for g in range(EG):
                act.wait_ge(R_ps, c.r)
                for fT in (XT2, YT2):
                    for k in range(KC):
                        act_evac(act, c, fT[:, k, :])
                act_root(act, c)
                if g:
                    for q in range(2):
                        act_root(act, c)
                c.r += 3 * TG
                act_ffn(act, c, TT2, F1T2)
            for q in range(2):
                act_root(act, c)
            act.wait_ge(ex_in, 1)
            nc.scalar.activation(EX[:, :, :], EX[:, :, :], ACT.Exp).then_inc(ex_rdy, 1)
            c.r += 2 * EG + 3
            for g in range(EG):
                act.wait_ge(R_ps, c.r)
                for k in range(KC):
                    act_evac(act, c, XT2[:, k, :])
                c.r += TG
                act_root(act, c)
                act_ffn(act, c, TT2, F1T2)
                for q in range(2):
                    act_root(act, c)

        def dve_L2(dve, c):
            nc.vector.memset(F1T2[32:34, :], 1.0)
            for g in range(EG):
                dve.wait_ge(*x2_s[g].full(16 * TG))
                link(dve, c, nc.vector.tensor_copy(T2, XS2[g % 2]))
                dve_ln(dve, c, T2)
                for j in range(TG):
                    t = TG * g + j
                    dve_evac(dve, c, lambda b: nc.vector.tensor_copy(KQ2[:, j, :], b[0:P, :]))
                    dve.wait_ge(R_sb, c.r)
                    dve_evac(dve, c, lambda b: nc.vector.tensor_tensor(KQ2[:, j, :], KQ2[:, j, :], b[0:P, :],
                                                                       ALU.mult))
                    dve_evac(dve, c, lambda b: nc.vector.tensor_copy(V2[:, t, :], b[0:P, :]))
                    if g:
                        dve_ffn_tail(dve, c, U2, XS2[(g - 1) % 2], j)
                dve.wait_ge(R_sb, c.r)
                for j in range(TG):
                    i = nc.vector.tensor_reduce(EE[:, TG * g + j, :],
                                                KQ2[:, j, :].rearrange("p (h d) -> p h d", h=H), AX.X, ALU.add)
                link(dve, c, i)
                if g:
                    dve.wait_ge(x3_put, 32 * g)
                dve_ffn_sum(dve, c, T2, U2)
            for part in range(4):
                dve_ffn_tail(dve, c, U2, XS2[(EG - 1) % 2], part)
            start = v20[:, 9, :]
            link(dve, c, nc.vector.tensor_scalar(start, RD[:, :, Q_DSC], float(FAR), NEG, ALU.is_lt, ALU.mult))
            nc.vector.tensor_copy(EN[:, :, :], b3(start, H)).then_inc(e_rdy, 1)
            for dst, f in ((eT, 0.125), (negT, 1.0)):
                assert DK == 64
                for g in range(EG):
                    dve_evac(dve, c, lambda b: nc.vector.tensor_scalar_mul(dst[:, g * GR:(g + 1) * GR],
                                                                           b[0:H, 0:GR], f))
            dve.wait_ge(R_sb, c.r)
            nc.vector.tensor_tensor_scan(FT, negT, eT, NEG, ALU.add, ALU.max).then_inc(ft_rdy, 1)
            last = v20[:, 10, :]
            link(dve, c, nc.vector.tensor_scalar_add(last, RD[:, :, Q_DUP], 1.0))
            link(dve, c, nc.vector.tensor_tensor(last, last, RD[:, :, Q_CNT], ALU.is_equal))
            dve_evac(dve, c, lambda b: nc.vector.tensor_tensor(
                FC[:, :, :], b[0:P, 0:ET * H].rearrange("p (t h) -> p t h", h=H), b3(last, H), ALU.mult))
            dve.wait_ge(R_sb, c.r)
            link(dve, c, nc.vector.memset(Bd[:, :], 0.0))
            dve_boundary_cols(dve, c, Bd, Sd, f_rdy)
            dve_b_evac(dve, c, BF2[:, 0:H], H)
            dve.wait_ge(R_ps, c.r + 1)
            bmax = bank[4 + c.r % 2][0:P, 0:ET * H].rearrange("p (t h) -> p t h", h=H)
            c.r += 1
            nc.vector.scalar_tensor_tensor(EX[:, :, :], EE[:, :, :], 0.125, bmax, ALU.mult,
                                           ALU.subtract).then_inc(R_sb, 1)
            dve.wait_ge(R_sb, c.r)
            nc.vector.memset(lst[:, :, :], 0.0).then_inc(ex_in, 1)
            dve_b_evac(dve, c, BF2[:, 0:H], H)
            dve_evac(dve, c, lambda b: nc.vector.reciprocal(
                FC[:, :, :], b[0:P, 0:ET * H].rearrange("p (t h) -> p t h", h=H)))
            dve.wait_ge(R_sb, c.r)
            link(dve, c, nc.vector.tensor_tensor(EX[:, :, :], EX[:, :, :], FC[:, :, :], ALU.mult))
            for t in range(ET):
                vt = V2[:, t, :].rearrange("p (h d) -> p h d", h=H)
                i = nc.vector.tensor_tensor(vt, vt, b3(EX[:, t, :], DK), ALU.mult)
            i.then_inc(at_rdy, 1)
            dve_b_evac(dve, c, BF2, D)
            dve.wait_ge(x3_put, 32 * EG)
            for g in range(EG):
                dve.wait_ge(*x2_d2[g].full(16 * TG))
                for j in range(TG):
                    dve_evac(dve, c, lambda b: nc.vector.tensor_tensor(T2[:, j, :], XD2[:, j, :], b[0:P, :],
                                                                       ALU.add))
                dve.wait_ge(R_sb, c.r)
                dve_ln(dve, c, T2)
                if g:
                    dve.wait_ge(x3_put, 32 * (EG + g))
                dve_ffn_sum(dve, c, T2, U2)
                for part in range(4):
                    dve_ffn_tail(dve, c, U2, XD2, part)

        diag3 = at(0, [ET, P], P)
        V3 = at(0, [ET, D], P)
        BF3 = at(10240, [D], NB)
        XS3, XD3, SR3, WA3 = (at(10752 + G4 * k, [TG, D], P) for k in range(4))
        PST, PDT, XG3, ND3 = (at(18944 + 2000 * k, [KC, GR]) for k in range(4))
        XST, XDT = (at(26944 + 2000 * k, [KC, GR]) for k in range(2))
        O3 = at(30944, [TG, D], P)
        G1T = at(32992, [2, GR])
        GT3, N1T3, IPT = (at(33992 + GR * k, [GR]) for k in range(3))
        SQ3 = XG3[:, 1:4, :]
        EAT, SX, SA, FS, SS = (at(35492 + GR * k, [GR], 32) for k in range(5))
        x3_s, x3_d, x3_d2 = per_group("a", A_L1 + 64), per_group("b", 320), per_group("b", 384)
        n1_in, n1_rdy, xg_rdy, ip_rdy, sp_in3, sp_rdy, v3_rdy = (sem(k) for k in
            "n1_in n1_ready xg_ready ip_ready softplus_in softplus_ready v3_ready".split())
        out_put = sem("out_put")

        XD3s = (XD3, XS3)

        def pool_L3(pool, c):
            pool.wait_ge(rec_done, 3)
            c.r += EG
            for g in range(EG):
                if g:
                    pool.wait_ge(R_sb, c.r)
                for k, (dst, s) in enumerate(((XS3, x3_s), (XD3, x3_d))):
                    for j in range(TG):
                        t = TG * g + j
                        gather(dst[:, j, :], X3d, idd[:, 1 - k, t:t + 1], s[g])
                    if g and not k:
                        for j in range(TG):
                            pool.wait_ge(L_y, c.y + j + 1)
                            scatter(out, idd[:, 2, TG * (g - 1) + j:TG * (g - 1) + j + 1], O3[:, j, :], out_put)
                        c.y += TG
                c.r += 4 * TG
            pool.wait_ge(R_sb, c.r)
            for g in range(2):
                for j in range(TG):
                    t = TG * g + j
                    gather(XD3s[g][:, j, :], X3d, idd[:, 0, t:t + 1], x3_d2[g])
            for j in range(TG):
                pool.wait_ge(L_y, c.y + j + 1)
                scatter(out, idd[:, 2, TG * (EG - 1) + j:TG * (EG - 1) + j + 1], O3[:, j, :], out_put)
            c.y += TG
            pool.wait_ge(out_put, 16 * ET)
            for g in range(EG):
                for j in range(TG):
                    pool.wait_ge(L_y, c.y + j + 1)
                    scatter(out, idd[:, 3, TG * g + j:TG * g + j + 1], O3[:, j, :], out_put)
                c.y += TG
                if g + 2 < EG:
                    for j in range(TG):
                        t = TG * (g + 2) + j
                        gather(XD3s[g % 2][:, j, :], X3d, idd[:, 0, t:t + 1], x3_d2[g + 2])
            pool.wait_ge(out_put, 2 * 16 * ET)

        def pe_one(pe, c, rows, n, pairs):
            b = t_open(pe, c)
            for q, (W, fT) in enumerate(pairs):
                i = nc.tensor.matmul(b[0:rows, 0:n], W, fT, start=q == 0, stop=q == len(pairs) - 1)
            i.then_inc(T_ps, 1)

        def pe_gate(pe, c, fT, n):
            pe.wait_ge(n1_rdy, n)
            for m in range(2):
                pe_one(pe, c, 128, GR, [(wcol(W_G1 + 128 * m, 128), fT[:, 0, :]),
                                        (wcol(W_G1 + 256 + 128 * m, 128), N1T3)])
            pe.wait_ge(T_sb, c.t)
            for m in range(2):
                pe_one(pe, c, 128, GR, [(wcol(W_G2 + 128 * m, 128), G1T[:, 0, :]),
                                        (wcol(W_G2 + 256 + 128 * m, 128), G1T[:, 1, :])])
            pe.wait_ge(xg_rdy, n)

        def act_gate(act, c, fT, n):
            for k in range(KC):
                act_evac(act, c, fT[:, k, :])
            act.wait_ge(n1_in, n)
            nc.scalar.activation(N1T3, SQ3[:, 0, :], ACT.Sqrt, scale=1.0 / 3.0).then_inc(n1_rdy, 1)
            for m in range(2):
                act_evac(act, c, G1T[:, m, :], func=ACT.Silu, bias=colv[:, C_BG1 + m:C_BG1 + m + 1])
            for m, dst in enumerate((XG3[:, 0, :], GT3)):
                act_evac(act, c, dst, bias=colv[:, C_BG2 + m:C_BG2 + m + 1])

        def dve_gate(dve, c, fT, n, t0):
            dve.wait_ge(T_sb, t0)
            for k in range(3):
                i = nc.vector.tensor_tensor(SQ3[:, k, :], fT[:, k + 1, :], fT[:, k + 1, :], ALU.mult)
            link(dve, c, i)
            link(dve, c, nc.vector.tensor_tensor(SQ3[:, 0, :], SQ3[:, 0, :], SQ3[:, 1, :], ALU.add))
            nc.vector.tensor_tensor(SQ3[:, 0, :], SQ3[:, 0, :], SQ3[:, 2, :], ALU.add).then_inc(n1_in, 1)
            dve.wait_ge(T_sb, t0 + 4)
            for k in range(3):
                i = nc.vector.tensor_tensor(XG3[:, k + 1, :], fT[:, k + 1, :], GT3, ALU.mult)
            i.then_inc(xg_rdy, 1)

        def dve_last(dve, c, rows):
            for j in range(TG):
                dve.wait_ge(R_ps, c.r + 1)
                b = bank[4 + c.r % 2]
                c.r += 1
                nc.vector.scalar_tensor_tensor(vec3(O3[:, j, 128:D]), vec3(rows[:, j, 128:D]), 2.0,
                                               b[0:P, 128:D].rearrange("p (c u) -> p c u", c=3),
                                               ALU.mult, ALU.add)
                nc.vector.scalar_tensor_tensor(O3[:, j, 0:128], rows[:, j, 0:128], 2.0, b[0:P, 0:128],
                                               ALU.mult, ALU.add).then_inc(R_sb, 1)
            dve.wait_ge(R_sb, c.r)
            link(dve, c, nc.vector.tensor_tensor(O3[:, :, 0:128], O3[:, :, 0:128], spread(row(R_L3, 128), TG),
                                                 ALU.add))
            dve_ln(dve, c, O3)

        def pe_last(pe, c, fT):
            for j in range(TG):
                b = r_open(pe, c)
                for k in range(KC):
                    i = nc.tensor.matmul(b[0:P, k * 128:(k + 1) * 128], fT[:, k, j * P:(j + 1) * P],
                                         wcol(W_O1 if k else W_O0, 128), start=k == 0, stop=k == KC - 1)
                i.then_inc(R_ps, 1)

        def pe_L3(pe, c):
            pe_build(pe, c, diag3, 3)
            for g in range(EG):
                pe.wait_ge(*x3_s[g].full(16 * TG))
                pe_transpose_rows(pe, c, XS3, True)
                pe_gate(pe, c, XST, g + 1)
                for k in range(KC):
                    pe_one(pe, c, 128, GR, [(wcol(W_ND1 if k else W_ND0, 128), XG3[:, k, :])])
                for j in range(TG):
                    b = r_open(pe, c)
                    for k in range(KC):
                        i = nc.tensor.matmul(b[0:P, k * 128:(k + 1) * 128], XG3[:, k, j * P:(j + 1) * P],
                                             wcol(W_ND1 if k else W_ND0, 128), start=k == 0, stop=k == KC - 1)
                    i.then_inc(R_ps, 1)
                pe.wait_ge(*x3_d[g].full(16 * TG))
                pe_transpose_rows(pe, c, XD3, True)
                pe.wait_ge(T_sb, c.t)
                for k in range(KC):
                    pe_one(pe, c, 128, GR, [(wcol(W_PRE1 if k else W_PRE0, 128), XDT[:, k, :])])
                for k in range(1, KC):
                    pe_one(pe, c, 128, GR, [(wcol(W_PRE1, 128), XST[:, k, :])])
                b = t_open(pe, c)
                for j in range(TG):
                    i = nc.tensor.transpose(b[0:32, j * P:(j + 1) * P], RD[:, TG * g + j, Q_EA:Q_SSC],
                                            ident[0:P, 0:P])
                i.then_inc(T_ps, 1)
                pe.wait_ge(T_sb, c.t)
                pe_one(pe, c, 32, GR, [(w32s[0:32, V_F1:V_F1 + 32], EAT)])
                pe.wait_ge(ip_rdy, g + 1)
                pe_one(pe, c, 32, GR, [(wcol(W_S1, 32), PDT[:, 0, :]), (wcol(W_S1 + 32, 32), PDT[:, 0, :]),
                                       (wcol(W_S1 + 64, 32), IPT)])
                pe.wait_ge(sp_rdy, 2 * g + 2)
                for j in range(TG):
                    for src, w in ((FS, V_F2), (SS, V_S2)):
                        b = r_open(pe, c)
                        nc.tensor.matmul(b[0:P, :], src[:, j * P:(j + 1) * P], w32s[0:32, w:w + D], start=True,
                                         stop=True).then_inc(R_ps, 1)
                pe_last(pe, c, ND3)
            pe.wait_ge(v3_rdy, EG)
            pe_boundaries(pe, c, Bd[:, :], lambda t: V3[:, t, :], D)
            pe.wait_ge(B_sb, c.b)
            for g in range(EG):
                pe.wait_ge(*x3_d2[g].full(16 * TG))
                pe_transpose_rows(pe, c, XD3s[g % 2], True)
                pe_gate(pe, c, XDT, EG + g + 1)
                for k in range(KC):
                    b = t_open(pe, c)
                    nc.tensor.matmul(b[:, 0:GR], wcol(W_ND1 if k else W_ND0, 128), XG3[:, k, :], start=True,
                                     stop=False)
                    pe_segment_T(pe, c, b, Sd, Md, V3, BF3, g, k, False).then_inc(T_ps, 1)
                pe.wait_ge(T_sb, c.t)
                pe_last(pe, c, ND3)

        def act_nd(act, c):
            act_evac(act, c, ND3[:, 0, :], bias=colv[:, C_BND:C_BND + 1])
            for k in range(1, KC):
                act_evac(act, c, ND3[:, k, :])

        def act_softplus(act, c):
            act.wait_ge(T_ps, c.t + 1)
            c.t += 1
            b = bank[(c.t - 1) % 4][0:32, 0:GR]
            nc.scalar.activation(SX, b, ACT.Identity)
            nc.scalar.activation(SA, b, ACT.Abs).then_inc(T_sb, 1)
            act.wait_ge(T_sb, c.t)
            nc.scalar.activation(SA, SA, ACT.Exp, scale=-1.0).then_inc(astep, 1)
            c.a += 1
            act.wait_ge(astep, c.a)
            nc.scalar.activation(SA, SA, ACT.Ln, bias=1.0).then_inc(sp_in3, 1)

        def act_L3(act, c):
            c.r += EG
            for g in range(EG):
                act.wait_ge(R_ps, c.r)
                act_gate(act, c, XST, g + 1)
                act_nd(act, c)
                for k in range(KC):
                    act_evac(act, c, XDT[:, k, :])
                act_evac(act, c, PDT[:, 0, :], bias=colv[:, C_BPRE:C_BPRE + 1])
                for k in range(1, KC):
                    act_evac(act, c, PDT[:, k, :])
                for k in range(1, KC):
                    act_evac(act, c, PST[:, k, :], scale=1.0 / 3.0)
                act_evac(act, c, EAT, src_rows=32)
                if g:
                    act.wait_ge(sp_rdy, 2 * g)
                act_softplus(act, c)
                act.wait_ge(sp_rdy, 2 * g + 1)
                act_softplus(act, c)
                act_root(act, c)
                c.r += TG + 2 * TG + TG
            for g in range(EG):
                act.wait_ge(R_ps, c.r)
                act_gate(act, c, XDT, EG + g + 1)
                act_nd(act, c)
                act_root(act, c)
                c.r += TG

        def dve_L3(dve, c):
            t0 = EG * (8 + 12 + 4) + EG * (13 + 9)
            dve.wait_ge(rec_back, 16 * 7)
            for k, col in enumerate((Q_SI, Q_XD, Q_DSC, Q_SSC)):
                i = nc.vector.tensor_copy(idd[:, k, :], RD[:, :, col])
            i.then_inc(rec_done, 1)
            dve.wait_ge(rec_done, 3)
            dve_build(dve, c, 1, RD[:, :, Q_SRC], Sd, Md, diag3)
            link(dve, c, nc.vector.memset(Bd[:, :], 0.0))
            dve_boundary_cols(dve, c, Bd, Sd, bd_rdy)
            dve.wait_ge(bd_rdy, 1)
            for g in range(EG):
                dve_gate(dve, c, XST, g + 1, t0 + 4)
                for j in range(TG):
                    dve_evac(dve, c, lambda b: nc.vector.tensor_copy(SR3[:, j, :], b[0:P, :]))
                dve.wait_ge(R_sb, c.r)
                link(dve, c, nc.vector.tensor_tensor(
                    SR3[:, :, 0:128], SR3[:, :, 0:128], spread(rowv[:, R_L3, 128:256], TG), ALU.add))
                dve.wait_ge(T_sb, t0 + 23)
                for k in range(1, KC):
                    i = nc.vector.tensor_tensor(PST[:, k, :], PST[:, k, :], PDT[:, k, :], ALU.mult)
                link(dve, c, i)
                link(dve, c, nc.vector.tensor_tensor(PST[:, 1, :], PST[:, 1, :], PST[:, 2, :], ALU.add))
                nc.vector.tensor_tensor(IPT, PST[:, 1, :], PST[:, 3, :], ALU.add).then_inc(ip_rdy, 1)
                for k, dst in enumerate((FS, SS)):
                    dve.wait_ge(sp_in3, 2 * g + k + 1)
                    link(dve, c, nc.vector.scalar_tensor_tensor(dst, SX, 0.0, SA, ALU.max, ALU.add))
                    nc.vector.tensor_scalar_add(dst, dst, -LN2).then_inc(sp_rdy, 1)
                for j in range(TG):
                    dve_evac(dve, c, lambda b: nc.vector.tensor_copy(WA3[:, j, :], b[0:P, :]))
                    dve.wait_ge(R_sb, c.r)
                    dve_evac(dve, c, lambda b: nc.vector.tensor_tensor(WA3[:, j, :], WA3[:, j, :], b[0:P, :],
                                                                       ALU.mult))
                dve.wait_ge(R_sb, c.r)
                if g:
                    dve.wait_ge(out_put, 64 * g)
                for j in range(TG):
                    t = TG * g + j
                    w = [WA3[:, j, 128 * k:128 * (k + 1)] for k in range(4)]
                    sh = [RD[:, t, Q_SH + k:Q_SH + k + 1] for k in range(4)]
                    x0, x1 = SR3[:, j, 0:128], [SR3[:, j, 128 * k:128 * (k + 1)] for k in (1, 2, 3)]
                    o = [V3[:, t, 128 * k:128 * (k + 1)] for k in range(4)]
                    tmp = O3[:, 0, :]
                    S1, S2, S3 = tmp[:, 0:128], tmp[:, 128:256], O3[:, 1, 128:D]
                    link(dve, c, nc.vector.tensor_scalar(S1, x1[0], sh[1], None, ALU.mult))
                    link(dve, c, nc.vector.scalar_tensor_tensor(S1, x1[1], sh[2], S1, ALU.mult, ALU.add))
                    link(dve, c, nc.vector.scalar_tensor_tensor(S1, x1[2], sh[3], S1, ALU.mult, ALU.add))
                    nc.vector.scalar_tensor_tensor(S1, S1, 3.0 ** -0.5, w[3], ALU.mult, ALU.mult)
                    nc.vector.scalar_tensor_tensor(S2, x0, sh[0], w[0], ALU.mult, ALU.mult)
                    for k in range(3):
                        nc.vector.scalar_tensor_tensor(o[k + 1], x0, sh[k + 1], w[1], ALU.mult, ALU.mult)
                    link(dve, c, nc.vector.scalar_tensor_tensor(
                        S3.rearrange("p (c u) -> p c u", c=3), SR3[:, j, 128:D].rearrange("p (c u) -> p c u", c=3),
                        sh[0], spread(w[2], 3), ALU.mult, ALU.mult))
                    nc.vector.tensor_tensor(o[0], S1, S2, ALU.add)
                    link(dve, c, nc.vector.tensor_tensor(V3[:, t, 128:D], V3[:, t, 128:D], S3, ALU.add))
                nc.vector.memset(lst[:, :, :], 0.0).then_inc(v3_rdy, 1)
                dve_last(dve, c, XS3)
                t0 += 26
            c.t = t0
            dve_b_evac(dve, c, BF3, D)
            for g in range(EG):
                dve.wait_ge(out_put, 64 * (EG + g))
                dve_gate(dve, c, XDT, EG + g + 1, c.t + 4)
                c.t += 12
                dve_last(dve, c, XD3s[g % 2])

        @block.sync
        def _(sp):
            for dst, src in ((ident, ident_in), (colv, cols), (ws, wsmall), (w32s, w32), (W1r, w_r1),
                             (W2r, w_r2)):
                sp.dma_start(dst[:], src).then_inc(s_w, 16)
            sp.dma_start(rowv[:, :, :], rows.partition_broadcast(P)).then_inc(s_w, 16)
            sp_in(sp, 0, 0)
            for q in range(2):
                sp.dma_start(keys_f[q].bitcast(I32), keys[q].partition_broadcast(P)).then_inc(keys_in, 16)
            sp.dma_start(kfc[:, :].bitcast(I32), key_cols).then_inc(keys_in, 16)
            sp.dma_start(ones[:, :], earlier_in).then_inc(keys_in, 16)
            sp_in(sp, 1, 1)

            def step(s, par):
                if not isinstance(s, int) or s + 1 < NG:
                    sp_in(sp, s + 1, 1 - par)
                if has(s, "S"):
                    sp_out(sp, s - LAG["S"])
            for s in range(1, LAG["S"]):
                step(s, s % 2)
            with sp.Fori(LAG["S"] // 2, NG // 2 - 1) as i:
                step(i * 2, 0)
                step(i * 2 + 1, 1)
            for s in range(NG - 2, STEPS):
                step(s, s % 2)
            c = Counts()
            sp_records(sp, c)
            c.ph, c.r = 1, EG
            sp_L0(sp, c)
            c.ph = 2
            sp.wait_ge(phase_end, 4 * c.ph)
            sp_L1(sp, c)
            c.ph = 3
            sp_L2(sp, c)
            c.ph = 4
            sp_L3(sp, c)

        @block.tensor
        def _(pe):
            pe.wait_ge(s_w, 16 * 7)
            node_steps(pe, lambda st_, s, par: pe_step(pe, st_, s, par))
            c = Counts()
            pe_build(pe, c, diag, 1)
            end_phase(pe, c)
            pe_L0(pe, c)
            end_phase(pe, c)
            pe_L1(pe, c)
            end_phase(pe, c)
            pe_L2(pe, c)
            end_phase(pe, c)
            pe_L3(pe, c)

        @block.scalar
        def _(act):
            act.wait_ge(s_w, 16 * 7)
            act.wait_ge(counts, 1)
            node_steps(act, lambda st_, s, par: act_step(act, st_, s, par))
            c = Counts()
            c.r = EG
            end_phase(act, c)
            act_L0(act, c)
            end_phase(act, c)
            act_L1(act, c)
            end_phase(act, c)
            act_L2(act, c)
            end_phase(act, c)
            act_L3(act, c)

        @block.vector
        def _(dve):
            nc.vector.memset(f1T[32:34, :], 1.0)
            nc.vector.memset(earlier[:, 0:E], 1)
            nc.vector.memset(earlier[:, E + P:2 * E], 0)
            dve.wait_ge(s_w, 16 * 7)
            dve.wait_ge(keys_in, 16 * 4)
            nc.vector.tensor_copy(earlier[:, E:E + P], ones[:, :])
            for q in range(2):
                nc.vector.tensor_copy(keys_f[q], keys_f[q].bitcast(I32))
            nc.vector.tensor_copy(kfc[:, :], kfc[:, :].bitcast(I32)).then_inc(neg_rdy, 1)
            dve.wait_ge(neg_rdy, 1)
            nc.vector.tensor_scalar_mul(neg_key[:, :], kfc[:, :], -1.0).then_inc(counts, 1)
            node_steps(dve, lambda st_, s, par: dve_step(dve, st_, s, par))
            c = Counts()
            dve_records(dve, c)
            dve_build(dve, c, 0, RD[:, :, Q_DST], Sd, Md, diag)
            end_phase(dve, c)
            dve_L0(dve, c)
            end_phase(dve, c)
            dve_L1(dve, c)
            end_phase(dve, c)
            dve_L2(dve, c)
            end_phase(dve, c)
            dve_L3(dve, c)

        @block.gpsimd
        def _(pool):
            pool.wait_ge(s_w, 16 * 7)
            node_steps(pool, lambda st_, s, par: pool_step(pool, st_, s, par))
            c = Counts()
            pool_records(pool, c)
            c.r = EG
            end_phase(pool, c)
            pool_L0(pool, c)
            end_phase(pool, c)
            pool_L1(pool, c)
            end_phase(pool, c)
            pool_L2(pool, c)
            end_phase(pool, c)
            pool_L3(pool, c)


def kernel(**inputs):
    import numpy as np
    import concourse.bacc as bacc
    from concourse.bass_utils import run_bass_kernel_spmd

    a = {k: np.asarray(v) for k, v in inputs.items()}
    f32 = np.float32

    def colsof(v):
        return v.reshape(-1, 128).T

    def chunks(w):
        return np.ascontiguousarray(w.reshape(w.shape[0] // 128, 128, -1).transpose(1, 0, 2))

    def flat(w):
        return chunks(w).reshape(128, -1)

    cols = np.zeros((128, C_END), f32)
    cols[:, C_L0B1:C_LN1G] = colsof(a["L0_gnn_b1"])
    cols[:, C_LN1G:C_LN1B] = colsof(a["L2_gnn_ln1_g"])
    cols[:, C_LN1B:C_L2B1] = colsof(a["L2_gnn_ln1_b"])
    cols[0:32, C_L2B1] = a["L2_gnn_b1"]
    cols[:, C_BG1:C_BG2] = colsof(a["L3_gnn_b_g1"])
    cols[:, C_BG2:C_BND] = colsof(a["L3_gnn_b_g2"])
    cols[:, C_BND] = a["L3_gnn_b_nd0"]
    cols[:, C_BPRE] = a["L3_gnn_b_pre0"]
    rows = np.zeros((R_END, D), f32)
    for r, k in ((R_L0B2, "L0_gnn_b2"), (R_LN1G, "L2_gnn_ln1_g"), (R_LN2G, "L2_gnn_ln2_g"),
                 (R_LN2B, "L2_gnn_ln2_b")):
        rows[r] = a[k]
    rows[R_L3, 0:128] = a["L3_gnn_b_o0"]
    rows[R_L3, 128:256] = a["L3_gnn_b_nd0"]
    rows[R_L3, 256:384] = a["L3_gnn_b_pre0"]
    wsmall = np.concatenate([flat(a["L3_gnn_" + k]) for k in
                             ("W_g1", "W_g2", "W_nd0", "W_nd1", "W_o0", "W_o1", "W_pre0", "W_pre1", "W_s1")]
                            + [flat(a["L2_gnn_W1"])], axis=1)
    w32 = np.zeros((34, V_END), f32)
    w32[0:32] = np.concatenate([a["L2_gnn_W2"], a["L3_gnn_W_f2"], a["L3_gnn_W_s2"], a["L3_gnn_W_f1"]], axis=1)
    w32[32, 0:D] = a["L2_gnn_ln1_b"]
    w32[33, 0:D] = a["L2_gnn_b2"]
    rec = np.zeros((E, Q_END), f32)
    rec[:, Q_W] = a["edge_weight"]
    rec[:, Q_SH:Q_EA] = a["edge_attr_4"]
    rec[:, Q_EA:Q_SSC] = a["edge_attr_32"]
    t = np.arange(ET)
    mask = np.concatenate([t[:, None] > t[None, :], t[:, None] < t[None, :]]).astype(f32)
    arrays = {"x": a["x"], "cols": cols, "rows": rows, "wsmall": wsmall, "w32": w32,
              "ident_in": np.eye(128, dtype=f32),
              "w_r1": chunks(a["L0_gnn_W1_r"].T), "w_r2": chunks(a["L0_gnn_W2_r"].T),
              "w_l1": chunks(a["L0_gnn_W1_l"].T), "w_l2": chunks(a["L0_gnn_W2_l"].T),
              "w_q": chunks(a["L2_gnn_Wq"]), "w_k": chunks(a["L2_gnn_Wk"]),
              "w_v": chunks(a["L2_gnn_Wv"]), "w_o": chunks(a["L2_gnn_Wo"]),
              "keys": np.stack([a["dst"], a["src"]]),
              "key_cols": np.concatenate([a["dst"].reshape(ET, P).T, a["src"].reshape(ET, P).T], axis=1),
              "rec_in": rec, "earlier_in": np.tril(np.ones((P, P), f32), -1), "mask_in": mask,
              "abs_in": np.concatenate([a["L1_gnn_alpha"], a["L1_gnn_beta"], a["L1_gnn_sigma"]])[None, :]}
    nc = bacc.Bacc("TRN2", target_bir_lowering=False, num_devices=1)
    args = [nc.dram_tensor(k, v.shape, mybir.dt.from_np(v.dtype), kind="ExternalInput").ap()
            for k, v in arrays.items()]
    out = nc.dram_tensor("out", (N, D), F32, kind="ExternalOutput").ap()
    gnn_kernel(nc, *args, out)
    r = run_bass_kernel_spmd(nc, [{k: np.ascontiguousarray(v) for k, v in arrays.items()}], core_ids=[0])
    return r.results[0]["out"]
```

```python
import concourse.bass as bass
from concourse import mybir
from contextlib import ExitStack

N, E, D = 10000, 2500, 512
P = 125
TG = 4
GR = P * TG
NG = N // GR
KC = D // 128
HI = 112
EPS = 1e-5
F32, I32 = mybir.dt.float32, mybir.dt.int32
ALU, ACT, AX = mybir.AluOpType, mybir.ActivationFunctionType, mybir.AxisListType

C_L0B1, C_LN1G, C_LN1B, C_L2B1, C_BG1, C_BG2, C_BND, C_BPRE, C_END = 0, 4, 8, 12, 13, 15, 17, 18, 19
R_L0B2, R_LN1G, R_LN2G, R_LN2B, R_L3, R_END = range(6)
W_G1, W_G2, W_ND0, W_ND1, W_O0, W_O1, W_PRE0, W_PRE1, W_S1, W_L2A, W_END = \
    0, 512, 1024, 1152, 1280, 1408, 1536, 1664, 1792, 1888, 2016
V_L2B, V_F2, V_S2, V_F1, V_END = 0, 512, 1024, 1536, 1568
ET = E // P
EG = ET // TG
NB = 2 * ET
H, DK = 8, D // 8
ITERS = 10
Q_DST, Q_SRC, Q_W, Q_DSC, Q_SH, Q_EA, Q_SSC, Q_CNT, Q_DUP, Q_SI, Q_DI, Q_RS, Q_YI, Q_XD, Q_END = \
    0, 1, 2, 3, 4, 8, 40, 41, 42, 43, 44, 45, 46, 47, 48
FAR = 1 << 20
NEG = -1e30
LN2 = 0.6931471805599453


def gnn_kernel(nc, x, cols, rows, wsmall, w32, ident_in, w_r1, w_r2, w_l1, w_l2, w_q, w_k, w_v, w_o,
               keys, key_cols, rec_in, earlier_in, mask_in, abs_in, out):
    ctx = ExitStack()
    with ctx:
        def sb(name, shape, dt=F32):
            return ctx.enter_context(nc.sbuf_tensor(name, shape, dt))

        def sem(name):
            return ctx.enter_context(nc.semaphore(name))

        bank = [ctx.enter_context(nc.psum_tensor(f"bank{i}", [128, 512], F32)) for i in range(8)]

        ident = sb("ident", [128, 128])
        colv = sb("colv", [128, C_END])
        rowv = sb("rowv", [P, R_END, D])
        ws = sb("ws", [128, W_END])
        w32s = sb("w32s", [34, V_END])
        AR = 38400
        arena = sb("arena", [128, AR])

        def at(off, shape, parts=128, dt=F32):
            n = 1
            for v in shape:
                n *= v
            assert off + n <= AR, (off, shape)
            ap = arena[0:parts, off:off + n]
            if dt != F32:
                ap = ap.bitcast(dt)
            if len(shape) == 2:
                ap = ap.rearrange("p (a b) -> p a b", b=shape[1])
            return ap

        G4 = TG * D
        W1r, W2r = at(0, [KC, D]), at(2048, [KC, D])
        X = [at(4096 + G4 * i, [TG, D], P) for i in range(2)]
        Z = at(8192, [TG, D], P)
        T = [at(10240 + G4 * i, [TG, D], P) for i in range(2)]
        U = at(14336, [TG, D], P)
        X3 = [at(16384 + G4 * i, [TG, D], P) for i in range(2)]
        O = at(20480, [TG, D], P)
        xT, hT, tT = at(22528, [KC, GR]), at(24528, [KC, GR]), at(26528, [KC, GR])
        x3T = at(28528, [KC, GR])
        xgT, ndT = at(30528, [KC, GR]), at(32528, [KC, GR])
        sq = xgT[:, 1:4, :]
        g1T = at(34528, [2, GR])
        f1T, n1T, gateT = at(35528, [GR], 34), at(36028, [GR]), at(36528, [GR])
        st = sb("st", [P, 4, TG, 6])
        n_even = sb("n_even", [P, 4, 1])
        mv = sb("mv", [P, 4, TG, 2])
        dd = sb("dd", [P, 2, TG])
        sr = sb("sr", [P, 4, 2, TG])
        rs = sb("rs", [P, 4, TG])
        nb = sb("nb", [P, 4, TG])
        q2 = [sb(f"q2_{i}", [P, TG]) for i in range(2)]

        s_w = sem("weights_in")
        A = {k: sem("A_" + k) for k in
             "x_in0 x_in1 xb z bn ag sc rt rc t".split()}
        B = {k: sem("B_" + k) for k in
             "tg z bn ag sc rt rc u ug ub z3 bn3 ag3 sc3 rt3 rc3 x3".split()}
        C = {k: sem("C_" + k) for k in
             "sq sqs n1 xg o bn ag sc rt rc y out".split()}

        def wcol(a, n):
            return ws[:, a:a + n]

        def row(r, n=D):
            return rowv[:, r, 0:n]

        def b3(ap, n):
            return ap.unsqueeze(2).broadcast_to([ap.shape[0], ap.shape[1], n])

        def spread(ap, n):
            return ap.unsqueeze(1).broadcast_to([ap.shape[0], n, ap.shape[1]])

        def vec3(ap):
            return ap.rearrange("p (u c) -> p c u", c=3)

        block = ctx.enter_context(nc.Block())

        def grows(dram, g):
            return dram[bass.ds(g * GR, GR), :].rearrange("(t p) d -> p t d", p=P)

        NT_ps, NT_sb, NR_ps, NR_sb = (sem(k) for k in "NT_ps NT_sb NR_ps NR_sb".split())
        TB, RB = [0, 1, 2, 3, 7], [4, 5, 6]
        PARTS = [("c_x", "C", "t", 4), ("a_x", "A", "t", 4), ("a_h1", "A", "t", 2), ("c_g1", "C", "t", 2),
                 ("a_h2", "A", "t", 2), ("b_t", "B", "t", 4), ("c_g2", "C", "t", 2), ("a_o1", "A", "r", 2),
                 ("b_f1", "B", "t", 1), ("c_nd", "C", "t", 4), ("a_o2", "A", "r", 2), ("b_f", "B", "r", 4),
                 ("c_o", "C", "r", 4)]
        LAG = {"A": 0, "B": 1, "L": 2, "C": 3, "S": 4}
        STEPS = NG + LAG["S"]
        FULL_T = sum(n for _, _, r, n in PARTS if r == "t")
        FULL_R = sum(n for _, _, r, n in PARTS if r == "r")
        assert FULL_T % len(TB) == 0 and FULL_R % len(RB) == 0

        def has(s, stage):
            return not isinstance(s, int) or 0 <= s - LAG[stage] < NG

        class Step:
            def __init__(self, s, k0):
                self.s, self.at = s, {}
                i0 = 0 if isinstance(s, int) else 1
                self.end = dict(k0)
                for part, stage, ring, n in PARTS:
                    self.at[part] = (self.end[ring], ring)
                    if has(s, stage):
                        self.end[ring] += n
                self.shift = {"t": 0, "r": 0}

            def count(self, part, i=0):
                k, ring = self.at[part]
                return self.shift[ring] + (k + i) if not isinstance(self.shift[ring], int) \
                    else self.shift[ring] + k + i

            def bank(self, part, i):
                k, ring = self.at[part]
                ring = TB if ring == "t" else RB
                return bank[ring[(k + i) % len(ring)]]

        def node_steps(eng, step):
            k = {"t": 0, "r": 0}
            for s in range(LAG["S"]):
                st_ = Step(s, k)
                step(st_, s, s % 2)
                k = st_.end
            lo, hi = LAG["S"] // 2, NG // 2
            with eng.Fori(lo, hi) as i:
                kk = k
                for par in range(2):
                    st_ = Step(i * 2 + par, kk)
                    st_.shift = {"t": i * (2 * FULL_T) - 2 * FULL_T * lo, "r": i * (2 * FULL_R) - 2 * FULL_R * lo}
                    step(st_, i * 2 + par, par)
                    kk = st_.end
            n = hi - lo
            k = {"t": k["t"] + 2 * FULL_T * n, "r": k["r"] + 2 * FULL_R * n}
            for s in range(NG, STEPS):
                st_ = Step(s, k)
                step(st_, s, s % 2)
                k = st_.end

        def later(n, least=1):
            return not isinstance(n, int) or n >= least

        def sp_in(sp, n, par):
            if later(n, 2):
                sp.wait_ge(A["t"], 4 * n - 4)
            src = grows(x, n)
            sp.dma_start(X[par][0:HI], src[0:HI]).then_inc(A[f"x_in{par}"], 16)
            sp.dma_start(X[par][HI:P], src[HI:P]).then_inc(A[f"x_in{par}"], 16)

        def sp_out(sp, n):
            sp.wait_ge(C["y"], 4 * n + 4)
            dst = grows(out, n)
            sp.dma_start(dst[0:HI], O[0:HI]).then_inc(C["out"], 16)
            sp.dma_start(dst[HI:P], O[HI:P]).then_inc(C["out"], 16)

        def pe_step(pe, st_, s, par):
            nC = s - LAG["C"]
            hA, hB, hC = has(s, "A"), has(s, "B"), has(s, "C")

            def t_bank(part, i):
                u = st_.count(part, i)
                if not isinstance(u, int) or u >= len(TB):
                    pe.wait_ge(NT_sb, u - (len(TB) - 1))
                return st_.bank(part, i)

            def r_bank(part, i):
                u = st_.count(part, i)
                if not isinstance(u, int) or u >= len(RB):
                    pe.wait_ge(NR_sb, u - (len(RB) - 1))
                return st_.bank(part, i)

            def rows_T(part, rows4, interleaved=False):
                for k in range(KC):
                    b = t_bank(part, k)
                    for j in range(TG):
                        src = vec3(rows4[:, j, 128:D])[:, k - 1, :] if interleaved and k \
                            else rows4[:, j, k * 128:(k + 1) * 128]
                        i = nc.tensor.transpose(b[:, j * P:(j + 1) * P], src, ident[0:P, 0:P])
                    i.then_inc(NT_ps, 1)

            def hidden(part, m0):
                for q in range(2):
                    m = m0 + q
                    b = t_bank(part, q)
                    for k in range(KC):
                        i = nc.tensor.matmul(b[:, 0:GR], W1r[:, k, m * 128:(m + 1) * 128], xT[:, k, :],
                                             start=k == 0, stop=k == KC - 1)
                    i.then_inc(NT_ps, 1)

            def gate(part, w, f0, f1):
                for m in range(2):
                    b = t_bank(part, m)
                    nc.tensor.matmul(b[:, 0:GR], wcol(w + 128 * m, 128), f0, start=True, stop=False)
                    nc.tensor.matmul(b[:, 0:GR], wcol(w + 256 + 128 * m, 128), f1, start=False,
                                     stop=True).then_inc(NT_ps, 1)

            def out_rows(part, j0):
                for q in range(2):
                    j = j0 + q
                    b = r_bank(part, q)
                    for k in range(KC):
                        i = nc.tensor.matmul(b[0:P, :], hT[:, k, j * P:(j + 1) * P], W2r[:, k, :],
                                             start=k == 0, stop=k == KC - 1)
                    i.then_inc(NR_ps, 1)

            if hC:
                pe.wait_ge(B["x3"], 4 * nC + 4)
                rows_T("c_x", X3[1 - par], True)
            if hA:
                pe.wait_ge(A[f"x_in{par}"], 16 * s + (32 - 16 * par))
                rows_T("a_x", X[par])
                pe.wait_ge(NT_sb, st_.count("a_x", 4))
                hidden("a_h1", 0)
            if hC:
                pe.wait_ge(C["n1"], nC + 1)
                gate("c_g1", W_G1, x3T[:, 0, :], n1T[:, :])
            if hA:
                hidden("a_h2", 2)
            if hB:
                pe.wait_ge(A["t"], 4 * s)
                rows_T("b_t", T[1 - par])
            if hC:
                pe.wait_ge(NT_sb, st_.count("c_g1", 2))
                gate("c_g2", W_G2, g1T[:, 0, :], g1T[:, 1, :])
            if hA:
                pe.wait_ge(NT_sb, st_.count("a_h2", 2))
                out_rows("a_o1", 0)
            if hB:
                pe.wait_ge(NT_sb, st_.count("b_t", 4))
                b = t_bank("b_f1", 0)
                for k in range(KC):
                    i = nc.tensor.matmul(b[0:32, 0:GR], wcol(W_L2A + 32 * k, 32), tT[:, k, :],
                                         start=k == 0, stop=k == KC - 1)
                i.then_inc(NT_ps, 1)
            if hC:
                pe.wait_ge(NT_sb, st_.count("c_g2", 2))
                for k in range(KC):
                    if k >= 1:
                        pe.wait_ge(C["xg"], 3 * nC + k)
                    nc.tensor.matmul(t_bank("c_nd", k)[:, 0:GR], wcol(W_ND1 if k else W_ND0, 128), xgT[:, k, :],
                                     start=True, stop=True).then_inc(NT_ps, 1)
            if hA:
                out_rows("a_o2", 2)
            if hB:
                pe.wait_ge(NT_sb, st_.count("b_f1", 1))
                for j in range(TG):
                    nc.tensor.matmul(r_bank("b_f", j)[0:P, :], f1T[:, j * P:(j + 1) * P],
                                     w32s[:, V_L2B:V_L2B + D], start=True, stop=True).then_inc(NR_ps, 1)
            if hC:
                pe.wait_ge(NT_sb, st_.count("c_nd", 4))
                for j in range(TG):
                    b = r_bank("c_o", j)
                    for k in range(KC):
                        i = nc.tensor.matmul(b[0:P, k * 128:(k + 1) * 128], ndT[:, k, j * P:(j + 1) * P],
                                             wcol(W_O1 if k else W_O0, 128), start=k == 0, stop=k == KC - 1)
                    i.then_inc(NR_ps, 1)

        def act_step(act, st_, s, par):
            nB, nL, nC, nS = (s - LAG[k] for k in "BLCS")

            def evac(part, i, dst, parts=128, func=ACT.Identity, **kw):
                act.wait_ge(NT_ps, st_.count(part, i + 1))
                nc.scalar.activation(dst, st_.bank(part, i)[0:parts, 0:GR], func, **kw).then_inc(NT_sb, 1)

            def col(c):
                return colv[:, c:c + 1]

            def hidden(part, m0):
                for q in range(2):
                    evac(part, q, hT[:, m0 + q, :], func=ACT.Relu, bias=col(C_L0B1 + m0 + q))

            def sign_pass(q):
                if has(s, "A"):
                    mine, theirs = ((0, 0), (1, 0), (0, 1))[q]
                    if later(s, 1) or q:
                        act.wait_ge(signs, 3 * s + q)
                    nc.scalar.activation(junk_s, keys_f[theirs], ACT.Sign, bias=key_of(neg_key, mine, s),
                                         accum_out=key_of(sgn, q, s)).then_inc(signs, 1)

            if has(s, "C"):
                if later(nC):
                    act.wait_ge(C["xg"], 3 * nC)
                for k in range(KC):
                    evac("c_x", k, x3T[:, k, :])
            if has(s, "A"):
                for k in range(KC):
                    evac("a_x", k, xT[:, k, :])
            if has(s, "L"):
                act.wait_ge(B["sc"], nL + 1)
                nc.scalar.activation(sr[:, 1, 0, :], sr[:, 1, 0, :], ACT.Sqrt).then_inc(B["rt"], 1)
            if has(s, "B"):
                act.wait_ge(A["rc"], 3 * s)
                if later(s, 3):
                    act.wait_ge(B["z3"], 4 * s - 8)
                for j in range(TG):
                    nc.scalar.activation(T[1 - par][:, j, :], Z[:, j, :], ACT.Identity, scale=rs[:, 0, j:j + 1],
                                         bias=nb[:, 0, j:j + 1]).then_inc(A["t"], 1)
            if has(s, "C"):
                act.wait_ge(C["sqs"], 2 * nC + 2)
                nc.scalar.activation(n1T[:, :], sq[:, 0, :], ACT.Sqrt, scale=1.0 / 3.0).then_inc(C["n1"], 1)
            if has(s, "A"):
                if later(s):
                    act.wait_ge(A["z"], 4 * s)
                hidden("a_h1", 0)
            if has(s, "C"):
                for m in range(2):
                    evac("c_g1", m, g1T[:, m, :], func=ACT.Silu, bias=col(C_BG1 + m))
            if has(s, "L"):
                act.wait_ge(B["rc"], 2 * nL + 2)
                for j in range(TG):
                    nc.scalar.activation(U[:, j, :], U[:, j, :], ACT.Identity, scale=rs[:, 1, j:j + 1],
                                         bias=nb[:, 1, j:j + 1]).then_inc(B["u"], 1)
            if has(s, "A"):
                hidden("a_h2", 2)
            sign_pass(0)
            if has(s, "B"):
                for k in range(KC):
                    evac("b_t", k, tT[:, k, :], scale=col(C_LN1G + k), bias=col(C_LN1B + k))
            if has(s, "C"):
                for m, dst in enumerate((xgT[:, 0, :], gateT[:, :])):
                    evac("c_g2", m, dst, bias=col(C_BG2 + m))
            if has(s, "L"):
                act.wait_ge(B["sc3"], nL + 1)
                nc.scalar.activation(sr[:, 2, 0, :], sr[:, 2, 0, :], ACT.Sqrt).then_inc(B["rt3"], 1)
                act.wait_ge(B["rc3"], 2 * nL + 2)
                if later(nL, 2):
                    act.wait_ge(C["o"], 4 * nL - 4)
                for j in range(TG):
                    nc.scalar.activation(X3[par][:, j, :], U[:, j, :], ACT.Identity, scale=rs[:, 2, j:j + 1],
                                         bias=nb[:, 2, j:j + 1]).then_inc(B["x3"], 1)
            if has(s, "B"):
                if later(s, 2):
                    act.wait_ge(B["z"], 4 * s - 4)
                evac("b_f1", 0, f1T[0:32, :], parts=32, func=ACT.Relu, bias=colv[0:32, C_L2B1:C_L2B1 + 1])
            if has(s, "S"):
                act.wait_ge(C["sc"], nS + 1)
                nc.scalar.activation(sr[:, 3, 0, :], sr[:, 3, 0, :], ACT.Sqrt).then_inc(C["rt"], 1)
                act.wait_ge(C["rc"], 2 * nS + 2)
                for j in range(TG):
                    nc.scalar.activation(O[:, j, :], O[:, j, :], ACT.Identity, scale=rs[:, 3, j:j + 1],
                                         bias=nb[:, 3, j:j + 1]).then_inc(C["y"], 1)
            if has(s, "C"):
                if later(nC):
                    act.wait_ge(C["o"], 4 * nC)
                for k in range(KC):
                    if k:
                        evac("c_nd", k, ndT[:, k, :])
                    else:
                        evac("c_nd", k, ndT[:, k, :], bias=col(C_BND))
            if has(s, "A"):
                act.wait_ge(A["sc"], 4 * s + 4)
                nc.scalar.activation(sr[:, 0, :, :], sr[:, 0, :, :], ACT.Sqrt).then_inc(A["rt"], 1)
            sign_pass(1)
            sign_pass(2)

        def dve_stats(dve, S, bn, ag, z, n, q, src):
            for j in range(TG):
                dve.wait_ge(S[z], 4 * n + j + 1)
                nc.vector.bn_stats(st[:, q, j, :], src[:, j, :]).then_inc(S[bn], 1)
            dve.wait_ge(S[bn], 4 * n + 4)
            nc.vector.tensor_copy(n_even[:, q, :], st[:, q, 0, 0:1]).then_inc(S[ag], 1)
            for j in range(TG):
                nc.vector.bn_aggr(mv[:, q, j, :], st[:, q, j, :]).then_inc(S[ag], 1)
            dve.wait_ge(S[ag], 5 * n + 5)

        def dve_norm(dve, S, sc, rt, rc, n, q):
            nc.vector.tensor_scalar_add(sr[:, q, 0, :], mv[:, q, :, 1], EPS).then_inc(S[sc], 1)
            dve.wait_ge(S[rt], n + 1)
            nc.vector.reciprocal(rs[:, q, :], sr[:, q, 0, :]).then_inc(S[rc], 1)
            dve.wait_ge(S[rc], 2 * n + 1)
            nc.vector.scalar_tensor_tensor(nb[:, q, :], mv[:, q, :, 0], -1.0, rs[:, q, :], ALU.mult,
                                           ALU.mult).then_inc(S[rc], 1)

        def dve_step(dve, st_, s, par):
            nB, nL, nC, nS = (s - LAG[k] for k in "BLCS")

            def count_pass(q):
                if has(s, "A"):
                    dve.wait_ge(counts, 6 * s + q + 1)
                    mine, kind = divmod(q, 3)
                    me, acc = key_of(own_key, mine, s), key_of(cnt3, q, s)
                    if kind == 1:
                        nc.vector.scalar_tensor_tensor(
                            junk_v, keys_f[mine], me, earlier[:, bass.ds(E - s * P, E)], ALU.is_equal, ALU.mult,
                            accum_out=acc).then_inc(counts, 1)
                    else:
                        nc.vector.tensor_scalar(junk_v, keys_f[mine if kind == 0 else 1 - mine], me, None,
                                                ALU.is_lt, ALU.add, accum_out=acc).then_inc(counts, 1)

            def finish(S, sc, rt, rc, n, q):
                dve.wait_ge(S[rt], n + 1)
                nc.vector.reciprocal(rs[:, q, :], sr[:, q, 0, :]).then_inc(S[rc], 1)
                dve.wait_ge(S[rc], 2 * n + 1)
                nc.vector.scalar_tensor_tensor(nb[:, q, :], mv[:, q, :, 0], -1.0, rs[:, q, :], ALU.mult,
                                               ALU.mult).then_inc(S[rc], 1)

            if has(s, "C"):
                for k in range(3):
                    dve.wait_ge(NT_sb, st_.count("c_x", k + 2))
                    nc.vector.tensor_tensor(sq[:, k, :], x3T[:, k + 1, :], x3T[:, k + 1, :],
                                            ALU.mult).then_inc(C["sq"], 1)
            if has(s, "L"):
                finish(B, "sc", "rt", "rc", nL, 1)
            if has(s, "C"):
                for k in range(2):
                    dve.wait_ge(C["sq"], 3 * nC + 2 + k)
                    if k:
                        dve.wait_ge(C["sqs"], 2 * nC + 1)
                    nc.vector.tensor_tensor(sq[:, 0, :], sq[:, 0, :], sq[:, k + 1, :],
                                            ALU.add).then_inc(C["sqs"], 1)
            count_pass(0)
            count_pass(1)
            if has(s, "L"):
                for j in range(TG):
                    dve.wait_ge(B["ub"], 4 * nL + j + 1)
                    nc.vector.scalar_tensor_tensor(U[:, j, :], T[par][:, j, :], q2[par][:, j:j + 1], U[:, j, :],
                                                   ALU.mult, ALU.add).then_inc(B["z3"], 1)
                if later(nL):
                    dve.wait_ge(B["x3"], 4 * nL)
                dve_stats(dve, B, "bn3", "ag3", "z3", nL, 2, U)
                nc.vector.tensor_scalar_add(sr[:, 2, 0, :], mv[:, 2, :, 1], EPS).then_inc(B["sc3"], 1)
            count_pass(2)
            if has(s, "C"):
                dve.wait_ge(NT_sb, st_.count("c_g2", 2))
                for k in range(3):
                    nc.vector.tensor_tensor(xgT[:, k + 1, :], x3T[:, k + 1, :], gateT[:, :],
                                            ALU.mult).then_inc(C["xg"], 1)
            if has(s, "L"):
                finish(B, "sc3", "rt3", "rc3", nL, 2)
            count_pass(3)
            count_pass(4)

            def z_tiles(part, j0):
                for q in range(2):
                    j = j0 + q
                    dve.wait_ge(A["xb"], 4 * s + j + 1)
                    dve.wait_ge(NR_ps, st_.count(part, q + 1))
                    nc.vector.tensor_tensor(Z[:, j, :], Z[:, j, :], st_.bank(part, q)[0:P, :],
                                            ALU.add).then_inc(NR_sb, 1)
                for q in range(2):
                    dve.wait_ge(NR_sb, st_.count(part, q + 1))
                    nc.vector.bn_stats(st[:, 0, j0 + q, :], Z[:, j0 + q, :]).then_inc(A["bn"], 1)
            if has(s, "A"):
                z_tiles("a_o1", 0)
            if has(s, "S"):
                finish(C, "sc", "rt", "rc", nS, 3)
            count_pass(5)
            if has(s, "A"):
                z_tiles("a_o2", 2)
                if later(s):
                    dve.wait_ge(A["t"], 4 * s)
                dve.wait_ge(A["bn"], 4 * s + 4)
                nc.vector.tensor_copy(n_even[:, 0, :], st[:, 0, 0, 0:1]).then_inc(A["z"], 4)
                for j in range(TG):
                    i = nc.vector.bn_aggr(mv[:, 0, j, :], st[:, 0, j, :])
                i.then_inc(A["ag"], 1)
                dve.wait_ge(A["ag"], s + 1)
                var = mv[:, 0, :, 1]
                nc.vector.tensor_scalar(dd[:, 0, :], var, 4.0 + EPS, EPS * EPS, ALU.mult,
                                        ALU.add).then_inc(A["sc"], 1)
                dve.wait_ge(A["sc"], 4 * s + 1)
                nc.vector.scalar_tensor_tensor(sr[:, 0, 0, :], dd[:, 0, :], EPS / 4, var, ALU.mult,
                                               ALU.add).then_inc(A["sc"], 1)
                nc.vector.reciprocal(dd[:, 1, :], dd[:, 0, :]).then_inc(A["sc"], 1)
                dve.wait_ge(A["sc"], 4 * s + 3)
                nc.vector.scalar_tensor_tensor(sr[:, 0, 1, :], dd[:, 1, :], 4.0, sr[:, 0, 0, :], ALU.mult,
                                               ALU.mult).then_inc(A["sc"], 1)

            def last_stats(S, ring_part, n, q, src):
                for j in range(TG):
                    nc.vector.bn_stats(st[:, q, j, :], src[:, j, :]).then_inc(S["bn"], 1)
                dve.wait_ge(S["bn"], 4 * n + 4)
                i = nc.vector.tensor_copy(n_even[:, q, :], st[:, q, 0, 0:1])
                if S is B:
                    i.then_inc(B["z"], 4)
                for j in range(TG):
                    i = nc.vector.bn_aggr(mv[:, q, j, :], st[:, q, j, :])
                i.then_inc(S["ag"], 1)
                dve.wait_ge(S["ag"], n + 1)
                nc.vector.tensor_scalar_add(sr[:, q, 0, :], mv[:, q, :, 1], EPS).then_inc(S["sc"], 1)

            if has(s, "B"):
                for j in range(TG):
                    dve.wait_ge(B["tg"], 4 * nB + j + 1)
                    dve.wait_ge(NR_ps, st_.count("b_f", j + 1))
                    nc.vector.tensor_tensor(U[:, j, :], U[:, j, :], st_.bank("b_f", j)[0:P, :],
                                            ALU.add).then_inc(NR_sb, 1)
                if later(nB):
                    dve.wait_ge(B["u"], 4 * nB)
                dve.wait_ge(NR_sb, st_.count("b_f", 4))
                last_stats(B, "b_f", nB, 1, U)
            if has(s, "A"):
                dve.wait_ge(A["rt"], s + 1)
                nc.vector.reciprocal(rs[:, 0, :], sr[:, 0, 0, :]).then_inc(A["rc"], 1)
                nc.vector.tensor_copy(q2[par][:, :], sr[:, 0, 1, :]).then_inc(A["rc"], 1)
                dve.wait_ge(A["rc"], 3 * s + 1)
                nc.vector.scalar_tensor_tensor(nb[:, 0, :], mv[:, 0, :, 0], -1.0, rs[:, 0, :], ALU.mult,
                                               ALU.mult).then_inc(A["rc"], 1)
            if has(s, "C"):
                if later(nC):
                    dve.wait_ge(C["out"], 32 * nC)
                rows = X3[1 - par]
                for j in range(TG):
                    dve.wait_ge(NR_ps, st_.count("c_o", j + 1))
                    b = st_.bank("c_o", j)
                    nc.vector.scalar_tensor_tensor(vec3(O[:, j, 128:D]), vec3(rows[:, j, 128:D]), 2.0,
                                                   b[0:P, 128:D].rearrange("p (c u) -> p c u", c=3),
                                                   ALU.mult, ALU.add)
                    nc.vector.scalar_tensor_tensor(O[:, j, 0:128], rows[:, j, 0:128], 2.0, b[0:P, 0:128],
                                                   ALU.mult, ALU.add).then_inc(NR_sb, 1)
                dve.wait_ge(NR_sb, st_.count("c_o", 4))
                nc.vector.tensor_tensor(O[:, :, 0:128], O[:, :, 0:128], spread(row(R_L3, 128), TG),
                                        ALU.add).then_inc(C["o"], 4)
            if has(s, "C"):
                dve.wait_ge(C["o"], 4 * nC + 4)
                last_stats(C, "c_o", nC, 3, O)

        def pool_step(pool, st_, s, par):
            nB, nL = s - LAG["B"], s - LAG["L"]
            if has(s, "A"):
                pool.wait_ge(A[f"x_in{par}"], 16 * s + (32 - 16 * par))
                if later(s):
                    pool.wait_ge(A["t"], 4 * s)
                for j in range(TG):
                    nc.gpsimd.tensor_tensor(Z[:, j, :], X[par][:, j, :], row(R_L0B2), ALU.add).then_inc(A["xb"], 1)
            if has(s, "L"):
                for j in range(TG):
                    pool.wait_ge(B["u"], 4 * nL + j + 1)
                    nc.gpsimd.tensor_tensor(U[:, j, :], U[:, j, :], row(R_LN2G), ALU.mult).then_inc(B["ug"], 1)
                for j in range(TG):
                    pool.wait_ge(B["ug"], 4 * nL + j + 1)
                    nc.gpsimd.tensor_tensor(U[:, j, :], U[:, j, :], row(R_LN2B), ALU.add).then_inc(B["ub"], 1)
            if has(s, "B"):
                if later(nB):
                    pool.wait_ge(B["x3"], 4 * nB)
                for j in range(TG):
                    pool.wait_ge(A["t"], 4 * nB + j + 1)
                    nc.gpsimd.tensor_tensor(U[:, j, :], T[1 - par][:, j, :], row(R_LN1G),
                                            ALU.mult).then_inc(B["tg"], 1)

        Sx, Ml, Bd, RD = sb("Sd", [P + 2, ET, P]), sb("Md", [P, ET, P]), sb("Bd", [P, NB * ET]), \
            sb("RD", [P, ET, Q_END])
        Sd, Md = Sx[0:P, :, :], Ml[0:NB, :, :]
        keys_f = [m[:, :, :].rearrange("p t f -> p (t f)") for m in (Sd, Ml)]
        junk_v = Bd[:, :].bitcast(mybir.dt.uint8)[:, 0:E]
        junk_s = RD[:, :, :].rearrange("p t q -> p (t q)").bitcast(mybir.dt.int8)[:, 0:E]
        neg_rdy, keys_in = sem("own_keys"), sem("keys_in")

        counts, signs = sem("counts"), sem("signs")
        kfc, neg_key = sb("kfc", [P, 2 * ET]), sb("neg_key", [P, 2 * ET])
        cnt3, sgn = sb("cnt3", [P, 6 * ET]), sb("sgn", [P, 3 * ET])
        own_key = kfc
        earlier = at(37028, [1250], P).bitcast(mybir.dt.uint8)

        def key_of(t_, q, s):
            if isinstance(s, int):
                return t_[:, q * ET + s:q * ET + s + 1]
            return t_[:, bass.ds(s + q * ET, 1)]

        T_ps, T_sb, R_ps, R_sb, B_ps, B_sb = (sem(k) for k in "T_ps T_sb R_ps R_sb B_ps B_sb".split())
        dstep, astep = sem("vector_step"), sem("scalar_step")
        L_sc, L_rt, L_y = sem("norm_variance"), sem("norm_root"), sem("norm_rows")
        phase_end = sem("phase_end")
        rec_done, rec_put, rec_back = (sem(k) for k in "rec_done rec_put rec_back".split())

        rows_in = {q: [sem(f"rows_in_{q}{g}") for g in range(EG)] for q in ("gather_a", "gather_b", "load")}

        class Arrival:
            def __init__(self, s, base):
                self.s, self.base = s, base

            def full(self, n):
                return self.s, n + self.base

        def per_group(q, base):
            return [Arrival(s, base) for s in rows_in[{"a": "gather_a", "b": "gather_b", "h": "load"}[q]]]

        Hd, X1d, X2d, X3d = (nc.dram_tensor(f"{n}_table", (2 * E, D), F32).ap() for n in ("h", "x1", "x2", "x3"))
        Yd = nc.dram_tensor("y_table", (E, D), F32).ap()
        PDd = nc.dram_tensor("part_rows", (E, D), F32).ap()
        RDd = nc.dram_tensor("records_by_dst", (E, Q_END), F32).ap()
        RSd = nc.dram_tensor("records_by_src", (E, Q_END), F32).ap()

        class Counts:
            def __init__(self):
                self.t = self.r = self.b = self.ln = self.y = self.d = self.a = self.ph = 0

        def end_phase(eng, c):
            eng.drain().then_inc(phase_end, 1)
            c.ph += 1
            eng.wait_ge(phase_end, 4 * c.ph)

        def gcols(ap2, g):
            return ap2[:, g * TG:(g + 1) * TG]

        spare = Ml[:, :, :].rearrange("p t f -> p (t f)")
        rec = spare[:, 0:ET * Q_END].rearrange("p (t q) -> p t q", q=Q_END)
        cnts, own = (spare[:, 1000 + 200 * k:1000 + 200 * k + n * ET].rearrange("p (a t) -> p a t", t=ET)
                     for k, n in enumerate((1, 6)))
        rank_i = spare[:, 1400:1400 + 2 * ET].bitcast(I32).rearrange("p (a t) -> p a t", t=ET)
        RSs = sb("RSs", [P, ET, 3])
        bk = sb("bk", [NB, 2])
        bkm = sb("bkm", [NB, 2, ET])
        mask = sb("mask", [NB, ET])
        idd = sb("idd", [P, 7, ET], I32)
        ids = sb("ids", [P, 3, ET], I32)
        abv = sb("abv", [P, 3])
        ck, many = sb("boundary_keys", [P, 2, NB]), sb("many_segments", [P, 2, ET])
        v20 = sb("v20", [P, 12, ET])
        lst = sb("lst", [P, TG, 6])
        lmv = sb("lmv", [P, TG, 2])
        lsr = sb("lsr", [P, TG])
        lrs = sb("lrs", [P, TG])
        s_end = sem("edge_constants")

        def t_open(pe, c):
            if c.t >= 4:
                pe.wait_ge(T_sb, c.t - 3)
            c.t += 1
            return bank[(c.t - 1) % 4]

        def r_open(pe, c):
            if c.r >= 2:
                pe.wait_ge(R_sb, c.r - 1)
            c.r += 1
            return bank[4 + (c.r - 1) % 2]

        def b_open(pe, c):
            if c.b:
                pe.wait_ge(B_sb, c.b)
            c.b += 1
            return bank[7]

        def pe_transpose_rows(pe, c, rows4, interleaved=False):
            for k in range(KC):
                b = t_open(pe, c)
                for j in range(TG):
                    if interleaved and k:
                        src = vec3(rows4[:, j, 128:D])[:, k - 1, :]
                    else:
                        src = rows4[:, j, k * 128:(k + 1) * 128]
                    i = nc.tensor.transpose(b[:, j * P:(j + 1) * P], src, ident[0:P, 0:P])
                i.then_inc(T_ps, 1)

        def pe_transpose_back(pe, c, fT):
            for j in range(TG):
                b = r_open(pe, c)
                for k in range(KC):
                    i = nc.tensor.transpose(b[0:P, k * 128:(k + 1) * 128], fT[:, k, j * P:(j + 1) * P],
                                            ident[:, :])
                i.then_inc(R_ps, 1)

        def pe_boundaries(pe, c, B, V, n, ready=None):
            b = b_open(pe, c)
            for t in range(ET):
                if ready is not None and t % TG == 0:
                    pe.wait_ge(*ready(t // TG))
                i = nc.tensor.matmul(b[0:NB, 0:n], B[:, t * NB:(t + 1) * NB], V(t), start=t == 0,
                                     stop=t == ET - 1)
            i.then_inc(B_ps, 1)

        def pe_segment_T(pe, c, b, S, V, g, k, fresh):
            for j in range(TG):
                t = TG * g + j
                i = nc.tensor.matmul(b[:, j * P:(j + 1) * P], V[:, t, k * 128:(k + 1) * 128], S[:, t, :],
                                     start=fresh and j == 0, stop=j == TG - 1)
            return i

        def pe_segment_narrow(pe, c, S, M, V, bf, n):
            b = r_open(pe, c)
            for t in range(ET):
                nc.tensor.matmul(b[0:P, t * n:(t + 1) * n], S[:, t, :], V(t), start=t == 0, stop=False)
                i = nc.tensor.matmul(b[0:P, t * n:(t + 1) * n], M[:, t, :], bf[0:NB, 0:n], start=False,
                                     stop=t == ET - 1)
            i.then_inc(R_ps, 1)

        def pe_rows_out(pe, c, pairs, n=D):
            for j in range(TG):
                b = r_open(pe, c)
                last = len(pairs) * KC - 1
                for q, (fT, W) in enumerate(pairs):
                    for k in range(KC):
                        i = nc.tensor.matmul(b[0:P, 0:n], fT[:, k, j * P:(j + 1) * P], W[:, k, :],
                                             start=q * KC + k == 0, stop=q * KC + k == last)
                i.then_inc(R_ps, 1)

        def act_evac(act, c, dst, src_rows=128, n=GR, func=ACT.Identity, **kw):
            act.wait_ge(T_ps, c.t + 1)
            c.t += 1
            nc.scalar.activation(dst, bank[(c.t - 1) % 4][0:src_rows, 0:n], func, **kw).then_inc(T_sb, 1)

        def act_root(act, c):
            act.wait_ge(L_sc, c.ln + 1)
            c.ln += 1
            nc.scalar.activation(lsr[:, :], lsr[:, :], ACT.Sqrt).then_inc(L_rt, 1)

        def link(dve, c, ins):
            ins.then_inc(dstep, 1)
            c.d += 1
            dve.wait_ge(dstep, c.d)

        def dve_evac(dve, c, f):
            dve.wait_ge(R_ps, c.r + 1)
            c.r += 1
            f(bank[4 + (c.r - 1) % 2]).then_inc(R_sb, 1)

        def dve_b_evac(dve, c, dst, n):
            dve.wait_ge(B_ps, c.b + 1)
            c.b += 1
            nc.vector.tensor_copy(dst, bank[7][0:NB, 0:n]).then_inc(B_sb, 1)

        def dve_ln_root(dve, c, rows4, doubled=False):
            for j in range(TG):
                i = nc.vector.bn_stats(lst[:, j, :], rows4[:, j, :])
            link(dve, c, i)
            for j in range(TG):
                i = nc.vector.bn_aggr(lmv[:, j, :], lst[:, j, :])
            link(dve, c, i)
            nc.vector.tensor_scalar(lsr[:, :], lmv[:, :, 1], 4.0 if doubled else 1.0, EPS, ALU.mult,
                                    ALU.add).then_inc(L_sc, 1)
            c.ln += 1

        def dve_ln_rows(dve, c, rows4, doubled=False):
            dve.wait_ge(L_rt, c.ln)
            link(dve, c, nc.vector.reciprocal(lrs[:, :], lsr[:, :]))
            if doubled:
                link(dve, c, nc.vector.tensor_scalar_mul(lrs[:, :], lrs[:, :], 2.0))
            for j in range(TG):
                nc.vector.tensor_scalar(rows4[:, j, :], rows4[:, j, :], lmv[:, j, 0:1], lrs[:, j:j + 1],
                                        ALU.subtract, ALU.mult).then_inc(L_y, 1)
            c.y += TG
            dve.wait_ge(L_y, c.y)

        def dve_ln(dve, c, rows4, doubled=False):
            dve_ln_root(dve, c, rows4, doubled)
            dve_ln_rows(dve, c, rows4, doubled)

        def gather(dst, table, idx, s, limit=None):
            nc.gpsimd.indirect_dma_start(out=dst, out_offset=None, in_=table,
                                         in_offset=bass.IndirectOffsetOnAxis(ap=idx, axis=0),
                                         bounds_check=limit, oob_is_err=limit is None).then_inc(s.s, 16)

        def store(sp, table, base, g, rows4, s):
            dst = grp(table[base:base + E, :], g)
            sp.dma_start(dst[0:HI], rows4[0:HI]).then_inc(s, 16)
            sp.dma_start(dst[HI:P], rows4[HI:P]).then_inc(s, 16)

        def load(sp, rows4, table, base, g, s):
            src = grp(table[base:base + E, :], g)
            sp.dma_start(rows4[0:HI], src[0:HI]).then_inc(s.s, 16)
            sp.dma_start(rows4[HI:P], src[HI:P]).then_inc(s.s, 16)

        def scatter(table, idx, src, s, limit=N - 1):
            nc.gpsimd.indirect_dma_start(out=table, out_offset=bass.IndirectOffsetOnAxis(ap=idx, axis=0),
                                         in_=src, in_offset=None, bounds_check=limit,
                                         oob_is_err=False).then_inc(s, 16)

        diag = at(AR - ET * P, [ET, P], P)
        ones = sb("ones", [P, P])

        def sp_records(sp):
            sp.wait_ge(counts, 6 * ET + 1)
            sp.wait_ge(signs, 3 * ET)
            sp.dma_start(rec[:, :, :], rec_in.rearrange("(t p) q -> p t q", p=P)).then_inc(keys_in, 16)
            sp.dma_start(mask[:, :], mask_in).then_inc(keys_in, 16)
            sp.dma_start(abv[:, :], abs_in[0].partition_broadcast(P)).then_inc(keys_in, 16)

        def sp_records_back(sp):
            sp.wait_ge(rec_put, 16 * 2 * ET)
            dv = RDd.rearrange("(t p) q -> p t q", p=P)
            sv = RSd.rearrange("(t p) q -> p t q", p=P)
            sp.dma_start(RD[:, :, :], dv).then_inc(rec_back, 16)
            sp.dma_start(rec[:, :, :], sv).then_inc(rec_back, 16)
            with nc.allow_non_contiguous_dma(reason="one key of each boundary record"):
                for q, (v, col) in enumerate(((dv, Q_DST), (sv, Q_SRC))):
                    sp.dma_start(bk[0:ET, q:q + 1], v[0, :, col:col + 1]).then_inc(rec_back, 16)
                    sp.dma_start(bk[ET:NB, q:q + 1], v[P - 1, :, col:col + 1]).then_inc(rec_back, 16)

        def dve_records(dve, c):
            dve.wait_ge(keys_in, 16 * 7)
            dve.wait_ge(counts, 6 * ET + 1)
            dve.wait_ge(signs, 3 * ET)
            by = cnt3[:, :].rearrange("p (q a t) -> p q a t", q=2, a=3)
            sg = sgn[:, :].rearrange("p (q t) -> p q t", q=3)
            for k, (q, a, dst) in enumerate(((0, 0, cnts[:, 0, :]), (1, 2, own[:, 1, :]), (0, 2, own[:, 0, :]))):
                link(dve, c, nc.vector.scalar_tensor_tensor(dst, by[:, q, a, :], 2.0, sg[:, k, :], ALU.mult,
                                                            ALU.add))
                link(dve, c, nc.vector.tensor_scalar(dst, dst, -1.0, float(E), ALU.mult, ALU.add))
            dup = v20[:, 0:2, :]
            link(dve, c, nc.vector.tensor_copy(dup, by[:, :, 1, :]))
            link(dve, c, nc.vector.tensor_tensor(v20[:, 2:4, :], by[:, :, 0, :], dup, ALU.add))
            link(dve, c, nc.vector.tensor_copy(rank_i[:, :, :], v20[:, 2:4, :]))
            link(dve, c, nc.vector.tensor_scalar_min(own[:, 0:2, :], own[:, 0:2, :], 1.0))
            link(dve, c, nc.vector.tensor_scalar_add(own[:, 2, :], v20[:, 2, :], float(E)))
            link(dve, c, nc.vector.tensor_tensor(own[:, 3, :], by[:, 0, 2, :], own[:, 2, :], ALU.subtract))
            link(dve, c, nc.vector.tensor_tensor(own[:, 3, :], own[:, 3, :], own[:, 0, :], ALU.mult))
            link(dve, c, nc.vector.tensor_tensor(own[:, 3, :], own[:, 3, :], own[:, 2, :], ALU.add))
            link(dve, c, nc.vector.scalar_tensor_tensor(own[:, 4, :], by[:, 1, 2, :], float(E), v20[:, 2, :],
                                                        ALU.add, ALU.subtract))
            link(dve, c, nc.vector.tensor_tensor(own[:, 4, :], own[:, 4, :], own[:, 1, :], ALU.mult))
            link(dve, c, nc.vector.tensor_tensor(own[:, 4, :], own[:, 4, :], v20[:, 2, :], ALU.add))
            link(dve, c, nc.vector.tensor_scalar(own[:, 5, :], own[:, 0, :], -float(FAR), float(FAR), ALU.mult,
                                                 ALU.add))
            link(dve, c, nc.vector.tensor_tensor(own[:, 5, :], own[:, 5, :], by[:, 0, 2, :], ALU.add))
            link(dve, c, nc.vector.tensor_scalar(v20[:, 4:6, :], dup, 1.0, float(FAR), ALU.min, ALU.mult))
            link(dve, c, nc.vector.tensor_tensor(v20[:, 6:8, :], v20[:, 4:6, :],
                                                 kfc[:, :].rearrange("p (q t) -> p q t", q=2), ALU.add))
            for col, src in ((Q_DST, kfc[:, 0:ET]), (Q_SRC, kfc[:, ET:2 * ET]), (Q_DSC, v20[:, 6, :]),
                             (Q_SSC, v20[:, 7, :]), (Q_DUP, v20[:, 0, :]), (Q_RS, v20[:, 3, :]),
                             (Q_XD, own[:, 2, :]), (Q_DI, own[:, 3, :]), (Q_SI, own[:, 4, :]),
                             (Q_YI, own[:, 5, :])):
                nc.vector.tensor_copy(rec[:, :, col], src)
            nc.vector.tensor_copy(rec[:, :, Q_CNT], cnts[:, 0, :]).then_inc(rec_done, 1)

        def dve_records_back(dve, c):
            dve.wait_ge(rec_back, 16 * 6)
            for k, col in enumerate((Q_DST, Q_SRC, Q_DSC, Q_SSC, Q_SI, Q_DI, Q_RS)):
                nc.vector.tensor_copy(idd[:, k, :], RD[:, :, col])
            for k, col in enumerate((Q_XD, Q_SI, Q_YI)):
                nc.vector.tensor_copy(ids[:, k, :], rec[:, :, col])
            for k, col in enumerate((Q_DST, Q_SRC, Q_W)):
                i = nc.vector.tensor_copy(RSs[:, :, k], rec[:, :, col])
            i.then_inc(rec_done, 1)
            nc.vector.memset(ones[:, :], 1.0)
            nc.vector.tensor_scalar_add(bk[:, :], bk[:, :], 1.0)
            link(dve, c, nc.vector.memset(Bd[:, :], 0.0))
            for q in range(2):
                i = nc.vector.tensor_scalar(bkm[:, q, :], mask[:, :], bk[:, q:q + 1], None, ALU.mult)
            link(dve, c, i)
            link(dve, c, nc.vector.tensor_scalar_add(bkm[:, :, :], bkm[:, :, :], -1.0))

        def dve_build(dve, c, q, key, S, M, dg):
            dve.wait_ge(dstep, c.d)
            nc.vector.tensor_tensor(dg[:, :, :], spread(ident[0:P, 0:P], ET), b3(key, P), ALU.mult).then_inc(s_end, 1)
            for g in range(EG):
                kt = gcols(key, g)
                dve.wait_ge(R_ps, c.r + 1)
                b = bank[4 + c.r % 2]
                c.r += 1
                row = b[0:P, 0:GR].rearrange("p (t f) -> p t f", f=P)
                nc.vector.tensor_tensor(S[0:P, g * TG:(g + 1) * TG, :], row, b3(kt, P), ALU.is_equal)
                nc.vector.tensor_copy(gcols(ck[:, q, 0:ET], g), row[:, :, 0])
                nc.vector.tensor_copy(gcols(ck[:, q, ET:NB], g), row[:, :, P - 1])
                nc.vector.tensor_tensor(M[:, g * TG:(g + 1) * TG, :],
                                        b[0:NB, 0:GR].rearrange("p (t f) -> p t f", f=P),
                                        b3(gcols(bkm[:, q, :], g), P), ALU.is_equal).then_inc(R_sb, 1)
            dve.wait_ge(R_sb, c.r)
            link(dve, c, nc.vector.tensor_tensor(many[:, q, :], ck[:, q, 0:ET], ck[:, q, ET:NB], ALU.not_equal))

        def dve_boundary_weights(dve, c, B, q, key, w, done):
            B3 = B.rearrange("p (t b) -> p t b", b=NB)
            link(dve, c, nc.vector.tensor_tensor(B3, b3(key, NB), spread(ck[:, q, :], ET), ALU.is_equal))
            if w is not None:
                link(dve, c, nc.vector.tensor_tensor(B3, B3, b3(w, NB), ALU.mult))
            link(dve, c, nc.vector.tensor_tensor(B3[:, :, ET:NB], B3[:, :, ET:NB], spread(many[:, q, :], ET),
                                                 ALU.mult))
            nc.vector.memset(B[:, 0:(ET - 1) * (NB + 1) + 1:NB + 1], 0.0)
            nc.vector.memset(B[:, ET:ET + (ET - 1) * (NB + 1) + 1:NB + 1], 0.0).then_inc(done, 1)

        def pe_build(pe, c, dg, n):
            pe.wait_ge(s_end, n)
            for g in range(EG):
                b = r_open(pe, c)
                nc.tensor.matmul(b[0:P, 0:GR], ones[:, :], dg[:, g * TG:(g + 1) * TG, :].rearrange("p t f -> p (t f)"),
                                 start=True, stop=True).then_inc(R_ps, 1)

        def dve_boundary_cols(dve, c, B, S, done):
            nc.vector.tensor_copy(B[:, 0:(ET - 1) * (NB + 1) + 1:NB + 1], S[0:P, :, 0])
            nc.vector.tensor_copy(B[:, ET:ET + (ET - 1) * (NB + 1) + 1:NB + 1], S[0:P, :, P - 1]).then_inc(done, 1)

        def pool_records(pool):
            pool.wait_ge(rec_done, 1)
            for q, table in enumerate((RDd, RSd)):
                for t in range(ET):
                    scatter(table, rank_i[:, q, t:t + 1], rec[:, t, :], rec_put, E - 1)

        W1l, W2l = at(4096, [KC, D]), at(6144, [KC, D])
        V0x, SNx = at(8192, [ET, D], P + 2), at(18432, [ET, P], P + 2)
        V0, SN = V0x[0:P], SNx[0:P]
        BN = at(20932, [NB * ET], P)
        BF0 = at(21732, [D], NB)
        XD0 = [at(22244, [TG, D], P), at(24292, [TG, D], P)]
        ZZ0 = at(26340, [TG, D], P)
        HR0 = at(28388, [TG, D], P)
        XT0, HT0, AT0 = at(30436, [KC, GR]), at(32436, [KC, GR]), at(34436, [KC, GR])
        w0_in = sem("layer0_weights_in")
        e0_x, e0_xd, e0_h, e0_pd = per_group("a", 0), per_group("b", 0), per_group("a", 64), per_group("h", 0)
        h_put, x1_put, pd_put, bn0 = sem("h_put"), sem("x1_put"), sem("pd_put"), sem("mean_weights")
        pd_sem = sem("part_rows_ready")

        def grp(dram, g):
            return dram[g * GR:(g + 1) * GR, :].rearrange("(t p) d -> p t d", p=P)

        s_ext, v_ext = sem("segment_ends_in"), sem("other_tiles_in")

        def sp_segment_ends(sp, dst, S):
            sp.dma_start(dst[P:P + 1, :, :], S[0:1, :, :]).then_inc(s_ext, 16)
            sp.dma_start(dst[P + 1:P + 2, :, :], S[P - 1:P, :, :]).then_inc(s_ext, 16)

        def sp_ext(sp, V, bf, n_b):
            sp.wait_ge(B_sb, n_b)
            sp.dma_start(V[P:P + 1, :, :], bf[0:ET, :]).then_inc(v_ext, 16)
            sp.dma_start(V[P + 1:P + 2, :, :], bf[ET:NB, :]).then_inc(v_ext, 16)

        def sp_L0(sp, c):
            sp.wait_ge(phase_end, 4 * c.ph)
            for dst, src in ((W1l, w_l1), (W2l, w_l2)):
                sp.dma_start(dst, src).then_inc(w0_in, 16)
            sp.wait_ge(bn0, 1)
            for dst in (Sx, SNx):
                sp_segment_ends(sp, dst, Sd)
            for g in range(EG):
                c.r += TG
                sp.wait_ge(R_sb, c.r)
                store(sp, Hd, 0, g, HR0, h_put)
                c.r += TG
                c.y += TG
                sp.wait_ge(L_y, c.y)
                store(sp, X1d, 0, g, ZZ0, x1_put)
            sp_ext(sp, V0x, BF0, 1)
            for g in range(EG):
                c.r += TG
                sp.wait_ge(R_sb, c.r)
                store(sp, Hd, E, g, HR0, h_put)
                c.r += TG
                sp.wait_ge(pd_sem, g + 1)
                store(sp, PDd, 0, g, ZZ0, pd_put)
            sp.wait_ge(pd_put, 32 * EG)
            for g in range(2):
                sp.wait_ge(R_sb, c.r)
                load(sp, XD0[g], PDd, 0, g, e0_pd[g])
            sp_ext(sp, V0x, BF0, 2)
            for g in range(EG):
                c.r += TG
                c.y += TG
                sp.wait_ge(L_y, c.y)
                store(sp, X1d, E, g, ZZ0, x1_put)
                if g + 2 < EG:
                    load(sp, XD0[g % 2], PDd, 0, g + 2, e0_pd[g + 2])
            sp.wait_ge(x1_put, 2 * 32 * EG)

        def sp_L1(sp, c):
            sp.wait_ge(w1_rdy, 1)
            sp_segment_ends(sp, Ss, Ss)
            for g in range(EG):
                load(sp, CR[:, g * TG:(g + 1) * TG, :], X1d, E, g, e1_b[g])
            for g in range(EG):
                c.y += TG
                sp.wait_ge(L_y, c.y)
                store(sp, X2d, E, g, CR[:, g * TG:(g + 1) * TG, :], x2_put)
            sp_ext(sp, V1, BF1, B1_0)
            c.r += EG + 1 + ET

            def step(i):
                for g in range(EG):
                    if isinstance(i, int) and i == 1:
                        sp.wait_ge(y_rdy, TG * (g + 1))
                    else:
                        sp.wait_ge(R_sb, i * ET + (c.r - 2 * ET + TG * (g + 1)))
                    store(sp, Yd, 0, g, Y[:, g * TG:(g + 1) * TG, :], y_put)
                sp_ext(sp, V1, BF1, i + B1_0)
            step(1)
            with sp.Fori(2, ITERS) as i:
                step(i)
            c.r += ET * (ITERS - 1)
            sp.wait_ge(R_sb, c.r)
            for dst, src in ((WQ, w_q), (WK, w_k), (WV, w_v), (WO, w_o)):
                sp.dma_start(dst, src).then_inc(w2_in, 16)
            for g in range(EG):
                c.y += TG
                sp.wait_ge(L_y, c.y)
                store(sp, X2d, 0, g, Y[:, g * TG:(g + 1) * TG, :], x2_put)
            sp.wait_ge(x2_put, 2 * 32 * EG)

        def pool_L0(pool, c):
            for t in range(ET):
                gather(V0[:, t, :], x, idd[:, 1, t:t + 1], e0_x[t // TG])
            for g in range(2):
                for j in range(TG):
                    gather(XD0[g][:, j, :], x, idd[:, 0, TG * g + j:TG * g + j + 1], e0_xd[g])
            c.r += 2 * TG * EG
            for g in range(EG):
                if g >= 2:
                    pool.wait_ge(R_sb, c.r - TG * 2)
                    for j in range(TG):
                        gather(XD0[g % 2][:, j, :], x, idd[:, 0, TG * g + j:TG * g + j + 1], e0_xd[g])
                c.r += 2 * TG
            pool.wait_ge(h_put, 2 * 32 * EG)
            pool.wait_ge(T_sb, c.t + 8 * EG + 12 * EG)
            for t in range(ET):
                gather(V0[:, t, :], Hd, idd[:, 4, t:t + 1], e0_h[t // TG])
            c.r += TG * EG
            c.t += 8 * EG + 12 * EG + 4 * EG
            c.y += 2 * TG * EG
            pool.wait_ge(x1_put, 2 * 32 * EG)

        def pe_L0(pe, c):
            for g in range(EG):
                pe.wait_ge(*e0_x[g].full(16 * TG))
                pe_transpose_rows(pe, c, V0[:, g * TG:(g + 1) * TG, :])
                pe.wait_ge(T_sb, c.t)
                for m in range(KC):
                    b = t_open(pe, c)
                    for k in range(KC):
                        i = nc.tensor.matmul(b[:, 0:GR], W1r[:, k, m * 128:(m + 1) * 128], XT0[:, k, :],
                                             start=k == 0, stop=k == KC - 1)
                    i.then_inc(T_ps, 1)
                pe.wait_ge(T_sb, c.t)
                pe_transpose_back(pe, c, HT0)
                pe_rows_out(pe, c, [(HT0, W2r)])
            pe.wait_ge(w0_in, 16 * 2)
            pe.wait_ge(bn0, 1)
            pe.wait_ge(s_ext, 64)
            pe_boundaries(pe, c, BN, lambda t: V0[:, t, :], D)
            for g in range(EG):
                pe.wait_ge(*e0_xd[g].full(16 * TG))
                pe_transpose_rows(pe, c, XD0[g % 2])
                pe.wait_ge(v_ext, 32)
                for k in range(KC):
                    b = t_open(pe, c)
                    pe_segment_T(pe, c, b, SNx, V0x, g, k, True).then_inc(T_ps, 1)
                pe.wait_ge(T_sb, c.t)
                for m in range(KC):
                    b = t_open(pe, c)
                    for q, (fT, W) in enumerate(((XT0, W1r), (AT0, W1l))):
                        for k in range(KC):
                            i = nc.tensor.matmul(b[:, 0:GR], W[:, k, m * 128:(m + 1) * 128], fT[:, k, :],
                                                 start=q + k == 0, stop=q == 1 and k == KC - 1)
                    i.then_inc(T_ps, 1)
                pe.wait_ge(T_sb, c.t)
                pe_transpose_back(pe, c, HT0)
                pe_rows_out(pe, c, [(HT0, W2r)])
            pe_boundaries(pe, c, BN, lambda t: V0[:, t, :], D, lambda g: e0_h[g].full(16 * TG))
            pe.wait_ge(v_ext, 64)
            for g in range(EG):
                for k in range(KC):
                    b = t_open(pe, c)
                    pe_segment_T(pe, c, b, SNx, V0x, g, k, True).then_inc(T_ps, 1)
                pe.wait_ge(T_sb, c.t)
                pe_rows_out(pe, c, [(AT0, W2l)])

        def act_L0(act, c):
            for loop in range(2):
                for g in range(EG):
                    for k in range(KC):
                        act_evac(act, c, XT0[:, k, :])
                    if loop == 1:
                        for k in range(KC):
                            act_evac(act, c, AT0[:, k, :])
                    if g and loop == 0:
                        act_root(act, c)
                    if g or loop:
                        act.wait_ge(R_ps, c.r)
                    for m in range(KC):
                        act_evac(act, c, HT0[:, m, :], func=ACT.Relu, bias=colv[:, C_L0B1 + m:C_L0B1 + m + 1])
                    if loop == 0 and g == EG - 1:
                        act_root(act, c)
                    c.r += 2 * TG
            for g in range(EG):
                act.wait_ge(R_ps, c.r)
                for k in range(KC):
                    act_evac(act, c, AT0[:, k, :])
                act_root(act, c)
                c.r += TG

        def dve_L0(dve, c):
            link(dve, c, nc.vector.reciprocal(v20[:, 8, :], RD[:, :, Q_CNT]))
            link(dve, c, nc.vector.tensor_tensor(SN[:, :, :], Sd[:, :, :], b3(v20[:, 8, :], P), ALU.mult))
            dve_boundary_weights(dve, c, BN, 0, RD[:, :, Q_DST], v20[:, 8, :], bn0)
            dve.wait_ge(bn0, 1)
            b2row = spread(row(R_L0B2), TG)
            for loop in range(2):
                for g in range(EG):
                    res = V0[:, g * TG:(g + 1) * TG, :] if loop == 0 else XD0[g % 2]
                    if loop == 0:
                        dve.wait_ge(*e0_x[g].full(16 * TG))
                    else:
                        dve.wait_ge(*e0_xd[g].full(16 * TG))
                    if loop or g:
                        dve.wait_ge(h_put, 32 * (EG * loop + g))
                    for j in range(TG):
                        dve_evac(dve, c, lambda b: nc.vector.tensor_copy(HR0[:, j, :], b[0:P, :]))
                    if loop == 0 and g:
                        dve.wait_ge(x1_put, 32 * g)
                    if loop == 1:
                        dve.wait_ge(x1_put, 32 * EG)
                        if g:
                            dve.wait_ge(pd_put, 32 * g)
                    for j in range(TG):
                        dve_evac(dve, c, lambda b: nc.vector.tensor_tensor(ZZ0[:, j, :], res[:, j, :],
                                                                           b[0:P, :], ALU.add))
                    dve.wait_ge(R_sb, c.r)
                    i = nc.vector.tensor_tensor(ZZ0, ZZ0, b2row, ALU.add)
                    if loop == 1:
                        i.then_inc(pd_sem, 1)
                    else:
                        link(dve, c, i)
                        dve_ln(dve, c, ZZ0)
                dve_b_evac(dve, c, BF0, D)
            dve.wait_ge(pd_put, 32 * EG)
            for g in range(EG):
                dve.wait_ge(*e0_pd[g].full(32))
                if g:
                    dve.wait_ge(x1_put, 32 * (EG + g))
                for j in range(TG):
                    dve_evac(dve, c, lambda b: nc.vector.tensor_tensor(ZZ0[:, j, :], XD0[g % 2][:, j, :],
                                                                       b[0:P, :], ALU.add))
                dve.wait_ge(R_sb, c.r)
                dve_ln(dve, c, ZZ0)

        Ss, Ms = at(0, [ET, P], P + 2), at(2500, [ET, P], NB)
        BW = at(5000, [NB * ET], P)
        BF1 = at(5800, [D], NB)
        V1, Y, CR = at(6312, [ET, D], P + 2), at(16552, [ET, D], P), at(26792, [ET, D], P)
        J1 = at(37032, [2, D], P)
        diag1 = at(16552, [ET, P], P)
        e1_b, e1_v, e1_x, e1_y, e1_f = (per_group(*q) for q in (
            ("h", 32), ("a", 128), ("b", 64), ("a", 192), ("b", 128)))
        x2_put, y_put = sem("x2_put"), sem("y_put")
        sc1, sc1a = sem("layer1_scalars"), sem("layer1_scalars_act")
        sup_rdy, w1_rdy, zr, y_rdy = sem("sup_ready"), sem("weights1_ready"), sem("zero_rows"), sem("y_ready")
        pre = sem("y_before_sums")
        B1_0 = 2 + 2
        SUP, NN, RR, NRR, SD, SSQ, DSQ, TMP = (v20[:, k, :] for k in range(8))

        EARLY = 3

        def pool_L1(pool, c):
            for g in range(EG):
                for j in range(TG):
                    gather(V1[0:P, TG * g + j, :], X1d, ids[:, 0, TG * g + j:TG * g + j + 1], e1_v[g])
                if g == 0:
                    pool.wait_ge(R_sb, c.r + EG)
                for j in range(TG):
                    gather(Y[:, TG * g + j, :], X1d, ids[:, 1, TG * g + j:TG * g + j + 1], e1_x[g])
            c.r += EG + 1 + ET
            c.y += ET
            pool.wait_ge(zr, 1)
            for i in range(1, ITERS):
                pool.wait_ge(y_put, i * (32 * EG))
                pool.wait_ge(R_sb, i * ET + (c.r - ET))
                for t in range(ET):
                    gather(V1[0:P, t, :], Yd, ids[:, 2, t:t + 1], e1_y[t // TG], E - 1)
            c.r += ET * (ITERS - 1)
            pool.wait_ge(pre, (ITERS - 1) * ET)
            for t in range(ET):
                gather(CR[:, t, :], X1d, ids[:, 1, t:t + 1], e1_f[t // TG])
            c.y += ET
            pool.wait_ge(x2_put, 2 * 32 * EG)

        def pe_segment_rows(pe, c, V, ring):
            for t in range(ET):
                b = ring(t)
                nc.tensor.matmul(b[0:P, :], Ss[:, t, :], V[:, t, :], start=True, stop=True).then_inc(R_ps, 1)

        def pe_L1(pe, c):
            pe_build(pe, c, diag1, 2)
            pe.wait_ge(sup_rdy, 1)
            pe_boundaries(pe, c, BW, lambda t: SUP[:, t:t + 1], 1)
            pe.wait_ge(B_sb, c.b)
            pe_segment_narrow(pe, c, Ss[0:P], Ms, lambda t: SUP[:, t:t + 1], BF1, 1)
            pe.wait_ge(w1_rdy, 2)
            pe_boundaries(pe, c, BW, lambda t: V1[0:P, t, :], D)
            pe.wait_ge(v_ext, 96)
            pe_segment_rows(pe, c, V1, lambda t: r_open(pe, c))
            r0, b0 = c.r, c.b
            assert ET % 2 == 0 and b0 == B1_0

            def step(i):
                def ring(t):
                    pe.wait_ge(R_sb, i * ET + (r0 - ET + t - 1))
                    return bank[4 + (r0 + t) % 2]
                pe.wait_ge(B_sb, i + (b0 - 1))
                for t in range(ET):
                    if t % TG == 0:
                        pe.wait_ge(*e1_y[t // TG].full(i * (16 * TG)))
                    q = nc.tensor.matmul(bank[7][0:NB, :], BW[:, t * NB:(t + 1) * NB], V1[0:P, t, :],
                                         start=t == 0, stop=t == ET - 1)
                q.then_inc(B_ps, 1)
                pe.wait_ge(v_ext, i * 32 + 96)
                pe_segment_rows(pe, c, V1, ring)
            step(1)
            with pe.Fori(2, ITERS) as i:
                step(i)
            c.r = r0 + ET * (ITERS - 1)
            c.b = b0 + ITERS - 1

        def act_L1(act, c):
            for t in range(ET):
                if t % TG == 0:
                    act.wait_ge(*e1_v[t // TG].full(16 * TG))
                    act.wait_ge(*e1_x[t // TG].full(16 * TG))
                for k, rows in enumerate((Y, V1[0:P])):
                    if c.a:
                        act.wait_ge(astep, c.a)
                    nc.scalar.activation(J1[:, 1, :], rows[:, t, :], ACT.Square,
                                         accum_out=v20[:, 5 + k, t:t + 1]).then_inc(astep, 1)
                    c.a += 1
                if t % TG == TG - 1 and t // TG < EARLY:
                    act_root(act, c)
            act.wait_ge(sc1, 1)
            nc.scalar.activation(v20[:, 5:7, :], v20[:, 5:7, :], ACT.Sqrt).then_inc(sc1a, 1)
            nc.scalar.activation(abv[:, :], abv[:, :], ACT.Exp).then_inc(sc1a, 1)
            act.wait_ge(sc1, 2)
            nc.scalar.activation(SD, SD, ACT.Exp).then_inc(sc1a, 1)
            for g in range(EARLY, EG):
                act_root(act, c)
            for t in range(ET):
                act.wait_ge(R_sb, EG + (8 + 8 + 4) * EG + EG + 1 + t + 1)
                nc.scalar.activation(Y[:, t, :], CR[:, t, :], ACT.Identity).then_inc(y_rdy, 1)
            for g in range(EG):
                act_root(act, c)

        def dve_L1(dve, c):
            def x2_of_targets(g):
                dve.wait_ge(*e1_b[g].full(32))
                dve_ln(dve, c, CR[:, g * TG:(g + 1) * TG, :], doubled=True)
            dve_build(dve, c, 1, RSs[:, :, 1], Ss, Ms, diag1)
            link(dve, c, nc.vector.memset(BW, 0.0))
            dve_boundary_cols(dve, c, BW, Ss, w1_rdy)
            dve.wait_ge(w1_rdy, 1)
            for t in range(ET):
                if t % TG == 0:
                    dve.wait_ge(*e1_v[t // TG].full(16 * TG))
                    dve.wait_ge(*e1_x[t // TG].full(16 * TG))
                link(dve, c, nc.vector.scalar_tensor_tensor(J1[:, 0, :], Y[:, t, :], 1.0, V1[0:P, t, :], ALU.mult,
                                                            ALU.mult, accum_out=v20[:, 4, t:t + 1]))
                if t % TG == TG - 1 and t // TG < EARLY:
                    x2_of_targets(t // TG)
            dve.wait_ge(astep, 2 * ET)
            nc.vector.tensor_scalar_max(v20[:, 5:7, :], v20[:, 5:7, :], 1e-12).then_inc(sc1, 1)
            dve.wait_ge(sc1a, 2)
            link(dve, c, nc.vector.reciprocal(v20[:, 5:7, :], v20[:, 5:7, :]))
            link(dve, c, nc.vector.tensor_tensor(SD, SD, SSQ, ALU.mult))
            link(dve, c, nc.vector.tensor_tensor(SD, SD, DSQ, ALU.mult))
            link(dve, c, nc.vector.tensor_tensor(TMP, RSs[:, :, 0], RSs[:, :, 1], ALU.not_equal))
            link(dve, c, nc.vector.tensor_tensor(SD, SD, TMP, ALU.mult))
            sg = v20[:, 8, 0:1]
            link(dve, c, nc.vector.tensor_tensor(sg, abv[:, 2:3], abv[:, 2:3], ALU.mult))
            link(dve, c, nc.vector.tensor_scalar_mul(sg, sg, 4.0))
            link(dve, c, nc.vector.reciprocal(sg, sg))
            nc.vector.tensor_scalar(SD, SD, sg, None, ALU.mult).then_inc(sc1, 1)
            dve.wait_ge(sc1a, 3)
            nc.vector.tensor_tensor(SUP, SD, RSs[:, :, 2], ALU.mult).then_inc(sup_rdy, 1)
            dve_b_evac(dve, c, BF1[:, 0:1], 1)
            dve_evac(dve, c, lambda b: nc.vector.tensor_copy(NN, b[0:P, 0:ET]))
            dve.wait_ge(R_sb, c.r)
            al, be = abv[:, 0:1], abv[:, 1:2]
            link(dve, c, nc.vector.tensor_scalar(RR, NN, al, be, ALU.mult, ALU.add))
            link(dve, c, nc.vector.tensor_scalar(RR, RR, al, None, ALU.add))
            link(dve, c, nc.vector.reciprocal(RR, RR))
            link(dve, c, nc.vector.tensor_scalar(RR, RR, al, None, ALU.mult))
            link(dve, c, nc.vector.scalar_tensor_tensor(NRR, RR, -1.0, NN, ALU.mult, ALU.mult))
            link(dve, c, nc.vector.tensor_tensor(TMP, SUP, RR, ALU.mult))
            dve.wait_ge(s_ext, 96)
            link(dve, c, nc.vector.tensor_tensor(Ss[0:P], Ss[0:P], b3(TMP, P), ALU.mult))
            dve_boundary_weights(dve, c, BW, 1, RSs[:, :, 1], TMP, w1_rdy)
            for g in range(EARLY, EG):
                x2_of_targets(g)
            dve_b_evac(dve, c, BF1, D)
            dve.wait_ge(x2_put, 32 * EG)
            for t in range(ET):
                dve_evac(dve, c, lambda b: nc.vector.scalar_tensor_tensor(
                    CR[:, t, :], Y[:, t, :], NRR[:, t:t + 1], b[0:P, :], ALU.mult, ALU.add))
                i = nc.vector.memset(V1[0:P, t, :], 0.0)
            i.then_inc(zr, 1)
            dve.wait_ge(R_sb, c.r)
            dve.wait_ge(y_rdy, ET)
            r0, b0 = c.r, c.b
            def step(i):
                dve.wait_ge(y_put, i * (32 * EG))
                for t in range(ET):
                    nc.vector.scalar_tensor_tensor(Y[:, t, :], Y[:, t, :], RR[:, t:t + 1], CR[:, t, :],
                                                   ALU.mult, ALU.add).then_inc(pre, 1)
                dve.wait_ge(B_ps, i + b0)
                nc.vector.tensor_copy(BF1, bank[7][0:NB, :]).then_inc(B_sb, 1)
                dve.wait_ge(pre, i * ET)
                for t in range(ET):
                    dve.wait_ge(R_ps, i * ET + (r0 - ET + t + 1))
                    nc.vector.tensor_tensor(Y[:, t, :], Y[:, t, :], bank[4 + (r0 + t) % 2][0:P, :],
                                            ALU.add).then_inc(R_sb, 1)
                dve.wait_ge(R_sb, i * ET + r0)
            step(1)
            with dve.Fori(2, ITERS) as i:
                step(i)
            c.r, c.b = r0 + ET * (ITERS - 1), b0 + ITERS - 1
            for g in range(EG):
                dve.wait_ge(*e1_f[g].full(16 * TG))
                Yg = Y[:, g * TG:(g + 1) * TG, :]
                link(dve, c, nc.vector.scalar_tensor_tensor(
                    Yg.rearrange("p t d -> p (t d)"), CR[:, g * TG:(g + 1) * TG, :].rearrange("p t d -> p (t d)"),
                    2.0, Yg.rearrange("p t d -> p (t d)"), ALU.mult, ALU.add))
                dve_ln(dve, c, Yg)

        WQ, WK, WV, WO = (at(2048 * k, [KC, D]) for k in range(4))
        V2x = at(8192, [ET, D], P + 2)
        V2 = V2x[0:P]
        BF2 = at(18432, [D], NB)
        XS2a, XD2, KQ2, T2, U2 = (at(18944 + G4 * k, [TG, D], P) for k in range(5))
        U2s = (U2, KQ2)
        XD2s = (XD2, XS2a)
        XS2 = (at(AR - G4, [TG, D], P), XS2a)
        XT2, YT2, TT2 = (at(29184 + 2000 * k, [KC, GR]) for k in range(3))
        AT2 = (XT2, YT2)
        F1T2 = at(35184, [GR], 34)
        eT, negT, FT = (at(18944 + 2500 * k, [E], H) for k in range(3))
        EE, EN, EX, FC = (at(35684 + ET * H * k, [ET, H], P) for k in range(4))
        w2_in, q_rdy, e_rdy, f_rdy, ft_rdy = (sem(k) for k in "w2_in q_ready e_ready fc_ready ft_ready".split())
        ex_in, ex_rdy, at_rdy, x3_put, bd_rdy = (sem(k) for k in "ex_in ex_ready attn_ready x3_put bd_ready".split())
        A_L1 = 192 + 64 * (ITERS - 1)
        x2_s, x2_d, x2_d2 = per_group("a", A_L1), per_group("b", 192), per_group("b", 256)

        T2_0 = EG * (8 + 12 + 4)
        Y2_0 = 4 * ET

        def y2_first(g):
            return Y2_0 + (3 * TG * g - TG if g else TG)

        def y2_tail(g):
            return Y2_0 + 3 * TG * (g + 1) + (TG if g + 1 < EG else 0)

        def y2t_first(g):
            return Y2_0 + 3 * TG * (EG + g) + TG

        def y2t_tail(g):
            return Y2_0 + 3 * TG * (EG + g + 1)

        def sp_L2(sp, c):
            for g in range(EG):
                sp.wait_ge(L_y, y2_tail(g))
                store(sp, X3d, 0, g, U2, x3_put)
            sp_ext(sp, V2x, BF2, B1_0 + ITERS - 1 + 3)
            sp.wait_ge(bd_rdy, 1)
            sp.dma_start(RD[:, :, :], RSd.rearrange("(t p) q -> p t q", p=P)).then_inc(rec_back, 16)
            c.y = y2_tail(EG - 1)
            for g in range(EG):
                sp.wait_ge(L_y, y2t_tail(g))
                sp.wait_ge(x3_put, 32 * (EG + g))
                store(sp, X3d, E, g, U2s[g % 2], x3_put)
            sp.wait_ge(x3_put, 2 * 32 * EG)

        def sp_L3(sp, c):
            sp.wait_ge(bd_rdy, 2)
            sp_segment_ends(sp, Sx, Sd)
            sp_ext(sp, V3x, BF3, B1_0 + ITERS - 1 + 4)

        def pe_ffn(pe, c, rows, TT, F1T):
            pe_transpose_rows(pe, c, rows)
            pe.wait_ge(T_sb, c.t)
            b = t_open(pe, c)
            for k in range(KC):
                i = nc.tensor.matmul(b[0:32, 0:GR], wcol(W_L2A + 32 * k, 32), TT[:, k, :], start=k == 0,
                                     stop=k == KC - 1)
            i.then_inc(T_ps, 1)
            pe.wait_ge(T_sb, c.t)
            for j in range(TG):
                b = r_open(pe, c)
                nc.tensor.matmul(b[0:P, :], F1T[:, j * P:(j + 1) * P], w32s[:, V_L2B:V_L2B + D], start=True,
                                 stop=True).then_inc(R_ps, 1)

        def act_ffn(act, c, TT, F1T):
            for k in range(KC):
                act_evac(act, c, TT[:, k, :], scale=colv[:, C_LN1G + k:C_LN1G + k + 1],
                         bias=colv[:, C_LN1B + k:C_LN1B + k + 1])
            act.wait_ge(R_ps, c.r)
            act_evac(act, c, F1T[0:32, :], src_rows=32, func=ACT.Relu, bias=colv[0:32, C_L2B1:C_L2B1 + 1])
            c.r += TG

        def dve_ffn_sum(dve, c, Tn, Un):
            link(dve, c, nc.vector.tensor_tensor(Un, Tn, spread(row(R_LN1G), TG), ALU.mult))
            for j in range(TG):
                dve_evac(dve, c, lambda b: nc.vector.tensor_tensor(Un[:, j, :], Un[:, j, :], b[0:P, :], ALU.add))
            dve.wait_ge(R_sb, c.r)

        def dve_ffn_tail(dve, c, Un, res, part, shifted=False):
            if part == 0:
                dve_ln_root(dve, c, Un)
            elif part == 1:
                dve_ln_rows(dve, c, Un)
                link(dve, c, nc.vector.tensor_tensor(Un, Un, spread(row(R_LN2G), TG), ALU.mult))
            elif part == 2:
                if not shifted:
                    link(dve, c, nc.vector.tensor_tensor(Un, Un, spread(row(R_LN2B), TG), ALU.add))
                link(dve, c, nc.vector.tensor_tensor(Un, Un, res, ALU.add))
                dve_ln_root(dve, c, Un)
            else:
                dve_ln_rows(dve, c, Un)

        shifted = sem("residual_shifted")

        def pool_L2(pool, c):
            for g in range(EG):
                if g >= 2:
                    c.y = y2_tail(g - 2)
                    pool.wait_ge(L_y, c.y)
                for j in range(TG):
                    t = TG * g + j
                    gather(XS2[g % 2][:, j, :], X2d, idd[:, 6, t:t + 1], x2_s[g])
                if g:
                    pool.wait_ge(T_sb, T2_0 + 13 * (g - 1) + 8)
                for j in range(TG):
                    t = TG * g + j
                    gather(XD2[:, j, :], X2d, idd[:, 5, t:t + 1], x2_d[g])
                c.r += 4 * TG
            c.y = y2_tail(EG - 1)
            c.r += 2 * EG + 1 + 1 + 1
            pool.wait_ge(R_sb, c.r)
            for g in range(EG):
                if g >= 2:
                    pool.wait_ge(L_y, y2t_tail(g - 2))
                for j in range(TG):
                    t = TG * g + j
                    gather(XD2s[g % 2][:, j, :], X2d, idd[:, 5, t:t + 1], x2_d2[g])
                for h in ((g - 1,) if g + 1 < EG else (g - 1, g)):
                    if h >= 0:
                        pool.wait_ge(R_sb, c.r + 2 * TG * h + TG)
                        for j in range(TG):
                            i = nc.gpsimd.tensor_tensor(XD2s[h % 2][:, j, :], XD2s[h % 2][:, j, :], row(R_LN2B),
                                                        ALU.add)
                        i.then_inc(shifted, 1)
            c.r += 2 * TG * EG
            c.y += 3 * TG * EG
            pool.wait_ge(x3_put, 2 * 32 * EG)

        def pe_L2(pe, c):
            pe.wait_ge(w2_in, 16 * 4)
            for g in range(EG):
                pe.wait_ge(*x2_s[g].full(16 * TG))
                pe_transpose_rows(pe, c, XS2[g % 2])
                pe.wait_ge(*x2_d[g].full(16 * TG))
                pe_transpose_rows(pe, c, XD2)
                pe.wait_ge(T_sb, c.t)
                for j in range(TG):
                    for fT, W in ((YT2, WQ), (XT2, WK), (XT2, WV)):
                        b = r_open(pe, c)
                        for k in range(KC):
                            i = nc.tensor.matmul(b[0:P, :], fT[:, k, j * P:(j + 1) * P], W[:, k, :],
                                                 start=k == 0, stop=k == KC - 1)
                        i.then_inc(R_ps, 1)
                pe.wait_ge(L_y, y2_first(g))
                pe_ffn(pe, c, T2, TT2, F1T2)
            c.y = y2_tail(EG - 1)
            pe.wait_ge(e_rdy, 1)
            for src in (EE, EN):
                for g in range(EG):
                    b = r_open(pe, c)
                    for j in range(TG):
                        i = nc.tensor.transpose(b[0:H, j * P:(j + 1) * P], src[:, TG * g + j, :], ident[0:P, 0:P])
                    i.then_inc(R_ps, 1)
            pe.wait_ge(ft_rdy, 1)
            b = r_open(pe, c)
            for t in range(ET):
                i = nc.tensor.transpose(b[0:P, t * H:(t + 1) * H], FT[:, t * P:(t + 1) * P], ident[0:H, 0:H])
            i.then_inc(R_ps, 1)
            for done, src in ((f_rdy, FC), (ex_rdy, EX)):
                pe.wait_ge(done, 1)
                pe_boundaries(pe, c, Bd[:, :], lambda t: src[:, t, :], H)
                pe.wait_ge(B_sb, c.b)
                pe_segment_narrow(pe, c, Sd, Md, lambda t: src[:, t, :], BF2, H)
            pe_boundaries(pe, c, Bd[:, :], lambda t: V2[:, t, :], D, lambda g: (at_rdy, g + 1))
            pe.wait_ge(v_ext, 32 * (2 + ITERS + 1))
            for g in range(EG + 1):
                if g:
                    pe.wait_ge(T_sb, c.t)
                    pe_rows_out(pe, c, [(AT2[(g - 1) % 2], WO)])
                if g < EG:
                    for k in range(KC):
                        pe_segment_T(pe, c, t_open(pe, c), Sx, V2x, g, k, True).then_inc(T_ps, 1)
                if g:
                    pe.wait_ge(L_y, y2t_first(g - 1))
                    pe_ffn(pe, c, T2, TT2, F1T2)

        def act_L2(act, c):
            c.r += EG + 1 + ET * ITERS
            for g in range(EG):
                act.wait_ge(R_ps, c.r)
                for fT in (XT2, YT2):
                    for k in range(KC):
                        act_evac(act, c, fT[:, k, :])
                act_root(act, c)
                if g:
                    for q in range(2):
                        act_root(act, c)
                c.r += 3 * TG
                act_ffn(act, c, TT2, F1T2)
            act_root(act, c)
            act.wait_ge(ex_in, 1)
            nc.scalar.activation(EX[:, :, :], EX[:, :, :], ACT.Exp).then_inc(ex_rdy, 1)
            act_root(act, c)
            c.r += 2 * EG + 3
            for g in range(EG + 1):
                if g >= 2:
                    for q in range(2):
                        act_root(act, c)
                if g:
                    c.r += TG
                    act_root(act, c)
                if g < EG:
                    for k in range(KC):
                        act_evac(act, c, AT2[g % 2][:, k, :])
                if g:
                    act_ffn(act, c, TT2, F1T2)
            for q in range(2):
                act_root(act, c)

        def dve_L2(dve, c):
            nc.vector.memset(F1T2[32:34, :], 1.0)
            for g in range(EG):
                dve.wait_ge(*x2_s[g].full(16 * TG))
                link(dve, c, nc.vector.tensor_copy(T2, XS2[g % 2]))
                dve_ln(dve, c, T2)
                for j in range(TG):
                    t = TG * g + j
                    dve_evac(dve, c, lambda b: nc.vector.tensor_copy(KQ2[:, j, :], b[0:P, :]))
                    dve.wait_ge(R_sb, c.r)
                    dve_evac(dve, c, lambda b: nc.vector.tensor_tensor(KQ2[:, j, :], KQ2[:, j, :], b[0:P, :],
                                                                       ALU.mult))
                    dve_evac(dve, c, lambda b: nc.vector.tensor_copy(V2[:, t, :], b[0:P, :]))
                    if g:
                        dve_ffn_tail(dve, c, U2, XS2[(g - 1) % 2], j)
                dve.wait_ge(R_sb, c.r)
                for j in range(TG):
                    i = nc.vector.tensor_reduce(EE[:, TG * g + j, :],
                                                KQ2[:, j, :].rearrange("p (h d) -> p h d", h=H), AX.X, ALU.add)
                link(dve, c, i)
                if g:
                    dve.wait_ge(x3_put, 32 * g)
                dve_ffn_sum(dve, c, T2, U2)
            start = v20[:, 9, :]
            link(dve, c, nc.vector.tensor_scalar(start, RD[:, :, Q_DSC], float(FAR), NEG, ALU.is_lt, ALU.mult))
            nc.vector.tensor_copy(EN[:, :, :], b3(start, H)).then_inc(e_rdy, 1)
            for dst, f in ((eT, 0.125), (negT, 1.0)):
                assert DK == 64
                for g in range(EG):
                    dve_evac(dve, c, lambda b: nc.vector.tensor_scalar_mul(dst[:, g * GR:(g + 1) * GR],
                                                                           b[0:H, 0:GR], f))
            dve.wait_ge(R_sb, c.r)
            nc.vector.tensor_tensor_scan(FT, negT, eT, NEG, ALU.add, ALU.max).then_inc(ft_rdy, 1)
            last = v20[:, 10, :]
            link(dve, c, nc.vector.tensor_scalar_add(last, RD[:, :, Q_DUP], 1.0))
            link(dve, c, nc.vector.tensor_tensor(last, last, RD[:, :, Q_CNT], ALU.is_equal))
            dve_evac(dve, c, lambda b: nc.vector.tensor_tensor(
                FC[:, :, :], b[0:P, 0:ET * H].rearrange("p (t h) -> p t h", h=H), b3(last, H), ALU.mult))
            dve.wait_ge(R_sb, c.r)
            link(dve, c, nc.vector.memset(Bd[:, :], 0.0))
            dve_boundary_cols(dve, c, Bd, Sd, f_rdy)
            dve_b_evac(dve, c, BF2[:, 0:H], H)
            for part in range(2):
                dve_ffn_tail(dve, c, U2, XS2[(EG - 1) % 2], part)
            dve.wait_ge(R_ps, c.r + 1)
            bmax = bank[4 + c.r % 2][0:P, 0:ET * H].rearrange("p (t h) -> p t h", h=H)
            c.r += 1
            nc.vector.scalar_tensor_tensor(EX[:, :, :], EE[:, :, :], 0.125, bmax, ALU.mult,
                                           ALU.subtract).then_inc(R_sb, 1)
            dve.wait_ge(R_sb, c.r)
            nc.vector.memset(lst[:, :, :], 0.0).then_inc(ex_in, 1)
            dve_b_evac(dve, c, BF2[:, 0:H], H)
            for part in range(2, 4):
                dve_ffn_tail(dve, c, U2, XS2[(EG - 1) % 2], part)
            dve_evac(dve, c, lambda b: nc.vector.reciprocal(
                FC[:, :, :], b[0:P, 0:ET * H].rearrange("p (t h) -> p t h", h=H)))
            dve.wait_ge(R_sb, c.r)
            link(dve, c, nc.vector.tensor_tensor(EX[:, :, :], EX[:, :, :], FC[:, :, :], ALU.mult))
            dve_boundary_weights(dve, c, Bd[:, :], 0, RD[:, :, Q_DST], None, bd_rdy)
            for t in range(ET):
                vt = V2[:, t, :].rearrange("p (h d) -> p h d", h=H)
                i = nc.vector.tensor_tensor(vt, vt, b3(EX[:, t, :], DK), ALU.mult)
                if t % TG == TG - 1:
                    i.then_inc(at_rdy, 1)
            dve_b_evac(dve, c, BF2, D)
            dve.wait_ge(x3_put, 32 * EG)
            for g in range(EG):
                dve.wait_ge(*x2_d2[g].full(16 * TG))
                for j in range(TG):
                    dve_evac(dve, c, lambda b: nc.vector.tensor_tensor(T2[:, j, :], XD2s[g % 2][:, j, :], b[0:P, :],
                                                                       ALU.add))
                    if g:
                        if j == 2:
                            dve.wait_ge(shifted, g)
                        dve_ffn_tail(dve, c, U2s[(g - 1) % 2], XD2s[(g - 1) % 2], j, shifted=True)
                dve.wait_ge(R_sb, c.r)
                dve_ln(dve, c, T2)
                if g >= 2:
                    dve.wait_ge(x3_put, 32 * (EG + g - 1))
                dve_ffn_sum(dve, c, T2, U2s[g % 2])
            dve.wait_ge(rec_back, 16 * 7)
            for k, col in enumerate((Q_SI, Q_XD, Q_DSC, Q_SSC)):
                i = nc.vector.tensor_copy(idd[:, k, :], RD[:, :, col])
            i.then_inc(rec_done, 1)
            dve.wait_ge(shifted, EG)
            for part in range(4):
                dve_ffn_tail(dve, c, U2s[(EG - 1) % 2], XD2s[(EG - 1) % 2], part, shifted=True)

        diag3 = at(0, [ET, P], P)
        V3x = at(0, [ET, D], P + 2)
        V3 = V3x[0:P]
        BF3 = at(10240, [D], NB)
        XS3, XD3, SR3, WA3 = (at(10752 + G4 * k, [TG, D], P) for k in range(4))
        PST, PDT, XG3, ND3 = (at(18944 + 2000 * k, [KC, GR]) for k in range(4))
        XST, XDT = (at(26944 + 2000 * k, [KC, GR]) for k in range(2))
        O3 = at(30944, [TG, D], P)
        G1T = at(32992, [2, GR])
        GT3, N1T3, IPT = (at(33992 + GR * k, [GR]) for k in range(3))
        SQ3 = XG3[:, 1:4, :]
        EAT, SX, SA, FS, SS = (at(35492 + GR * k, [GR], 32) for k in range(5))
        x3_s, x3_d, x3_d2 = per_group("a", A_L1 + 64), per_group("b", 320), per_group("b", 384)
        n1_in, n1_rdy, xg_rdy, ip_rdy, sp_in3, sp_rdy, v3_rdy = (sem(k) for k in
            "n1_in n1_ready xg_ready ip_ready softplus_in softplus_ready v3_ready".split())
        out_put = sem("out_put")

        T3_0 = EG * (8 + 12 + 4) + EG * (13 + 9)
        XD3s = (XD3, XS3)

        def pool_L3(pool, c):
            pool.wait_ge(rec_done, 3)
            c.r += EG
            for g in range(EG + 1):
                for j in range(TG):
                    if g == EG:
                        break
                    if g and j == 0:
                        pool.wait_ge(R_sb, c.r - 2 * TG)
                    gather(XS3[:, j, :], X3d, idd[:, 1, TG * g + j:TG * g + j + 1], x3_s[g])
                for j in range(TG):
                    if g == EG:
                        break
                    if g and j == 0:
                        pool.wait_ge(T_sb, T3_0 + 26 * g - 10)
                    gather(XD3[:, j, :], X3d, idd[:, 0, TG * g + j:TG * g + j + 1], x3_d[g])
                if g == EG:
                    pool.wait_ge(R_sb, c.r)
                    for q in range(2):
                        for j in range(TG):
                            gather(XD3s[q][:, j, :], X3d, idd[:, 0, TG * q + j:TG * q + j + 1], x3_d2[q])
                if g:
                    for j in range(TG):
                        pool.wait_ge(L_y, c.y + j + 1)
                        scatter(out, idd[:, 2, TG * (g - 1) + j:TG * (g - 1) + j + 1], O3[:, j, :], out_put)
                    c.y += TG
                c.r += 4 * TG
            pool.wait_ge(out_put, 16 * ET)
            for g in range(EG):
                for j in range(TG):
                    pool.wait_ge(L_y, c.y + j + 1)
                    scatter(out, idd[:, 3, TG * g + j:TG * g + j + 1], O3[:, j, :], out_put)
                c.y += TG
                if g + 2 < EG:
                    for j in range(TG):
                        t = TG * (g + 2) + j
                        gather(XD3s[g % 2][:, j, :], X3d, idd[:, 0, t:t + 1], x3_d2[g + 2])
            pool.wait_ge(out_put, 2 * 16 * ET)

        def pe_one(pe, c, rows, n, pairs):
            b = t_open(pe, c)
            for q, (W, fT) in enumerate(pairs):
                i = nc.tensor.matmul(b[0:rows, 0:n], W, fT, start=q == 0, stop=q == len(pairs) - 1)
            i.then_inc(T_ps, 1)

        def pe_gate(pe, c, fT, n):
            pe.wait_ge(n1_rdy, n)
            for m in range(2):
                pe_one(pe, c, 128, GR, [(wcol(W_G1 + 128 * m, 128), fT[:, 0, :]),
                                        (wcol(W_G1 + 256 + 128 * m, 128), N1T3)])
            pe.wait_ge(T_sb, c.t)
            for m in range(2):
                pe_one(pe, c, 128, GR, [(wcol(W_G2 + 128 * m, 128), G1T[:, 0, :]),
                                        (wcol(W_G2 + 256 + 128 * m, 128), G1T[:, 1, :])])
            pe.wait_ge(xg_rdy, n)

        def act_gate_in(act, c, fT, n):
            for k in range(KC):
                act_evac(act, c, fT[:, k, :])
            act.wait_ge(n1_in, n)
            nc.scalar.activation(N1T3, SQ3[:, 0, :], ACT.Sqrt, scale=1.0 / 3.0).then_inc(n1_rdy, 1)

        def act_gate(act, c):
            for m in range(2):
                act_evac(act, c, G1T[:, m, :], func=ACT.Silu, bias=colv[:, C_BG1 + m:C_BG1 + m + 1])
            for m, dst in enumerate((XG3[:, 0, :], GT3)):
                act_evac(act, c, dst, bias=colv[:, C_BG2 + m:C_BG2 + m + 1])

        def dve_gate_in(dve, c, fT, t0):
            dve.wait_ge(T_sb, t0)
            for k in range(3):
                i = nc.vector.tensor_tensor(SQ3[:, k, :], fT[:, k + 1, :], fT[:, k + 1, :], ALU.mult)
            link(dve, c, i)
            link(dve, c, nc.vector.tensor_tensor(SQ3[:, 0, :], SQ3[:, 0, :], SQ3[:, 1, :], ALU.add))
            nc.vector.tensor_tensor(SQ3[:, 0, :], SQ3[:, 0, :], SQ3[:, 2, :], ALU.add).then_inc(n1_in, 1)

        def dve_gate(dve, c, fT, t0):
            dve.wait_ge(T_sb, t0 + 4)
            for k in range(3):
                i = nc.vector.tensor_tensor(XG3[:, k + 1, :], fT[:, k + 1, :], GT3, ALU.mult)
            i.then_inc(xg_rdy, 1)

        def dve_last(dve, c, rows):
            for j in range(TG):
                dve.wait_ge(R_ps, c.r + 1)
                b = bank[4 + c.r % 2]
                c.r += 1
                nc.vector.scalar_tensor_tensor(vec3(O3[:, j, 128:D]), vec3(rows[:, j, 128:D]), 2.0,
                                               b[0:P, 128:D].rearrange("p (c u) -> p c u", c=3),
                                               ALU.mult, ALU.add)
                nc.vector.scalar_tensor_tensor(O3[:, j, 0:128], rows[:, j, 0:128], 2.0, b[0:P, 0:128],
                                               ALU.mult, ALU.add).then_inc(R_sb, 1)
            dve.wait_ge(R_sb, c.r)
            link(dve, c, nc.vector.tensor_tensor(O3[:, :, 0:128], O3[:, :, 0:128], spread(row(R_L3, 128), TG),
                                                 ALU.add))

        def dve_messages(dve, c, g, tiles):
            for j in tiles:
                t = TG * g + j
                w = [WA3[:, j, 128 * k:128 * (k + 1)] for k in range(4)]
                sh = [RD[:, t, Q_SH + k:Q_SH + k + 1] for k in range(4)]
                x0, x1 = SR3[:, j, 0:128], [SR3[:, j, 128 * k:128 * (k + 1)] for k in (1, 2, 3)]
                o = [V3[:, t, 128 * k:128 * (k + 1)] for k in range(4)]
                S1, S2, S3 = PST[0:P, 1, 0:128], PST[0:P, 1, 128:256], PST[0:P, 2, 0:384]
                link(dve, c, nc.vector.tensor_scalar(S1, x1[0], sh[1], None, ALU.mult))
                link(dve, c, nc.vector.scalar_tensor_tensor(S1, x1[1], sh[2], S1, ALU.mult, ALU.add))
                link(dve, c, nc.vector.scalar_tensor_tensor(S1, x1[2], sh[3], S1, ALU.mult, ALU.add))
                nc.vector.scalar_tensor_tensor(S1, S1, 3.0 ** -0.5, w[3], ALU.mult, ALU.mult)
                nc.vector.scalar_tensor_tensor(S2, x0, sh[0], w[0], ALU.mult, ALU.mult)
                for k in range(3):
                    nc.vector.scalar_tensor_tensor(o[k + 1], x0, sh[k + 1], w[1], ALU.mult, ALU.mult)
                link(dve, c, nc.vector.scalar_tensor_tensor(
                    S3.rearrange("p (c u) -> p c u", c=3), SR3[:, j, 128:D].rearrange("p (c u) -> p c u", c=3),
                    sh[0], spread(w[2], 3), ALU.mult, ALU.mult))
                nc.vector.tensor_tensor(o[0], S1, S2, ALU.add)
                i = nc.vector.tensor_tensor(V3[:, t, 128:D], V3[:, t, 128:D], S3, ALU.add)
                if j + 1 < TG:
                    link(dve, c, i)
                else:
                    i.then_inc(v3_rdy, 1)

        def pe_last(pe, c, fT):
            for j in range(TG):
                b = r_open(pe, c)
                for k in range(KC):
                    i = nc.tensor.matmul(b[0:P, k * 128:(k + 1) * 128], fT[:, k, j * P:(j + 1) * P],
                                         wcol(W_O1 if k else W_O0, 128), start=k == 0, stop=k == KC - 1)
                i.then_inc(R_ps, 1)

        def pe_L3(pe, c):
            pe_build(pe, c, diag3, 3)
            pe.wait_ge(*x3_s[0].full(16 * TG))
            pe_transpose_rows(pe, c, XS3, True)
            for g in range(EG):
                pe_gate(pe, c, XST, g + 1)
                for k in range(KC):
                    pe_one(pe, c, 128, GR, [(wcol(W_ND1 if k else W_ND0, 128), XG3[:, k, :])])
                for j in range(TG):
                    b = r_open(pe, c)
                    for k in range(KC):
                        i = nc.tensor.matmul(b[0:P, k * 128:(k + 1) * 128], XG3[:, k, j * P:(j + 1) * P],
                                             wcol(W_ND1 if k else W_ND0, 128), start=k == 0, stop=k == KC - 1)
                    i.then_inc(R_ps, 1)
                pe.wait_ge(T_sb, c.t)
                pe_last(pe, c, ND3)
                pe.wait_ge(*x3_d[g].full(16 * TG))
                pe_transpose_rows(pe, c, XD3, True)
                pe.wait_ge(T_sb, c.t)
                for k in range(KC):
                    pe_one(pe, c, 128, GR, [(wcol(W_PRE1 if k else W_PRE0, 128), XDT[:, k, :])])
                for k in range(1, KC):
                    pe_one(pe, c, 128, GR, [(wcol(W_PRE1, 128), XST[:, k, :])])
                b = t_open(pe, c)
                for j in range(TG):
                    i = nc.tensor.transpose(b[0:32, j * P:(j + 1) * P], RD[:, TG * g + j, Q_EA:Q_SSC],
                                            ident[0:P, 0:P])
                i.then_inc(T_ps, 1)
                pe.wait_ge(T_sb, c.t)
                pe_one(pe, c, 32, GR, [(w32s[0:32, V_F1:V_F1 + 32], EAT)])
                pe.wait_ge(ip_rdy, g + 1)
                pe_one(pe, c, 32, GR, [(wcol(W_S1, 32), PDT[:, 0, :]), (wcol(W_S1 + 32, 32), PDT[:, 0, :]),
                                       (wcol(W_S1 + 64, 32), IPT)])
                if g + 1 < EG:
                    pe.wait_ge(*x3_s[g + 1].full(16 * TG))
                    pe_transpose_rows(pe, c, XS3, True)
                pe.wait_ge(sp_rdy, 2 * g + 2)
                for j in range(TG):
                    for src, w in ((FS, V_F2), (SS, V_S2)):
                        b = r_open(pe, c)
                        nc.tensor.matmul(b[0:P, :], src[:, j * P:(j + 1) * P], w32s[0:32, w:w + D], start=True,
                                         stop=True).then_inc(R_ps, 1)
            pe.wait_ge(s_ext, 128)
            pe_boundaries(pe, c, Bd[:, :], lambda t: V3[:, t, :], D, lambda g: (v3_rdy, g + 1))
            pe.wait_ge(v_ext, 32 * (2 + ITERS + 2))
            for g in range(EG + 1):
                if g < EG:
                    pe.wait_ge(*x3_d2[g].full(16 * TG))
                    pe_transpose_rows(pe, c, XD3s[g % 2], True)
                if g:
                    pe.wait_ge(T_sb, T3_0 + 26 * EG + 12 * g)
                    pe_last(pe, c, ND3)
                if g == EG:
                    break
                pe_gate(pe, c, XDT, EG + g + 1)
                for k in range(KC):
                    b = t_open(pe, c)
                    nc.tensor.matmul(b[:, 0:GR], wcol(W_ND1 if k else W_ND0, 128), XG3[:, k, :], start=True,
                                     stop=False)
                    pe_segment_T(pe, c, b, Sx, V3x, g, k, False).then_inc(T_ps, 1)

        def act_nd(act, c):
            act_evac(act, c, ND3[:, 0, :], bias=colv[:, C_BND:C_BND + 1])
            for k in range(1, KC):
                act_evac(act, c, ND3[:, k, :])

        def act_softplus(act, c):
            act.wait_ge(T_ps, c.t + 1)
            c.t += 1
            b = bank[(c.t - 1) % 4][0:32, 0:GR]
            nc.scalar.activation(SX, b, ACT.Identity)
            nc.scalar.activation(SA, b, ACT.Abs).then_inc(T_sb, 1)
            act.wait_ge(T_sb, c.t)
            nc.scalar.activation(SA, SA, ACT.Exp, scale=-1.0).then_inc(astep, 1)
            c.a += 1
            act.wait_ge(astep, c.a)
            nc.scalar.activation(SA, SA, ACT.Ln, bias=1.0).then_inc(sp_in3, 1)

        def act_L3(act, c):
            c.r += EG
            act_gate_in(act, c, XST, 1)
            for g in range(EG):
                act_gate(act, c)
                act.wait_ge(R_ps, c.r)
                act_nd(act, c)
                for k in range(KC):
                    act_evac(act, c, XDT[:, k, :])
                act_root(act, c)
                act_evac(act, c, PDT[:, 0, :], bias=colv[:, C_BPRE:C_BPRE + 1])
                for k in range(1, KC):
                    act_evac(act, c, PDT[:, k, :])
                if g:
                    act.wait_ge(v3_rdy, g)
                for k in range(1, KC):
                    act_evac(act, c, PST[:, k, :], scale=1.0 / 3.0)
                act_evac(act, c, EAT, src_rows=32)
                if g:
                    act.wait_ge(sp_rdy, 2 * g)
                act_softplus(act, c)
                act.wait_ge(sp_rdy, 2 * g + 1)
                act_softplus(act, c)
                if g + 1 < EG:
                    act_gate_in(act, c, XST, g + 2)
                c.r += TG + 2 * TG + TG
            for g in range(EG + 1):
                if g < EG:
                    act_gate_in(act, c, XDT, EG + g + 1)
                if g:
                    act_root(act, c)
                if g < EG:
                    act_gate(act, c)
                    act.wait_ge(R_ps, c.r)
                    act_nd(act, c)
                c.r += TG

        def dve_L3(dve, c):
            t0 = EG * (8 + 12 + 4) + EG * (13 + 9)
            dve_build(dve, c, 1, RD[:, :, Q_SRC], Sd, Md, diag3)
            dve_boundary_weights(dve, c, Bd[:, :], 1, RD[:, :, Q_SRC], None, bd_rdy)
            dve.wait_ge(bd_rdy, 2)
            dve_gate_in(dve, c, XST, t0 + 4)
            for g in range(EG):
                if g:
                    dve_messages(dve, c, g - 1, (0, 1))
                dve_gate(dve, c, XST, t0 + 4)
                if g:
                    dve_messages(dve, c, g - 1, (2, 3))
                for j in range(TG):
                    dve_evac(dve, c, lambda b: nc.vector.tensor_copy(SR3[:, j, :], b[0:P, :]))
                dve.wait_ge(R_sb, c.r)
                link(dve, c, nc.vector.tensor_tensor(
                    SR3[:, :, 0:128], SR3[:, :, 0:128], spread(rowv[:, R_L3, 128:256], TG), ALU.add))
                if g:
                    dve.wait_ge(out_put, 64 * g)
                dve_last(dve, c, XS3)
                dve_ln(dve, c, O3)
                dve.wait_ge(T_sb, t0 + 23)
                for k in range(1, KC):
                    i = nc.vector.tensor_tensor(PST[:, k, :], PST[:, k, :], PDT[:, k, :], ALU.mult)
                link(dve, c, i)
                link(dve, c, nc.vector.tensor_tensor(PST[:, 1, :], PST[:, 1, :], PST[:, 2, :], ALU.add))
                nc.vector.tensor_tensor(IPT, PST[:, 1, :], PST[:, 3, :], ALU.add).then_inc(ip_rdy, 1)
                for k, dst in enumerate((FS, SS)):
                    dve.wait_ge(sp_in3, 2 * g + k + 1)
                    link(dve, c, nc.vector.scalar_tensor_tensor(dst, SX, 0.0, SA, ALU.max, ALU.add))
                    nc.vector.tensor_scalar_add(dst, dst, -LN2).then_inc(sp_rdy, 1)
                if g + 1 < EG:
                    dve_gate_in(dve, c, XST, t0 + 26 + 4)
                for j in range(TG):
                    dve_evac(dve, c, lambda b: nc.vector.tensor_copy(WA3[:, j, :], b[0:P, :]))
                    dve.wait_ge(R_sb, c.r)
                    dve_evac(dve, c, lambda b: nc.vector.tensor_tensor(WA3[:, j, :], WA3[:, j, :], b[0:P, :],
                                                                       ALU.mult))
                dve.wait_ge(R_sb, c.r)
                t0 += 26
            dve_messages(dve, c, EG - 1, range(TG))
            dve_b_evac(dve, c, BF3, D)
            for g in range(EG + 1):
                if g < EG:
                    dve_gate_in(dve, c, XDT, t0 + 4)
                if g:
                    dve.wait_ge(out_put, 64 * (EG + g - 1))
                    dve_last(dve, c, XD3s[(g - 1) % 2])
                    dve_ln_root(dve, c, O3)
                if g < EG:
                    dve_gate(dve, c, XDT, t0 + 4)
                if g:
                    dve_ln_rows(dve, c, O3)
                t0 += 12
            c.t = t0 - 12

        @block.sync
        def _(sp):
            for dst, src in ((ident, ident_in), (colv, cols), (ws, wsmall), (w32s, w32), (W1r, w_r1),
                             (W2r, w_r2)):
                sp.dma_start(dst[:], src).then_inc(s_w, 16)
            sp.dma_start(rowv[:, :, :], rows.partition_broadcast(P)).then_inc(s_w, 16)
            sp_in(sp, 0, 0)
            for q in range(2):
                sp.dma_start(keys_f[q].bitcast(I32), keys[q].partition_broadcast(P)).then_inc(keys_in, 16)
            sp.dma_start(kfc[:, :].bitcast(I32), key_cols).then_inc(keys_in, 16)
            sp.dma_start(ones[:, :], earlier_in).then_inc(keys_in, 16)
            sp_in(sp, 1, 1)

            def step(s, par):
                if not isinstance(s, int) or s + 1 < NG:
                    sp_in(sp, s + 1, 1 - par)
                if has(s, "S"):
                    sp_out(sp, s - LAG["S"])
            for s in range(1, LAG["S"]):
                step(s, s % 2)
            with sp.Fori(LAG["S"] // 2, NG // 2 - 1) as i:
                step(i * 2, 0)
                step(i * 2 + 1, 1)
            for s in range(NG - 2, STEPS):
                if s == NG:
                    sp_records(sp)
                step(s, s % 2)
                if s == NG + 2:
                    sp_records_back(sp)
            c = Counts()
            c.ph, c.r = 1, EG
            sp_L0(sp, c)
            c.ph = 2
            sp.wait_ge(phase_end, 4 * c.ph)
            sp_L1(sp, c)
            c.ph = 3
            sp_L2(sp, c)
            c.ph = 4
            sp_L3(sp, c)

        @block.tensor
        def _(pe):
            pe.wait_ge(s_w, 16 * 7)
            node_steps(pe, lambda st_, s, par: pe_step(pe, st_, s, par))
            c = Counts()
            end_phase(pe, c)
            pe_build(pe, c, diag, 1)
            pe_L0(pe, c)
            end_phase(pe, c)
            pe_L1(pe, c)
            end_phase(pe, c)
            pe_L2(pe, c)
            end_phase(pe, c)
            pe_L3(pe, c)

        @block.scalar
        def _(act):
            act.wait_ge(s_w, 16 * 7)
            act.wait_ge(counts, 1)
            node_steps(act, lambda st_, s, par: act_step(act, st_, s, par))
            c = Counts()
            c.r = EG
            end_phase(act, c)
            act_L0(act, c)
            end_phase(act, c)
            act_L1(act, c)
            end_phase(act, c)
            act_L2(act, c)
            end_phase(act, c)
            act_L3(act, c)

        @block.vector
        def _(dve):
            nc.vector.memset(f1T[32:34, :], 1.0)
            nc.vector.memset(earlier[:, 0:E], 1)
            nc.vector.memset(earlier[:, E + P:2 * E], 0)
            dve.wait_ge(s_w, 16 * 7)
            dve.wait_ge(keys_in, 16 * 4)
            nc.vector.tensor_copy(earlier[:, E:E + P], ones[:, :])
            for q in range(2):
                nc.vector.tensor_copy(keys_f[q], keys_f[q].bitcast(I32))
            nc.vector.tensor_copy(kfc[:, :], kfc[:, :].bitcast(I32)).then_inc(neg_rdy, 1)
            dve.wait_ge(neg_rdy, 1)
            nc.vector.tensor_scalar_mul(neg_key[:, :], kfc[:, :], -1.0).then_inc(counts, 1)
            c = Counts()

            def step(st_, s, par):
                dve_step(dve, st_, s, par)
                if isinstance(s, int) and s == NG:
                    dve_records(dve, c)
            node_steps(dve, step)
            dve_records_back(dve, c)
            end_phase(dve, c)
            dve.wait_ge(C["out"], 32 * NG)
            dve_build(dve, c, 0, RD[:, :, Q_DST], Sd, Md, diag)
            dve_L0(dve, c)
            end_phase(dve, c)
            dve_L1(dve, c)
            end_phase(dve, c)
            dve_L2(dve, c)
            end_phase(dve, c)
            dve_L3(dve, c)

        @block.gpsimd
        def _(pool):
            pool.wait_ge(s_w, 16 * 7)
            def step(st_, s, par):
                pool_step(pool, st_, s, par)
                if isinstance(s, int) and s == NG + 1:
                    pool_records(pool)
            node_steps(pool, step)
            c = Counts()
            c.r = EG
            end_phase(pool, c)
            pool.wait_ge(C["out"], 32 * NG)
            pool.wait_ge(rec_done, 2)
            pool_L0(pool, c)
            end_phase(pool, c)
            pool_L1(pool, c)
            end_phase(pool, c)
            pool_L2(pool, c)
            end_phase(pool, c)
            pool_L3(pool, c)


def kernel(**inputs):
    import numpy as np
    import concourse.bacc as bacc
    from concourse.bass_utils import run_bass_kernel_spmd

    a = {k: np.asarray(v) for k, v in inputs.items()}
    f32 = np.float32

    def colsof(v):
        return v.reshape(-1, 128).T

    def chunks(w):
        return np.ascontiguousarray(w.reshape(w.shape[0] // 128, 128, -1).transpose(1, 0, 2))

    def flat(w):
        return chunks(w).reshape(128, -1)

    cols = np.zeros((128, C_END), f32)
    cols[:, C_L0B1:C_LN1G] = colsof(a["L0_gnn_b1"])
    cols[:, C_LN1G:C_LN1B] = colsof(a["L2_gnn_ln1_g"])
    cols[:, C_LN1B:C_L2B1] = colsof(a["L2_gnn_ln1_b"])
    cols[0:32, C_L2B1] = a["L2_gnn_b1"]
    cols[:, C_BG1:C_BG2] = colsof(a["L3_gnn_b_g1"])
    cols[:, C_BG2:C_BND] = colsof(a["L3_gnn_b_g2"])
    cols[:, C_BND] = a["L3_gnn_b_nd0"]
    cols[:, C_BPRE] = a["L3_gnn_b_pre0"]
    rows = np.zeros((R_END, D), f32)
    for r, k in ((R_L0B2, "L0_gnn_b2"), (R_LN1G, "L2_gnn_ln1_g"), (R_LN2G, "L2_gnn_ln2_g"),
                 (R_LN2B, "L2_gnn_ln2_b")):
        rows[r] = a[k]
    rows[R_L3, 0:128] = a["L3_gnn_b_o0"]
    rows[R_L3, 128:256] = a["L3_gnn_b_nd0"]
    rows[R_L3, 256:384] = a["L3_gnn_b_pre0"]
    wsmall = np.concatenate([flat(a["L3_gnn_" + k]) for k in
                             ("W_g1", "W_g2", "W_nd0", "W_nd1", "W_o0", "W_o1", "W_pre0", "W_pre1", "W_s1")]
                            + [flat(a["L2_gnn_W1"])], axis=1)
    w32 = np.zeros((34, V_END), f32)
    w32[0:32] = np.concatenate([a["L2_gnn_W2"], a["L3_gnn_W_f2"], a["L3_gnn_W_s2"], a["L3_gnn_W_f1"]], axis=1)
    w32[32, 0:D] = a["L2_gnn_ln1_b"]
    w32[33, 0:D] = a["L2_gnn_b2"]
    rec = np.zeros((E, Q_END), f32)
    rec[:, Q_W] = a["edge_weight"]
    rec[:, Q_SH:Q_EA] = a["edge_attr_4"]
    rec[:, Q_EA:Q_SSC] = a["edge_attr_32"]
    t = np.arange(ET)
    mask = np.concatenate([t[:, None] > t[None, :], t[:, None] < t[None, :]]).astype(f32)
    arrays = {"x": a["x"], "cols": cols, "rows": rows, "wsmall": wsmall, "w32": w32,
              "ident_in": np.eye(128, dtype=f32),
              "w_r1": chunks(a["L0_gnn_W1_r"].T), "w_r2": chunks(a["L0_gnn_W2_r"].T),
              "w_l1": chunks(a["L0_gnn_W1_l"].T), "w_l2": chunks(a["L0_gnn_W2_l"].T),
              "w_q": chunks(a["L2_gnn_Wq"]), "w_k": chunks(a["L2_gnn_Wk"]),
              "w_v": chunks(a["L2_gnn_Wv"]), "w_o": chunks(a["L2_gnn_Wo"]),
              "keys": np.stack([a["dst"], a["src"]]),
              "key_cols": np.concatenate([a["dst"].reshape(ET, P).T, a["src"].reshape(ET, P).T], axis=1),
              "rec_in": rec, "earlier_in": np.tril(np.ones((P, P), f32), -1), "mask_in": mask,
              "abs_in": np.concatenate([a["L1_gnn_alpha"], a["L1_gnn_beta"], a["L1_gnn_sigma"]])[None, :]}
    nc = bacc.Bacc("TRN2", target_bir_lowering=False, num_devices=1)
    args = [nc.dram_tensor(k, v.shape, mybir.dt.from_np(v.dtype), kind="ExternalInput").ap()
            for k, v in arrays.items()]
    out = nc.dram_tensor("out", (N, D), F32, kind="ExternalOutput").ap()
    gnn_kernel(nc, *args, out)
    r = run_bass_kernel_spmd(nc, [{k: np.ascontiguousarray(v) for k, v in arrays.items()}], core_ids=[0])
    return r.results[0]["out"]
```
